# Optimizing a Trainium2 kernel written in Bass

```python
import numpy as np
import jax
import jax.numpy as jnp

def _softmax(x, axis=-1):
    return jax.nn.softmax(x, axis=axis)

def _gelu(x):
    return jax.nn.gelu(x, approximate=True)

def _silu(x):
    return jax.nn.silu(x)

def _sigmoid(x):
    return jax.nn.sigmoid(x)

def _layernorm(x, axis=-1, eps=1e-05):
    m = jnp.mean(x, axis=axis, keepdims=True)
    v = jnp.var(x, axis=axis, keepdims=True)
    return (x - m) / jnp.sqrt(v + eps)

def _scatter_add(tgt, idx, src, axis=0):
    return tgt.at[idx].add(src)

def _segment_sum(src, seg, n):
    return jax.ops.segment_sum(src, seg, n)
kernel_name = 'mk_conv_attn_hybrid_d2_conv_nchw256_r2_df0b41'

def setup_inputs(seed: int=0):
    np.random.seed(seed)
    _w = jnp.asarray

    def _rec_inputs():
        import jax
        import jax.numpy as jnp
        _gk = jax.random.key(seed)
        x = -0.0002928 + 1 * jax.random.normal(jax.random.fold_in(_gk, 1), (4, 128, 32, 32), jnp.float32)
        return x
    x = _rec_inputs()

    def _L0_conv_setup():
        import jax, jax.numpy as jnp
        import numpy as np
        E = 128
        C = 128
        QH = 4
        KVH = 2
        HD = E // QH
        KVE = HD * KVH

        def _conv(x, w, stride):
            return jax.lax.conv_general_dilated(x, w, (stride, stride), 'VALID', dimension_numbers=('NCHW', 'OIHW', 'NCHW'))
        key = jax.random.key(seed)
        ks = jax.random.split(key, 16)
        B, H, W = (4, 32, 32)
        s = 0.02
        return {'x': jax.random.normal(ks[0], (B, C, H, W), jnp.float32), 'wK': jax.random.normal(ks[1], (C, C, 1, 1), jnp.float32) * s, 'wQ': jax.random.normal(ks[2], (C, C, 2, 2), jnp.float32) * s, 'wV': jax.random.normal(ks[3], (C, C, 2, 2), jnp.float32) * s, 'q_w': jax.random.normal(ks[4], (E, E), jnp.float32) * s, 'q_b': jax.random.normal(ks[5], (E,), jnp.float32) * s, 'k_w': jax.random.normal(ks[6], (KVE, E), jnp.float32) * s, 'k_b': jax.random.normal(ks[7], (KVE,), jnp.float32) * s, 'v_w': jax.random.normal(ks[8], (KVE, E), jnp.float32) * s, 'v_b': jax.random.normal(ks[9], (KVE,), jnp.float32) * s, 'ln_g': jnp.ones((E,), jnp.float32), 'ln_b': jnp.zeros((E,), jnp.float32), 'o_w': jax.random.normal(ks[10], (E, E), jnp.float32) * s, 'o_b': jax.random.normal(ks[11], (E,), jnp.float32) * s}
    _L0_conv_all = _L0_conv_setup()
    _L0_conv_in = {k: v for k, v in _L0_conv_all.items() if k in ('wK', 'wQ', 'wV', 'q_w', 'q_b', 'k_w', 'k_b', 'v_w', 'v_b', 'ln_g', 'ln_b', 'o_w', 'o_b')}
    del _L0_conv_all

    def _L1_attn_setup():
        import jax, jax.numpy as jnp
        import numpy as np
        B, S, D, U = (8, 1024, 128, 64)
        key = jax.random.key(seed)
        ks = jax.random.split(key, 5)
        inputs = jax.random.normal(ks[0], (B, S, D), dtype=jnp.float32)
        W_q = jax.random.normal(ks[1], (D, U), dtype=jnp.float32) * (1.0 / np.sqrt(D))
        W_k = jax.random.normal(ks[2], (D, U), dtype=jnp.float32) * (1.0 / np.sqrt(D))
        W_v = jax.random.normal(ks[3], (D, U), dtype=jnp.float32) * (1.0 / np.sqrt(D))
        W_o = jax.random.normal(ks[4], (U, D), dtype=jnp.float32) * (1.0 / np.sqrt(U))
        b_o = jnp.zeros((D,), dtype=jnp.float32)
        return {'inputs': inputs, 'W_q': W_q, 'W_k': W_k, 'W_v': W_v, 'W_o': W_o, 'b_o': b_o}
    _L1_attn_all = _L1_attn_setup()
    _L1_attn_in = {k: v for k, v in _L1_attn_all.items() if k in ('W_q', 'W_k', 'W_v', 'W_o', 'b_o')}
    del _L1_attn_all

    def _L1_ffn_setup():
        import jax, jax.numpy as jnp
        import numpy as np
        N_EXPERTS = 8
        TOP_K = 2
        key = jax.random.key(seed)
        ks = jax.random.split(key, 5)
        B, T, C, E, H = (8, 1024, 128, 8, 341)
        scale = 1.0 / np.sqrt(C)
        return {'x': jax.random.normal(ks[0], (B, T, C), dtype=jnp.float32), 'router_w': jax.random.normal(ks[1], (E, C), dtype=jnp.float32) * scale, 'w1': jax.random.normal(ks[2], (E, H, C), dtype=jnp.float32) * scale, 'w2': jax.random.normal(ks[3], (E, C, H), dtype=jnp.float32) * (1.0 / np.sqrt(H)), 'w3': jax.random.normal(ks[4], (E, H, C), dtype=jnp.float32) * scale}
    _L1_ffn_all = _L1_ffn_setup()
    _L1_ffn_in = {k: v for k, v in _L1_ffn_all.items() if k in ('router_w', 'w1', 'w2', 'w3')}
    del _L1_ffn_all
    return {'x': x, 'L0_conv_wK': _L0_conv_in['wK'], 'L0_conv_wQ': _L0_conv_in['wQ'], 'L0_conv_wV': _L0_conv_in['wV'], 'L0_conv_q_w': _L0_conv_in['q_w'], 'L0_conv_q_b': _L0_conv_in['q_b'], 'L0_conv_k_w': _L0_conv_in['k_w'], 'L0_conv_k_b': _L0_conv_in['k_b'], 'L0_conv_v_w': _L0_conv_in['v_w'], 'L0_conv_v_b': _L0_conv_in['v_b'], 'L0_conv_ln_g': _L0_conv_in['ln_g'], 'L0_conv_ln_b': _L0_conv_in['ln_b'], 'L0_conv_o_w': _L0_conv_in['o_w'], 'L0_conv_o_b': _L0_conv_in['o_b'], 'L1_attn_W_q': _L1_attn_in['W_q'], 'L1_attn_W_k': _L1_attn_in['W_k'], 'L1_attn_W_v': _L1_attn_in['W_v'], 'L1_attn_W_o': _L1_attn_in['W_o'], 'L1_attn_b_o': _L1_attn_in['b_o'], 'L1_ffn_router_w': _L1_ffn_in['router_w'], 'L1_ffn_w1': _L1_ffn_in['w1'], 'L1_ffn_w2': _L1_ffn_in['w2'], 'L1_ffn_w3': _L1_ffn_in['w3']}

def reference(x, L0_conv_wK, L0_conv_wQ, L0_conv_wV, L0_conv_q_w, L0_conv_q_b, L0_conv_k_w, L0_conv_k_b, L0_conv_v_w, L0_conv_v_b, L0_conv_ln_g, L0_conv_ln_b, L0_conv_o_w, L0_conv_o_b, L1_attn_W_q, L1_attn_W_k, L1_attn_W_v, L1_attn_W_o, L1_attn_b_o, L1_ffn_router_w, L1_ffn_w1, L1_ffn_w2, L1_ffn_w3):
    import jax
    import jax.numpy as jnp

    def _L0_conv_ref(x, wK, wQ, wV, q_w, q_b, k_w, k_b, v_w, v_b, ln_g, ln_b, o_w, o_b):
        import jax, jax.numpy as jnp
        import numpy as np
        E = 128
        C = 128
        QH = 4
        KVH = 2
        HD = E // QH
        KVE = HD * KVH

        def _conv(x, w, stride):
            return jax.lax.conv_general_dilated(x, w, (stride, stride), 'VALID', dimension_numbers=('NCHW', 'OIHW', 'NCHW'))
        B = x.shape[0]
        k = _conv(x, wK, 1).reshape(B, -1, E)
        q = _conv(x, wQ, 2).reshape(B, -1, E)
        v = _conv(x, wV, 2).reshape(B, -1, E)
        Q = k @ q_w.T + q_b
        K = q @ k_w.T + k_b
        V = v @ v_w.T + v_b
        n, sl = (Q.shape[1], K.shape[1])
        G = QH // KVH
        Qh = Q.reshape(B, n, KVH, G, HD).transpose(0, 2, 3, 1, 4)
        Kh = K.reshape(B, sl, KVH, HD).transpose(0, 2, 1, 3)
        Vh = V.reshape(B, sl, KVH, HD).transpose(0, 2, 1, 3)
        scores = jnp.einsum('bhgnd,bhsd->bhgns', Qh, Kh) / jnp.sqrt(jnp.float32(HD))
        attn = jax.nn.softmax(scores, axis=-1)
        out = jnp.einsum('bhgns,bhsd->bhgnd', attn, Vh)
        out = out.transpose(0, 3, 1, 2, 4).reshape(B, n, E)
        mu = out.mean(-1, keepdims=True)
        var = out.var(-1, keepdims=True)
        out = (out - mu) * jax.lax.rsqrt(var + 1e-05) * ln_g + ln_b
        out = out @ o_w.T + o_b
        return out.reshape(x.shape)

    def _L1_attn_ref(inputs, W_q, W_k, W_v, W_o, b_o):
        import jax, jax.numpy as jnp
        import numpy as np
        B, S, D, U = (8, 1024, 128, 64)
        Q = jnp.einsum('bsd,du->bsu', inputs, W_q)
        K = jnp.einsum('bsd,du->bsu', inputs, W_k)
        V = jnp.einsum('bsd,du->bsu', inputs, W_v)
        scale = 1.0 / jnp.sqrt(jnp.asarray(U, dtype=inputs.dtype))
        attn = jnp.einsum('bqu,bku->bqk', Q, K) * scale
        w = jax.nn.softmax(attn, axis=-1)
        out = jnp.einsum('bqk,bku->bqu', w, V)
        return jnp.einsum('bsu,ud->bsd', out, W_o) + b_o + inputs

    def _L1_ffn_ref(x, router_w, w1, w2, w3):
        import jax, jax.numpy as jnp
        import numpy as np
        N_EXPERTS = 8
        TOP_K = 2
        B, T, C = x.shape
        flat = x.reshape(-1, C)
        logits = flat @ router_w.T
        probs = jax.nn.softmax(logits, axis=-1)
        topk_probs, topk_idx = jax.lax.top_k(probs, TOP_K)
        topk_probs = topk_probs / (jnp.sum(topk_probs, axis=-1, keepdims=True) + 1e-09)
        onehot = jax.nn.one_hot(topk_idx, N_EXPERTS, dtype=flat.dtype)
        gates = jnp.einsum('nk,nke->ne', topk_probs, onehot)
        h1 = jnp.einsum('nc,ehc->neh', flat, w1)
        h3 = jnp.einsum('nc,ehc->neh', flat, w3)
        h = jax.nn.silu(h1) * h3
        y = jnp.einsum('neh,ech->nec', h, w2)
        out = jnp.einsum('ne,nec->nc', gates, y)
        return out.reshape(B, T, C)

    def _gn(v, G=32, eps=1e-05):
        B_, C_, H_, W_ = v.shape
        g = v.reshape(B_, G, C_ // G, H_, W_)
        m = jnp.mean(g, axis=(2, 3, 4), keepdims=True)
        s = jnp.var(g, axis=(2, 3, 4), keepdims=True)
        return ((g - m) / jnp.sqrt(s + eps)).reshape(v.shape)

    def _ln_c(v, eps=1e-06):
        m = jnp.mean(v, axis=1, keepdims=True)
        s = jnp.var(v, axis=1, keepdims=True)
        return (v - m) / jnp.sqrt(s + eps)

    def _ln_t(v, eps=1e-05):
        m = jnp.mean(v, axis=-1, keepdims=True)
        s = jnp.var(v, axis=-1, keepdims=True)
        return (v - m) / jnp.sqrt(s + eps)

    def _to_tokens(v):
        B_, C_, H_, W_ = v.shape
        return v.reshape(B_, C_, H_ * W_).transpose(0, 2, 1)

    def _from_tokens(t, like):
        B_, C_, H_, W_ = like.shape
        return t.transpose(0, 2, 1).reshape(B_, C_, H_, W_)
    x = x + _L0_conv_ref(_gn(x), L0_conv_wK, L0_conv_wQ, L0_conv_wV, L0_conv_q_w, L0_conv_q_b, L0_conv_k_w, L0_conv_k_b, L0_conv_v_w, L0_conv_v_b, L0_conv_ln_g, L0_conv_ln_b, L0_conv_o_w, L0_conv_o_b)
    t = _to_tokens(x)
    t = t + _L1_attn_ref(_ln_t(t), L1_attn_W_q, L1_attn_W_k, L1_attn_W_v, L1_attn_W_o, L1_attn_b_o)
    t = t + _L1_ffn_ref(_ln_t(t), L1_ffn_router_w, L1_ffn_w1, L1_ffn_w2, L1_ffn_w3)
    x = _from_tokens(t, x)
    return x

_drawn_inputs = setup_inputs


def setup_inputs(seed=0):
    import zlib

    import numpy as np

    out = dict(_drawn_inputs(seed))
    spreads = {'L0_conv_ln_g': (1.0, 0.591), 'L0_conv_ln_b': (0.0, 0.8), 'L1_attn_b_o': (0.0, 0.1)}
    factors = {'L0_conv_wK': 8.0,
     'L0_conv_wQ': 8.0,
     'L0_conv_q_w': 8.0,
     'L0_conv_q_b': 8.0,
     'L0_conv_k_w': 8.0,
     'L0_conv_k_b': 8.0,
     'L0_conv_o_b': 5.397}
    for name, (base, spread) in spreads.items():
        noise = np.random.default_rng([zlib.crc32(name.encode()), seed]).standard_normal(out[name].shape)
        drawn = base * np.exp(spread * noise) if base else spread * noise
        out[name] = jnp.asarray(drawn.astype(out[name].dtype))
    for name, factor in factors.items():
        out[name] = (out[name] * factor).astype(out[name].dtype)
    return out
```

```python
from contextlib import ExitStack

import concourse.bass as bass
from concourse import mybir

F32 = mybir.dt.float32
F32R = mybir.dt.float32r
I32 = mybir.dt.int32
ALU = mybir.AluOpType
ACT = mybir.ActivationFunctionType
AX = mybir.AxisListType

P = 128
B, C, HW = 4, 128, 1024
NT = HW // P
HEADS, HD, KEYS = 4, 32, 256
U = 64
E, H = 8, 341
HC = 114
CHUNKS = 3
HALF_B = 2
TT = HALF_B * NT
HALF_TOK = TT * P
NB = 8
NC = 4
SLOT_TILES = -(-(2 * HALF_TOK // P + E - 1) // NB) * NB
TURNS = SLOT_TILES // NB
SLOTS = SLOT_TILES * P
ROW = C + 2
Y_ROWS = 2 * HALF_TOK + SLOTS
CONV_SCALE = float(HD) ** -0.5
TOK_SCALE = float(U) ** -0.5
GROUP = 4
MAGIC = 0x5F3759DF
BIG = -3.0e38
NEWTON = 4
IMAGE_STEPS = 87
ROUTE_STEPS = 42


def build(nc, a, out):
    ctx = ExitStack()
    with ctx:
        def sb(name, shape, dt=F32):
            return ctx.enter_context(nc.sbuf_tensor(name, shape, dt))

        def ps(name, shape, dt=F32):
            return ctx.enter_context(nc.psum_tensor(name, shape, dt))

        def sem(name):
            return ctx.enter_context(nc.semaphore(name))

        ident = sb("ident", [P, P])
        ones = sb("ones", [P, P])
        spare = sb("spare", [P, 2])
        before = sb("before", [P, P])
        groups = sb("groups", [P, P])
        rev = sb("rev", [P, TT, E])
        tile_no = sb("tile_no", [P, SLOT_TILES, E])
        wK_in = sb("wK_in", [P, C])
        wQ_in = sb("wQ_in", [P, C * 4])
        wV_in = sb("wV_in", [P, C * 4])
        qw_in = sb("qw_in", [P, P])
        kw_in = sb("kw_in", [P, P])
        vw_in = sb("vw_in", [P, P])
        ow_in = sb("ow_in", [P, P])
        router_in = sb("router_in", [E, C])
        w13_in = sb("w13_in", [P, 2, C])
        rows_in = sb("rows_in", [1, 3, P])
        q_b = sb("q_b", [P, 1])
        k_b = sb("k_b", [P, 1])
        ln_g = sb("ln_g", [P, 1])
        ln_b = sb("ln_b", [P, 1])
        wK_T = sb("wK_T", [P, C])
        wQV_T = sb("wQV_T", [P, 4, 2, C])
        q_wT = sb("q_wT", [P, P])
        k_wT = sb("k_wT", [P, P])
        v_wT = sb("v_wT", [P, P])
        o_wT = sb("o_wT", [P, P])
        o_wTg = sb("o_wTg", [P, P])
        Wq2 = sb("Wq2", [P, P])
        Wk2 = sb("Wk2", [P, P])
        Wv2 = sb("Wv2", [P, P])
        Wo2 = sb("Wo2", [P, C])
        router_T = sb("router_T", [P, P])
        v_b_rows = sb("v_b_rows", [P, P])
        o_b_rows = sb("o_b_rows", [P, P])
        b_o_rows = sb("b_o_rows", [P, P])
        w13_T = sb("w13_T", [P, E, 2 * H])
        w2_T = sb("w2_T", [P, E, CHUNKS * C])
        x = sb("x", [P, B, HW])
        chan = sb("chan", [P, B, 2, 6])
        chan_mv = sb("chan_mv", [P, B, 2])
        grp = sb("grp", [P, B, 2])
        dev = sb("dev", [P, B])
        gvar = sb("gvar", [P, 8])
        operandT = sb("operandT", [P, HW])
        kT = conv_lnT = tok_lnT = x2T = operandT
        qvT = sb("qvT", [P, 2, 2, C])
        Qhi = sb("Qhi", [P, HW], F32R)
        Qlo = sb("Qlo", [P, HW], F32R)
        QS, KH = Qhi, Qlo
        Khi = sb("Khi", [P, HEADS, KEYS], F32R)
        Klo = sb("Klo", [P, HEADS, KEYS], F32R)
        V4 = sb("V4", [P, 2, P])
        shared = sb("shared", [P, 4 * HW])
        probs = shared[:, 0:2 * HW].rearrange("p (i n) -> p i n", i=2)
        probsT = shared[:, 2 * HW:4 * HW].rearrange("p (i n) -> p i n", i=2)
        wstage = shared[:, 0:3 * 6 * C].rearrange("p (i n) -> p i n", i=3)
        outT = sb("outT", [P, 2, P])
        normed = sb("normed", [P, NT, P])
        conv_out = tok_ln = x2 = normed
        lnb_rep = sb("lnb_rep", [P, P])
        pixels = sb("pixels", [P, HW])
        xn_b = x_new = pixels
        taps = sb("taps", [P, 4, 256])
        tok = sb("tok", [P, NT, C])
        KL = sb("KL", [P, HW], F32R)
        Vt = sb("Vt", [P, NT, U])
        t1 = sb("t1", [P, B * NT, C])
        w2stage = t1[:, :, :].rearrange("p i c -> p (i c)")[:, 0:E * H].rearrange("p (e h) -> p e h", e=E)
        rows = [sb(f"rows{k}", [P, TT, ROW]) for k in range(2)]
        logits = sb("logits", [P, 2 * TT, E])
        stats = sb("stats", [P, NT, 6])
        mv = sb("mv", [P, NT, 2])
        rs_v = sb("rs_v", [P, NT])
        rs_a = sb("rs_a", [P, NT])
        rs_y = sb("rs_y", [P, NT])
        rs_i = sb("rs_i", [P, NT], I32)
        rowmax = sb("rowmax", [P, 2, HEADS])
        negmax = sb("negmax", [P, 2, HEADS])
        rowsum = sb("rowsum", [P, 4, HEADS])
        rowinv = sb("rowinv", [P, 4, HEADS])
        r8 = {n: sb("r_" + n, [P, TT, E]) for n in ("eq", "w", "oh1", "oh2", "l2", "ex", "a", "c0", "c1", "rank", "tmp")}
        r1 = {n: sb("r1_" + n, [P, TT]) for n in ("m1", "m2", "mw", "z", "e2", "p1", "p2", "g1", "g2", "s", "pos")}
        pos_i = sb("pos_i", [P, 2, 2, TT], I32)
        cnt = sb("cnt", [P, E])
        cnt_i = sb("cnt_i", [P, E], I32)
        cum = [sb(f"cum{k}", [P, E]) for k in range(2)]
        tile_cmp = sb("tile_cmp", [P, SLOT_TILES, E])
        tile_sum = sb("tile_sum", [P, SLOT_TILES])
        tile_expert = sb("tile_expert", [P, 2, SLOT_TILES], I32)
        late = sb("late", [P, SLOT_TILES * ROW])
        empty = late[:, :].rearrange("p (k c) -> p k c", c=ROW)

        def carve(base, at, n, width):
            return base[:, at:at + n * width].rearrange("p (i n) -> p i n", i=n), at + n * width

        xs, at = carve(late, 0, NB, ROW)
        hid, at = carve(late, at, NC, CHUNKS * HC)
        y12, at = carve(late, at, 2, 4 * 2 * C)
        y12 = y12.rearrange("p i (t n) -> p i t n", t=4)
        res = x[:, 0, :].rearrange("p (i n) -> p i n", i=2)
        assert at <= SLOT_TILES * ROW
        hidT, at = carve(shared, 0, NC, CHUNKS * P)
        act_h, at = carve(shared, at, NC, H)
        xsT, at = carve(shared, at, NC, P)
        ys, at = carve(shared, at, NC, C)
        assert at <= 4 * HW

        slots = [nc.dram_tensor(f"slots{h}", [SLOTS, ROW], F32).ap() for h in range(2)]
        y_rows = [nc.dram_tensor(f"y_rows{h}", [Y_ROWS, C], F32).ap() for h in range(2)]

        S = [ps(f"S{i}", [P, HW]) for i in range(2)]
        TA = ps("TA", [P, 512])
        TB = ps("TB", [P, 512])
        OB = ps("OB", [P, 512])
        MB = ps("MB", [P, 512])

        names = """x_in w_in const_z const_set pad_z wt_done wt_used bias_done bias_used
            gn_pe gn_dve wx0 wx1 wx2 small_in w2stage_in w2_pe w2_copied xb_ready taps_ready wexp_pe wexp_copied dve_pre
            kT_pe kT_act kT_dve qv_pe qv_act q_pe q_hi q_lo k_pe k_hi k_lo v_pe v_dve
            scores_done neg_ready exp_done pt_done ptA_copied ptB_copied pv_done ot_copied post_done post_used
            dve_step cln_ready clnT_pe clnT_act clnT_dve o_pe xnew_ready
            t_pe t_act tln_ready tlnT_pe tlnT_act tlnT_dve Q_pe Q_hi Q_lo K_pe K_hi K_lo V_pe V_act V_dve
            x2_ready x2T_pe x2T_act x2T_dve l_pe l_dve
            r_step r_exp_in r_exp r_cnt_in r_pe route_done pool_step init_z init_done dispatched
            xs_in0 xs_in1 xs_in2 xs_in3 xs_in4 xs_in5 xs_in6 xs_in7 xsT_pe xsT_act h_pe silu_done hid_ready hT_pe hT_dve y_pe ys_ready ys_out0 ys_out1 ys_out2 ys_out3 ys_out4 ys_out5 ys_out6 ys_out7
            y12_in0 y12_in1 sum_step sum_ready fin_pe fin_act out_done0 out_done1""".split()
        s = {n: sem(n) for n in names}
        xs_in = [s[f"xs_in{k}"] for k in range(NB)]
        ys_out = [s[f"ys_out{k}"] for k in range(NB)]
        y12_in = [s[f"y12_in{k}"] for k in range(2)]

        N_W = 21
        SMALL_T = [
            (wK_in[:, :], wK_T[:, :]),
            *[(wQ_in[:, tap:C * 4:4], wQV_T[:, tap, 0, :]) for tap in range(4)],
            *[(wV_in[:, tap:C * 4:4], wQV_T[:, tap, 1, :]) for tap in range(4)],
            (qw_in[:, :], q_wT[:, :]), (kw_in[:, :], k_wT[:, :]), (vw_in[:, :], v_wT[:, :]), (ow_in[:, :], o_wT[:, :]),
        ]
        SMALL_BANK = [OB, MB, TA, TB]
        out_r = out.rearrange("b c h w -> c b (h w)")
        block = ctx.enter_context(nc.Block())

        def tile(i):
            return slice(i * P, (i + 1) * P)

        def wait_if(eng, semaphore, value):
            if not (isinstance(value, int) and value <= 0):
                eng.wait_ge(semaphore, value)

        OFFSET = {"B": 0, "T": 1, "D": -2, "C": -1}

        def schedule(eng, half, stages):
            def step(q, k, i=None):
                for name, stage in stages:
                    d = OFFSET[name]
                    if i is not None and not 0 <= i + d < SLOT_TILES:
                        continue
                    qq = q + (k + d) // NB
                    stage(qq * NB + (k + d) % NB, qq, (k + d) % NB)

            if any(name == "T" for name, _ in stages):
                dict(stages)["T"](half * SLOT_TILES, half * TURNS, 0)
            for i in range(NB):
                step(half * TURNS, i, i)
            with eng.Fori(half * TURNS + 1, half * TURNS + TURNS - 1) as t:
                for k in range(NB):
                    step(t, k)
            for i in range(SLOT_TILES - NB, SLOT_TILES + 2):
                step(half * TURNS + i // NB, i % NB, i)

        @block.sync
        def _(sp):
            xr = a["x"].rearrange("b c h w -> c b (h w)")
            for b in range(B):
                sp.dma_start(x[:, b, :], xr[:, b, :]).then_inc(s["x_in"], 16)
            sp.dma_start(wK_in[:, :], a["L0_conv_wK"].rearrange("o c h w -> o (c h w)")).then_inc(s["w_in"], 16)
            sp.dma_start(wQ_in[:, :], a["L0_conv_wQ"].rearrange("o c h w -> o (c h w)")).then_inc(s["w_in"], 16)
            sp.dma_start(wV_in[:, :], a["L0_conv_wV"].rearrange("o c h w -> o (c h w)")).then_inc(s["w_in"], 16)
            sp.dma_start(qw_in[:, :], a["L0_conv_q_w"]).then_inc(s["w_in"], 16)
            sp.dma_start(ow_in[:, :], a["L0_conv_o_w"]).then_inc(s["w_in"], 16)
            kv = lambda w: w.rearrange("(k d) e -> k d e", k=2)
            for k in range(2):
                for src, dst in ((a["L0_conv_k_w"], kw_in), (a["L0_conv_v_w"], vw_in)):
                    for g in range(2):
                        sp.dma_start(dst[(2 * k + g) * HD:(2 * k + g + 1) * HD, :], kv(src)[k]).then_inc(s["w_in"], 16)
            col = lambda v: v.rearrange("(p a) -> p a", a=1)
            sp.dma_start(q_b[:, :], col(a["L0_conv_q_b"])).then_inc(s["w_in"], 16)
            sp.dma_start(ln_g[:, :], col(a["L0_conv_ln_g"])).then_inc(s["w_in"], 16)
            sp.dma_start(ln_b[:, :], col(a["L0_conv_ln_b"])).then_inc(s["w_in"], 16)
            for k in range(2):
                for g in range(2):
                    h = 2 * k + g
                    sp.dma_start(k_b[h * HD:(h + 1) * HD, :],
                                 col(a["L0_conv_k_b"])[k * HD:(k + 1) * HD, :]).then_inc(s["w_in"], 16)

            def experts_tiles(half):
                sp.wait_ge(s["init_done"], 32)
                sp.wait_ge(s["dispatched"], 16 * 2 * TT * (half + 1))

                def load(i, q, k):
                    wait_if(sp, ys_out[k], q * 16)
                    row = bass.ds(i * P, P) if not isinstance(i, int) else slice(i * P, i * P + P)
                    sp.dma_start(xs[:, k, :], slots[half][row, :]).then_inc(xs_in[k], 16)

                for k in range(NB):
                    load(k, half * TURNS, k)
                with sp.Fori(1, TURNS) as t:
                    for k in range(NB):
                        load(t * NB + k, t + half * TURNS, k)

            for half in range(2):
                experts_tiles(half)
            for k in range(NB):
                sp.wait_ge(ys_out[k], 16 * 2 * TURNS)
            y_view = [y_rows[h][0:2 * HALF_TOK, :].rearrange("(i p r) c -> p i (r c)", p=P, r=2) for h in range(2)]
            for q in range(2 * TT // 4 + 2):
                if q < 2 * TT // 4:
                    if q >= 2:
                        sp.wait_ge(s["sum_ready"], q - 1)
                    h, r = q // (TT // 4), q % (TT // 4)
                    sp.dma_start(y12[:, q % 2, :, :], y_view[h][:, r * 4:r * 4 + 4, :]).then_inc(y12_in[q % 2], 16)
                if q >= 2:
                    m = q - 2
                    sp.wait_ge(s["fin_act"], m + 1)
                    sp.dma_start(out_r[:, m // 2, (m % 2) * 512:(m % 2) * 512 + 512],
                                 res[:, m % 2, :]).then_inc(s[f"out_done{m % 2}"], 16)
            for k in range(2):
                sp.wait_ge(s[f"out_done{k}"], 16 * TT // 4)

        @block.gpsimd
        def _(pool):
            for k, (m, v) in enumerate(((ident, 0.0), (ones, 1.0), (before, 1.0), (groups, 1.0 / GROUP), (router_T, 0.0),
                                        (empty, 0.0), (w2_T, 0.0))):
                nc.gpsimd.memset(m[:], v).then_inc(s["const_z"], 1)
            pool.wait_ge(s["const_z"], 7)
            nc.gpsimd.affine_select(out=ident[:, :], in_=ident[:, :], compare_op=ALU.not_equal, fill=1.0, base=0,
                                    pattern=[[-1, P]], channel_multiplier=1).then_inc(s["const_set"], 1)
            nc.gpsimd.affine_select(out=before[:, :], in_=before[:, :], compare_op=ALU.is_gt, fill=0.0, base=0,
                                    pattern=[[1, P]], channel_multiplier=-1).then_inc(s["const_set"], 1)
            gv = groups[:, :].rearrange("p (g r) -> p g r", r=GROUP)
            nc.gpsimd.affine_select(out=gv, in_=gv, compare_op=ALU.is_ge, fill=0.0, base=0,
                                    pattern=[[-GROUP, P // GROUP], [0, GROUP]], channel_multiplier=1).then_inc(s["const_z"], 1)
            pool.wait_ge(s["const_z"], 8)
            nc.gpsimd.affine_select(out=gv, in_=gv, compare_op=ALU.is_ge, fill=0.0, base=GROUP - 1,
                                    pattern=[[GROUP, P // GROUP], [0, GROUP]], channel_multiplier=-1).then_inc(s["const_set"], 1)
            nc.gpsimd.iota(rev[:, :, :], pattern=[[0, TT], [-1, E]], base=E, channel_multiplier=0,
                           allow_small_or_imprecise_dtypes=True).then_inc(s["const_set"], 1)
            nc.gpsimd.iota(tile_no[:, :, :], pattern=[[1, SLOT_TILES], [0, E]], base=0, channel_multiplier=0,
                           allow_small_or_imprecise_dtypes=True).then_inc(s["const_set"], 1)
            nc.gpsimd.iota(empty[:, :, C:C + 1].bitcast(I32), pattern=[[1, SLOT_TILES]], base=2 * HALF_TOK,
                           channel_multiplier=SLOT_TILES).then_inc(s["init_z"], 1)
            for k in range(2):
                if True:
                    nc.gpsimd.iota(rows[k][:, :, C:C + 1].bitcast(I32), pattern=[[2 * P, TT]], base=k,
                                   channel_multiplier=2).then_inc(s["init_z"], 1)
            pool.wait_ge(s["init_z"], 3)
            for half in range(2):
                pool.dma_start(slots[half].rearrange("(p k) c -> p (k c)", k=SLOT_TILES),
                               empty[:, :, :].rearrange("p k c -> p (k c)")).then_inc(s["init_done"], 16)
            pool.wait_ge(s["init_done"], 32)
            def dispatch(half, j):
                pool.indirect_dma_start(
                    slots[half], bass.IndirectOffsetOnAxis(pos_i[:, half, j % 2, j // 2:j // 2 + 1], 0),
                    rows[j % 2][:, j // 2, :], None).then_inc(s["dispatched"], 16)

            def scatter(half, k):
                pool.indirect_dma_start(
                    y_rows[half], bass.IndirectOffsetOnAxis(xs[:, k, C:C + 1].bitcast(I32), 0),
                    ys[:, k % NC, :], None).then_inc(ys_out[k], 16)

            pool.wait_ge(s["route_done"], 1)
            for j in range(2 * TT):
                dispatch(0, j)
            pool.wait_ge(s["route_done"], 2)
            for n in range(SLOT_TILES):
                if n < 2 * TT:
                    dispatch(1, n)
                pool.wait_ge(s["ys_ready"], n + 1)
                scatter(0, n % NB)
            with pool.Fori(TURNS, 2 * TURNS) as t:
                for k in range(NB):
                    pool.wait_ge(s["ys_ready"], t * NB + (k + 1))
                    pool.wait_ge(s["pool_step"], t * NB + (k - SLOT_TILES))
                    nc.gpsimd.tensor_tensor(spare[:, 1:2], ones[:, 0:1], ones[:, 1:2], ALU.mult).then_inc(s["pool_step"], 1)
                    scatter(1, k)

        @block.scalar
        def _(act):
            act.dma_start(router_in[:, :], a["L1_ffn_router_w"]).then_inc(s["w_in"], 16)
            for dst, w in ((Wq2, "L1_attn_W_q"), (Wk2, "L1_attn_W_k"), (Wv2, "L1_attn_W_v")):
                for k in range(2):
                    act.dma_start(dst[:, k * U:(k + 1) * U], a[w]).then_inc(s["small_in"], 16)
            for k in range(2):
                act.dma_start(Wo2[k * U:(k + 1) * U, :], a["L1_attn_W_o"]).then_inc(s["small_in"], 16)
            row = lambda v: v.rearrange("(a n) -> a n", a=1)
            for h in range(HEADS):
                act.dma_start(rows_in[0:1, 0, h * HD:(h + 1) * HD],
                              row(a["L0_conv_v_b"])[:, (h // 2) * HD:(h // 2 + 1) * HD]).then_inc(s["small_in"], 16)
            act.dma_start(rows_in[0:1, 1, :], row(a["L0_conv_o_b"])).then_inc(s["small_in"], 16)
            act.dma_start(rows_in[0:1, 2, :], row(a["L1_attn_b_o"])).then_inc(s["small_in"], 16)
            act.dma_start(w2stage[:, :, :], a["L1_ffn_w2"].rearrange("e c h -> c e h")).then_inc(s["w2stage_in"], 16)

            def load_w13(e):
                for m, w in enumerate(("L1_ffn_w1", "L1_ffn_w3")):
                    for c in range(CHUNKS):
                        n = min(HC, H - c * HC)
                        act.dma_start(wstage[0:n, e % 3, (m * CHUNKS + c) * C:(m * CHUNKS + c + 1) * C],
                                      a[w][e, c * HC:c * HC + n, :]).then_inc(s[("wx0", "wx1", "wx2")[e % 3]], 16)
            for e in range(3):
                load_w13(e)
            for e in range(E):
                act.wait_ge(s["wexp_pe"], e + 1)
                act.activation(w13_T[:, e, :].rearrange("p (m h) -> p m h", m=2)[:, :, 0:H],
                               S[e % 2][:, :].rearrange("p (m h) -> p m h", m=2)[:, :, 0:H],
                               ACT.Copy).then_inc(s["wexp_copied"], 1)
                if e + 3 < E:
                    load_w13(e + 3)

            def attention(b, g0, conv):
                for j in range(NT):
                    g = g0 + j
                    act.wait_ge(s["neg_ready"], b * 16 + (g + 1))
                    if g >= 2:
                        act.wait_ge(s["pt_done"], b * 16 + (g - 1))
                    else:
                        act.wait_ge(s["pt_done"], b * 16)
                    act.wait_ge(s["post_used"], b * 16 + max(0, g - 3))
                    if conv:
                        for h in range(HEADS):
                            ins = act.activation(probs[:, j % 2, h * KEYS:(h + 1) * KEYS],
                                                 S[j % 2][:, h * KEYS:(h + 1) * KEYS], ACT.Exp,
                                                 bias=negmax[:, j % 2, h:h + 1], scale=CONV_SCALE,
                                                 accum_out=rowsum[:, j % 4, h:h + 1])
                    else:
                        ins = act.activation(probs[:, j % 2, :], S[j % 2][:, :], ACT.Exp, bias=negmax[:, j % 2, 0:1],
                                             scale=TOK_SCALE, accum_out=rowsum[:, j % 4, 0:1])
                    ins.then_inc(s["exp_done"], 1)
                    if j >= 1:
                        out_copy(b, g - 1)
                    act.wait_ge(s["pt_done"], b * 16 + (g + 1))
                    if j >= 2:
                        act.wait_ge(s["pv_done"], b * 16 + (g - 1))
                    act.activation(probsT[:, j % 2, 512:1024], TB[:, :], ACT.Copy).then_inc(s["ptB_copied"], 1)
                out_copy(b, g0 + NT - 1)

            def out_copy(b, g):
                act.wait_ge(s["pv_done"], b * 16 + (g + 1))
                if g >= 2:
                    act.wait_ge(s["post_done"], b * 16 + (g - 1))
                else:
                    act.wait_ge(s["post_done"], b * 16)
                act.activation(outT[:, g % 2, :], OB[:, 0:P], ACT.Copy).then_inc(s["ot_copied"], 1)

            def image(b):
                act.wait_ge(s["xb_ready"], b + 1)
                act.wait_ge(s["qv_pe"], b)
                grid = xn_b[:, :].rearrange("p (oy dy ox dx) -> p dy dx oy ox", oy=16, dy=2, ox=16, dx=2)
                for dy in range(2):
                    ins = act.activation(taps[:, 2 * dy:2 * dy + 2, :].rearrange("p x (oy ox) -> p x oy ox", oy=16),
                                         grid[:, dy], ACT.Copy)
                ins.then_inc(s["taps_ready"], 1)
                act.wait_ge(s["kT_pe"], b + 1)
                act.activation(kT[:, 0:512], S[0][:, 0:512], ACT.Copy).then_inc(s["kT_act"], 1)
                act.wait_ge(s["qv_pe"], b + 1)
                act.activation(qvT[:, :, :, :].rearrange("p j m c -> p (j m c)"), TA[:, :], ACT.Copy).then_inc(s["qv_act"], 1)
                act.wait_ge(s["q_pe"], b + 1)
                act.activation(Qhi[:, :], S[1][:, :], ACT.Identity, bias=q_b[:, 0:1]).then_inc(s["q_hi"], 1)
                act.wait_ge(s["k_pe"], b + 1)
                for h in range(HEADS):
                    r = slice(h * HD, (h + 1) * HD)
                    ins = act.activation(Khi[r, h, :], TB[r, 0:KEYS], ACT.Identity, bias=k_b[r, 0:1])
                ins.then_inc(s["k_hi"], 1)
                attention(b, 0, True)
                act.wait_ge(s["clnT_pe"], b + 1)
                act.activation(conv_lnT[:, 0:512], TA[:, :], ACT.Copy).then_inc(s["clnT_act"], 1)
                act.wait_ge(s["t_pe"], b + 1)
                act.wait_ge(s["x2_ready"], b)
                act.activation(tok[:, :, :].rearrange("p i c -> p (i c)"), S[1][:, :], ACT.Copy).then_inc(s["t_act"], 1)
                act.wait_ge(s["tlnT_pe"], b + 1)
                act.activation(tok_lnT[:, 0:512], TA[:, :], ACT.Copy).then_inc(s["tlnT_act"], 1)
                act.wait_ge(s["Q_pe"], b + 1)
                act.activation(QS[:, :], S[0][:, :], ACT.Copy).then_inc(s["Q_hi"], 1)
                act.wait_ge(s["K_pe"], b + 1)
                act.activation(KH[:, :], S[1][:, :], ACT.Copy).then_inc(s["K_hi"], 1)
                act.wait_ge(s["V_pe"], b + 1)
                act.activation(Vt[:, 0:4, :], TA[:, :].rearrange("p (i u) -> p i u", i=4)[:, :, 0:U], ACT.Copy).then_inc(s["V_act"], 1)
                attention(b, NT, False)
                act.wait_ge(s["x2T_pe"], b + 1)
                act.activation(x2T[:, 0:512], TA[:, :], ACT.Copy).then_inc(s["x2T_act"], 1)

            act.wait_ge(s["w_in"], 16 * N_W)
            for half in range(2):
                with act.Fori(half * HALF_B, (half + 1) * HALF_B) as b:
                    image(b)
                act.wait_ge(s["r_exp_in"], half + 1)
                act.activation(r8["ex"][:, :, :], r8["ex"][:, :, :], ACT.Exp).then_inc(s["r_exp"], 1)

            def x_copy(n, q, k):
                act.wait_ge(s["xsT_pe"], n + 1)
                wait_if(act, s["h_pe"], n - (NC - 1))
                act.activation(xsT[:, k % NC, :], OB[:, 0:P], ACT.Copy).then_inc(s["xsT_act"], 1)

            def silu(n, q, k):
                act.wait_ge(s["h_pe"], n + 1)
                wait_if(act, s["hid_ready"], n - (NC - 1))
                act.activation(act_h[:, k % NC, :], S[k % 2][:, 0:H], ACT.Silu).then_inc(s["silu_done"], 1)

            def gate(n, q, k):
                act.wait_ge(s["y_pe"], n + 1)
                wait_if(act, ys_out[(k - NC) % NB], (q + (k - NC) // NB + 1) * 16)
                act.activation(ys[:, k % NC, :], MB[:, 0:P], ACT.Copy, scale=xs[:, k, C + 1:C + 2]).then_inc(s["ys_ready"], 1)

            for half in range(2):
                schedule(act, half, (("B", silu), ("T", x_copy), ("D", gate)))

            for q in range(2 * TT // 4):
                act.wait_ge(s["fin_pe"], q + 1)
                if q >= 2:
                    act.wait_ge(s[f"out_done{q % 2}"], 16 * (q // 2))
                act.activation(res[:, q % 2, :], (TA if q % 2 == 0 else TB)[:, :], ACT.Copy).then_inc(s["fin_act"], 1)

        @block.vector
        def _(dve):
            class Steps:
                def __init__(self, semaphore, base):
                    self.semaphore, self.base, self.n = semaphore, base, 0

                def __call__(self, ins):
                    ins.then_inc(self.semaphore, 1)
                    self.n += 1
                    dve.wait_ge(self.semaphore, self.base + self.n)

            def rsqrt(link, y, v, n, eps):
                h, t = rs_v[:, 0:n], rs_a[:, 0:n]
                link(nc.vector.tensor_scalar(h, v, eps, None, ALU.add))
                link(nc.vector.tensor_scalar(rs_i[:, 0:n], h.bitcast(I32), 1, None, ALU.logical_shift_right))
                link(nc.vector.tensor_scalar(y.bitcast(I32), rs_i[:, 0:n], -1.0, float(MAGIC), ALU.mult, ALU.add))
                for _ in range(NEWTON):
                    link(nc.vector.tensor_tensor(t, y, y, ALU.mult))
                    link(nc.vector.scalar_tensor_tensor(out=t, in0=t, scalar=-0.5, in1=h, op0=ALU.mult, op1=ALU.mult))
                    link(nc.vector.scalar_tensor_tensor(out=y, in0=t, scalar=1.5, in1=y, op0=ALU.add, op1=ALU.mult))

            pre = Steps(s["dve_pre"], 0)
            dve.wait_ge(s["x_in"], 16 * B)
            for b in range(B):
                for i in range(2):
                    last = nc.vector.bn_stats(chan[:, b, i, :], x[:, b, i * 512:(i + 1) * 512])
            pre(last)
            for b in range(B):
                last = nc.vector.bn_aggr(chan_mv[:, b, :], chan[:, b, :, :].rearrange("p i s -> p (i s)"))
            last.then_inc(s["gn_dve"], 1)
            dve.wait_ge(s["gn_dve"], 1)
            dve.wait_ge(s["gn_pe"], 1)
            pre(nc.vector.tensor_copy(grp[:, :, :].rearrange("p b s -> p (b s)"), S[0][:, 0:2 * B]))
            pre(nc.vector.tensor_tensor(dev[:, :], chan_mv[:, :, 0], grp[:, :, 0], ALU.subtract))
            nc.vector.tensor_tensor(dev[:, :], dev[:, :], dev[:, :], ALU.mult).then_inc(s["gn_dve"], 1)
            dve.wait_ge(s["gn_pe"], 2)
            pre(nc.vector.tensor_tensor(gvar[:, 0:B], S[0][:, 0:B], grp[:, :, 1], ALU.add))
            rsqrt(pre, gvar[:, 4:4 + B], gvar[:, 0:B], B, 1e-5)
            nc.vector.memset(Khi[:, :, :].bitcast(F32), 0.0)
            nc.vector.memset(Klo[:, :, :].bitcast(F32), 0.0).then_inc(s["pad_z"], 1)
            for i, (_, dst) in enumerate(SMALL_T):
                if i % 4 == 0:
                    dve.wait_ge(s["wt_done"], i // 4 + 1)
                last = nc.vector.tensor_copy(dst, SMALL_BANK[i // 4][:, tile(i % 4)])
                if i % 4 == 3 or i == len(SMALL_T) - 1:
                    if i == len(SMALL_T) - 1:
                        dve.wait_ge(s["const_z"], 7)
                        last = nc.vector.tensor_copy(router_T[:, 0:E], TB[:, P:P + E])
                    last.then_inc(s["wt_used"], 1)
            dve.wait_ge(s["wt_used"], 4)
            nc.vector.tensor_scalar(o_wTg[:, :], o_wT[:, :], ln_g[:, 0:1], None, ALU.mult)
            dve.wait_ge(s["const_z"], 7)
            nc.vector.tensor_scalar(lnb_rep[:, :], ones[:, :], ln_b[:, 0:1], None, ALU.mult).then_inc(s["bias_used"], 1)
            dve.wait_ge(s["bias_done"], 1)
            nc.vector.tensor_copy(v_b_rows[:, :], OB[:, tile(0)])
            nc.vector.tensor_copy(o_b_rows[:, :], OB[:, tile(1)])
            nc.vector.tensor_copy(b_o_rows[:, :], OB[:, tile(2)]).then_inc(s["bias_used"], 1)
            dve.wait_ge(s["bias_used"], 2)
            for e in range(E):
                dve.wait_ge(s["w2_pe"], e + 1)
                T = TA if e % 2 == 0 else TB
                nc.vector.tensor_copy(w2_T[0:HC, e, 0:2 * C], T[0:HC, 0:2 * C])
                nc.vector.tensor_copy(w2_T[0:HC - 1, e, 2 * C:3 * C], T[0:HC - 1, 2 * C:3 * C]).then_inc(s["w2_copied"], 1)

            def row_max(b, g, conv):
                j = g % NT
                dve.wait_ge(s["scores_done"], b * 16 + (g + 1))
                if g >= 2:
                    dve.wait_ge(s["exp_done"], b * 16 + (g - 1))
                else:
                    dve.wait_ge(s["exp_done"], b * 16)
                n = HEADS if conv else 1
                link(nc.vector.tensor_reduce(rowmax[:, j % 2, 0:n], S[j % 2][:, :].rearrange("p (h k) -> p h k", h=n),
                                             AX.X, ALU.max))
                nc.vector.tensor_scalar(negmax[:, j % 2, 0:n], rowmax[:, j % 2, 0:n], -(CONV_SCALE if conv else TOK_SCALE),
                                        None, ALU.mult).then_inc(s["neg_ready"], 1)

            def probs_copy(b, g):
                dve.wait_ge(s["pt_done"], b * 16 + (g + 1))
                if g % NT >= 2:
                    dve.wait_ge(s["pv_done"], b * 16 + (g - 1))
                nc.vector.tensor_copy(probsT[:, g % 2, 0:512], TA[:, :]).then_inc(s["ptA_copied"], 1)

            def normalise(b, g, conv):
                j = g % NT
                n = HEADS if conv else 1
                link(nc.vector.reciprocal(rowinv[:, j % 4, 0:n], rowsum[:, j % 4, 0:n]))
                dve.wait_ge(s["post_done"], b * 16 + (g + 1))
                if conv:
                    nc.vector.tensor_tensor(conv_out[:, j, :].rearrange("p (h d) -> p h d", h=HEADS),
                                            MB[:, 0:P].rearrange("p (h d) -> p h d", h=HEADS),
                                            rowinv[:, j % 4, :].unsqueeze(2).broadcast_to((P, HEADS, HD)),
                                            ALU.mult).then_inc(s["post_used"], 1)
                else:
                    nc.vector.scalar_tensor_tensor(out=t1[:, bass.ds(b * NT + j, 1), :].rearrange("p a c -> p (a c)"),
                                                   in0=MB[:, 0:P], scalar=rowinv[:, j % 4, 0:1], in1=tok[:, j, :],
                                                   op0=ALU.mult, op1=ALU.add).then_inc(s["post_used"], 1)

            def attention(b, g0, conv):
                row_max(b, g0, conv)
                for g in range(g0, g0 + NT):
                    if g + 1 < g0 + NT:
                        row_max(b, g + 1, conv)
                    probs_copy(b, g)
                    if g > g0:
                        normalise(b, g - 1, conv)
                normalise(b, g0 + NT - 1, conv)

            def layer_norm(src, dst, done):
                nc.vector.memset(spare[:, 0:1], 0.0)
                for i in range(NT):
                    last = nc.vector.bn_stats(stats[:, i, :], src(i))
                link(last)
                nc.vector.memset(spare[:, 0:1], 0.0)
                for i in range(NT):
                    last = nc.vector.bn_aggr(mv[:, i, :], stats[:, i, :])
                link(last)
                rsqrt(link, rs_y[:, :], mv[:, :, 1], NT, 1e-5)
                for i in range(NT):
                    last = nc.vector.tensor_scalar(dst(i), src(i), mv[:, i, 0:1], rs_y[:, i:i + 1], ALU.subtract, ALU.mult)
                last.then_inc(done, 1)

            def image(b, half):
                dve.wait_ge(s["qv_pe"], b)
                nc.vector.tensor_scalar(xn_b[:, :], x[:, bass.ds(b, 1), :].rearrange("p a n -> p (a n)"),
                                        grp[:, bass.ds(b, 1), 0], gvar[:, bass.ds(b + 4, 1)],
                                        ALU.subtract, ALU.mult).then_inc(s["xb_ready"], 1)
                dve.wait_ge(s["kT_pe"], b + 1)
                nc.vector.tensor_copy(kT[:, 512:1024], S[0][:, 512:1024]).then_inc(s["kT_dve"], 1)
                xv = x[:, bass.ds(b, 1), :].rearrange("p a (j f) -> p (a j) f", j=NT)
                link(nc.vector.tensor_tensor(xv, xv, o_b_rows[:, :].unsqueeze(1).broadcast_to((P, NT, P)), ALU.add))
                dve.wait_ge(s["q_hi"], b + 1)
                nc.vector.scalar_tensor_tensor(out=Qlo[:, :], in0=S[1][:, :], scalar=q_b[:, 0:1], in1=Qhi[:, :].bitcast(F32),
                                               op0=ALU.add, op1=ALU.subtract).then_inc(s["q_lo"], 1)
                dve.wait_ge(s["k_hi"], b + 1)
                for h in range(HEADS):
                    r = slice(h * HD, (h + 1) * HD)
                    last = nc.vector.scalar_tensor_tensor(out=Klo[r, h, :], in0=TB[r, 0:KEYS], scalar=k_b[r, 0:1],
                                                          in1=Khi[r, h, :].bitcast(F32), op0=ALU.add, op1=ALU.subtract)
                last.then_inc(s["k_lo"], 1)
                dve.wait_ge(s["v_pe"], b + 1)
                nc.vector.tensor_tensor(V4[:, :, :], OB[:, 0:2 * P].rearrange("p (j v) -> p j v", j=2),
                                        v_b_rows[:, :].unsqueeze(1).broadcast_to((P, 2, P)), ALU.add).then_inc(s["v_dve"], 1)
                attention(b, 0, True)
                dve.wait_ge(s["post_used"], b * 16 + NT)
                layer_norm(lambda i: conv_out[:, i, :], lambda i: conv_out[:, i, :], s["cln_ready"])
                dve.wait_ge(s["clnT_pe"], b + 1)
                nc.vector.tensor_copy(conv_lnT[:, 512:1024], TB[:, :]).then_inc(s["clnT_dve"], 1)
                dve.wait_ge(s["o_pe"], b + 1)
                nc.vector.tensor_tensor(x_new[:, :].unsqueeze(1), S[0][:, :].unsqueeze(1), x[:, bass.ds(b, 1), :], ALU.add).then_inc(s["xnew_ready"], 1)
                dve.wait_ge(s["t_act"], b + 1)
                layer_norm(lambda i: tok[:, i, :], lambda i: tok_ln[:, i, :], s["tln_ready"])
                dve.wait_ge(s["tln_ready"], b + 1)
                link(nc.vector.tensor_tensor(tok[:, :, :], tok[:, :, :], tok_ln[:, :, :], ALU.add))
                dve.wait_ge(s["tlnT_pe"], b + 1)
                nc.vector.tensor_copy(tok_lnT[:, 512:1024], TB[:, :]).then_inc(s["tlnT_dve"], 1)
                link(nc.vector.tensor_tensor(tok[:, :, :], tok[:, :, :],
                                             b_o_rows[:, :].unsqueeze(1).broadcast_to((P, NT, C)), ALU.add))
                dve.wait_ge(s["Q_hi"], b + 1)
                nc.vector.tensor_tensor(QS[U:P, :], S[0][U:P, :], QS[U:P, :].bitcast(F32), ALU.subtract).then_inc(s["Q_lo"], 1)
                dve.wait_ge(s["K_hi"], b + 1)
                nc.vector.tensor_tensor(KL[:, :], S[1][:, :], KH[:, :].bitcast(F32), ALU.subtract).then_inc(s["K_lo"], 1)
                dve.wait_ge(s["V_pe"], b + 1)
                nc.vector.tensor_copy(Vt[:, 4:8, :], TB[:, :].rearrange("p (i u) -> p i u", i=4)[:, :, 0:U]).then_inc(s["V_dve"], 1)
                attention(b, NT, False)
                dve.wait_ge(s["post_used"], b * 16 + 2 * NT)
                t1v = lambda i: t1[:, bass.ds(b * NT + i, 1), :].rearrange("p a c -> p (a c)")
                x2v = lambda i: x2[:, i, :]
                layer_norm(t1v, x2v, s["x2_ready"])
                dve.wait_ge(s["x2_ready"], b + 1)
                dve.wait_ge(s["dispatched"], 16 * 2 * TT * half)
                for k in range(2):
                    last = nc.vector.tensor_copy(rows[k][:, bass.ds((b - half * HALF_B) * NT, NT), 0:C], x2[:, :, :])
                link(last)
                dve.wait_ge(s["x2T_pe"], b + 1)
                nc.vector.tensor_copy(x2T[:, 512:1024], TB[:, :]).then_inc(s["x2T_dve"], 1)
                dve.wait_ge(s["l_pe"], b + 1)
                nc.vector.tensor_copy(logits[:, bass.ds(b * NT, NT), :],
                                      S[0][:, :].rearrange("p (i e) -> p i e", i=NT)[:, :, 0:E]).then_inc(s["l_dve"], 1)

            def route(half):
                step = Steps(s["r_step"], half * ROUTE_STEPS)
                V = nc.vector
                L = logits[:, half * TT:(half + 1) * TT, :]
                dve.wait_ge(s["l_dve"], HALF_B * (half + 1))
                wide = lambda t: t[:, :].unsqueeze(2).broadcast_to((P, TT, E))
                R, r = r8, r1

                def first_of(values, m, onehot):
                    step(V.tensor_reduce(r[m][:, :], values, AX.X, ALU.max))
                    step(V.tensor_tensor(R["eq"][:, :, :], values, wide(r[m]), ALU.is_equal))
                    step(V.tensor_tensor(R["w"][:, :, :], R["eq"][:, :, :], rev[:, :, :], ALU.mult))
                    step(V.tensor_reduce(r["mw"][:, :], R["w"][:, :, :], AX.X, ALU.max))
                    step(V.tensor_tensor(R[onehot][:, :, :], R["w"][:, :, :], wide(r["mw"]), ALU.is_equal))

                first_of(L, "m1", "oh1")
                V.tensor_tensor(R["ex"][:, :, :], L, wide(r["m1"]), ALU.subtract).then_inc(s["r_exp_in"], 1)
                step(V.scalar_tensor_tensor(out=R["l2"][:, :, :], in0=R["oh1"][:, :, :], scalar=BIG, in1=L,
                                            op0=ALU.mult, op1=ALU.add))
                first_of(R["l2"][:, :, :], "m2", "oh2")
                step(V.tensor_tensor(R["a"][:, :, :], R["oh1"][:, :, :], R["oh2"][:, :, :], ALU.add))
                src = "a"
                for n, d in enumerate((1, 2, 4, 8)):
                    dst = ("c0", "c1")[n % 2]
                    V.tensor_copy(R[dst][:, 0:d, :], R[src][:, 0:d, :])
                    step(V.tensor_tensor(R[dst][:, d:TT, :], R[src][:, d:TT, :], R[src][:, 0:TT - d, :], ALU.add))
                    src = dst
                V.tensor_tensor(R["c0"][:, :, :], R["c1"][:, :, :], R["a"][:, :, :], ALU.subtract).then_inc(s["r_cnt_in"], 1)
                dve.wait_ge(s["r_exp"], half + 1)
                step(V.tensor_reduce(r["z"][:, :], R["ex"][:, :, :], AX.X, ALU.add))
                step(V.tensor_tensor(R["tmp"][:, :, :], R["ex"][:, :, :], R["oh2"][:, :, :], ALU.mult))
                step(V.tensor_reduce(r["e2"][:, :], R["tmp"][:, :, :], AX.X, ALU.add))
                step(V.reciprocal(r["p1"][:, :], r["z"][:, :]))
                step(V.tensor_tensor(r["p2"][:, :], r["e2"][:, :], r["p1"][:, :], ALU.mult))
                step(V.scalar_tensor_tensor(out=r["s"][:, :], in0=r["p1"][:, :], scalar=1e-9, in1=r["p2"][:, :],
                                            op0=ALU.add, op1=ALU.add))
                step(V.reciprocal(r["z"][:, :], r["s"][:, :]))
                dve.wait_ge(s["init_z"], 3)
                for k, p in enumerate(("p1", "p2")):
                    step(V.tensor_tensor(rows[k][:, :, C + 1], r[p][:, :], r["z"][:, :], ALU.mult))
                dve.wait_ge(s["r_pe"], half + 1)
                step(V.tensor_scalar(cnt_i[:, :], MB[:, 128:128 + E], float(P - 1), None, ALU.add))
                step(V.tensor_scalar(cnt_i[:, :], cnt_i[:, :], 7, None, ALU.logical_shift_right))
                step(V.tensor_copy(cnt[:, :], cnt_i[:, :]))
                src = cnt
                for n, d in enumerate((1, 2, 4)):
                    V.tensor_copy(cum[n % 2][:, 0:d], src[:, 0:d])
                    step(V.tensor_tensor(cum[n % 2][:, d:E], src[:, d:E], src[:, 0:E - d], ALU.add))
                    src = cum[n % 2]
                step(V.tensor_tensor(tile_cmp[:, :, :], tile_no[:, :, :],
                                     cum[0][:, :].unsqueeze(1).broadcast_to((P, SLOT_TILES, E)), ALU.is_ge))
                step(V.tensor_reduce(tile_sum[:, :], tile_cmp[:, :, :], AX.X, ALU.add))
                step(V.tensor_scalar(tile_expert[:, half, :], tile_sum[:, :], float(E - 1), None, ALU.min))
                step(V.tensor_tensor(cum[1][:, :], cum[0][:, :], cnt[:, :], ALU.subtract))
                step(V.tensor_scalar(cum[1][:, :], cum[1][:, :], float(P), None, ALU.mult))
                step(V.tensor_tensor(R["rank"][:, :, :], MB[:, 0:TT * E].rearrange("p (i e) -> p i e", e=E),
                                     cum[1][:, :].unsqueeze(1).broadcast_to((P, TT, E)), ALU.add))
                for k, oh in enumerate(("oh1", "oh2")):
                    step(V.tensor_tensor(R["tmp"][:, :, :], R["rank"][:, :, :], R[oh][:, :, :], ALU.mult))
                    step(V.tensor_reduce(r["pos"][:, :], R["tmp"][:, :, :], AX.X, ALU.add))
                    last = V.tensor_copy(pos_i[:, half, k, :], r["pos"][:, :])
                    if k == 0:
                        step(last)
                last.then_inc(s["route_done"], 1)
                assert step.n == ROUTE_STEPS, step.n

            dve.wait_ge(s["w_in"], 16 * N_W)
            for half in range(2):
                with dve.Fori(half * HALF_B, (half + 1) * HALF_B) as b:
                    link = Steps(s["dve_step"], b * IMAGE_STEPS)
                    image(b, half)
                    assert link.n == IMAGE_STEPS, link.n
                route(half)

            def hidden(n, q, k):
                dve.wait_ge(s["silu_done"], n + 1)
                wait_if(dve, s["hT_pe"], n - (NC - 1))
                nc.vector.tensor_tensor(hid[:, k % NC, 0:H], S[k % 2][:, 512:512 + H], act_h[:, k % NC, :], ALU.mult).then_inc(s["hid_ready"], 1)

            def hidden_copy(n, q, k):
                dve.wait_ge(s["hT_pe"], n + 1)
                wait_if(dve, s["y_pe"], n - (NC - 1))
                nc.vector.tensor_copy(hidT[0:HC, k % NC, :], TA[0:HC, 0:CHUNKS * P]).then_inc(s["hT_dve"], 1)

            dve.wait_ge(s["init_done"], 32)
            nc.vector.memset(hid[:, :, :], 0.0).then_inc(s["pad_z"], 1)
            dve.wait_ge(s["pad_z"], 2)
            for half in range(2):
                schedule(dve, half, (("B", hidden), ("C", hidden_copy)))
            for q in range(2 * TT // 4):
                dve.wait_ge(y12_in[q % 2], 16 * (q // 2 + 1))
                t = t1[:, 4 * q:4 * q + 4, :]
                nc.vector.tensor_tensor(t, t, y12[:, q % 2, :, 0:C], ALU.add).then_inc(s["sum_step"], 1)
                dve.wait_ge(s["sum_step"], q + 1)
                nc.vector.tensor_tensor(t, t, y12[:, q % 2, :, C:2 * C], ALU.add).then_inc(s["sum_ready"], 1)

        @block.tensor
        def _(pe):
            mm, tr = nc.tensor.matmul, nc.tensor.transpose

            pe.wait_ge(s["const_set"], 5)
            pe.wait_ge(s["gn_dve"], 1)
            mm(S[0][:, 0:2 * B], groups[:, :], chan_mv[:, :, :].rearrange("p b s -> p (b s)"), start=True, stop=True).then_inc(s["gn_pe"], 1)
            pe.wait_ge(s["gn_dve"], 2)
            mm(S[0][:, 0:B], groups[:, :], dev[:, :], start=True, stop=True).then_inc(s["gn_pe"], 1)
            pe.wait_ge(s["w_in"], 16 * N_W)
            for i, (src, _) in enumerate(SMALL_T):
                last = tr(SMALL_BANK[i // 4][:, tile(i % 4)], src, ident[:, :])
                if i == len(SMALL_T) - 1:
                    last = tr(TB[:, P:P + E], router_in[:, :], ident[0:E, 0:E])
                if i % 4 == 3 or i == len(SMALL_T) - 1:
                    last.then_inc(s["wt_done"], 1)
            pe.wait_ge(s["small_in"], 16 * 14)
            pe.wait_ge(s["bias_used"], 1)
            mm(OB[:, tile(0)], ones[0:1, :], rows_in[0:1, 0, :], start=True, stop=True)
            mm(OB[:, tile(1)], lnb_rep[:, :], o_wT[:, :], start=True, stop=False)
            mm(OB[:, tile(1)], ones[0:1, :], rows_in[0:1, 1, :], start=False, stop=True)
            mm(OB[:, tile(2)], ones[0:1, :], rows_in[0:1, 2, :], start=True, stop=True).then_inc(s["bias_done"], 1)
            pe.wait_ge(s["w2stage_in"], 16)
            for e in range(E):
                pe.wait_ge(s[f"wx{e % 3}"], 16 * 6 * (e // 3 + 1))
                if e >= 2:
                    pe.wait_ge(s["wexp_copied"], e - 1)
                for m in range(2):
                    for c in range(CHUNKS):
                        n = min(HC, H - c * HC)
                        last = tr(S[e % 2][:, m * 512 + c * HC:m * 512 + c * HC + n],
                                  wstage[0:n, e % 3, (m * CHUNKS + c) * C:(m * CHUNKS + c + 1) * C], ident[0:n, 0:n])
                last.then_inc(s["wexp_pe"], 1)
                T = TA if e % 2 == 0 else TB
                if e >= 2:
                    pe.wait_ge(s["w2_copied"], e - 1)
                else:
                    pe.wait_ge(s["wt_used"], 4)
                for c in range(CHUNKS):
                    n = min(HC, H - c * HC)
                    last = tr(T[0:n, tile(c)], w2stage[:, e, c * HC:c * HC + n], ident[:, :])
                last.then_inc(s["w2_pe"], 1)
            pe.wait_ge(s["wexp_copied"], E)
            pe.wait_ge(s["w2_copied"], E)
            pe.wait_ge(s["pad_z"], 1)
            pe.wait_ge(s["bias_used"], 2)

            def scores(b, g, conv):
                j = g % NT
                if j >= 2:
                    pe.wait_ge(s["exp_done"], b * 16 + (g - 1))
                if conv:
                    for half in range(2):
                        dst = S[j % 2][:, half * 512:(half + 1) * 512]
                        kh = Khi[:, 2 * half:2 * half + 2, :].rearrange("p h k -> p (h k)")
                        kl = Klo[:, 2 * half:2 * half + 2, :].rearrange("p h k -> p (h k)")
                        mm(dst, Qhi[:, tile(j)], kh, start=True, stop=False)
                        mm(dst, Qhi[:, tile(j)], kl, start=False, stop=False)
                        last = mm(dst, Qlo[:, tile(j)], kh, start=False, stop=True)
                else:
                    for half in range(2):
                        r = slice(half * 512, (half + 1) * 512)
                        mm(S[j % 2][:, r], QS[:, tile(j)], KH[:, r], start=True, stop=False)
                        last = mm(S[j % 2][:, r], QS[:, tile(j)], KL[:, r], start=False, stop=True)
                last.then_inc(s["scores_done"], 1)

            def probs_T(b, g):
                pe.wait_ge(s["exp_done"], b * 16 + (g + 1))
                if g % NT:
                    pe.wait_ge(s["ptA_copied"], b * 16 + g)
                    pe.wait_ge(s["ptB_copied"], b * 16 + g)
                for k in range(8):
                    last = tr((TA if k < 4 else TB)[:, tile(k % 4)], probs[:, g % 2, tile(k)], ident[:, :])
                last.then_inc(s["pt_done"], 1)

            def values(b, g, conv):
                pe.wait_ge(s["ptA_copied"], b * 16 + (g + 1))
                pe.wait_ge(s["ptB_copied"], b * 16 + (g + 1))
                if g % NT:
                    pe.wait_ge(s["ot_copied"], b * 16 + g)
                pT = probsT[:, g % 2, :]
                if conv:
                    for st in range(2):
                        for h in range(HEADS):
                            last = mm(OB[h * HD:(h + 1) * HD, 0:P], V4[:, st, h * HD:(h + 1) * HD],
                                      pT[:, tile(2 * h + st)], start=(st == 0), stop=(st == 1))
                else:
                    for kt in range(NT):
                        r = slice((kt % 2) * U, (kt % 2 + 1) * U)
                        last = mm(OB[r, 0:P], Vt[:, kt, :], pT[:, tile(kt)], start=(kt < 2), stop=(kt >= NT - 2))
                last.then_inc(s["pv_done"], 1)

            def post(b, g, conv):
                pe.wait_ge(s["ot_copied"], b * 16 + (g + 1))
                if g:
                    pe.wait_ge(s["post_used"], b * 16 + g)
                if conv:
                    last = tr(MB[:, 0:P], outT[:, g % 2, :], ident[:, :])
                else:
                    last = mm(MB[:, 0:P], outT[:, g % 2, :], Wo2[:, :], start=True, stop=True)
                last.then_inc(s["post_done"], 1)

            def attention(b, g0, conv):
                scores(b, g0, conv)
                for g in range(g0, g0 + NT):
                    if g + 1 < g0 + NT:
                        scores(b, g + 1, conv)
                    if g > g0:
                        values(b, g - 1, conv)
                    probs_T(b, g)
                    if g > g0:
                        post(b, g - 1, conv)
                values(b, g0 + NT - 1, conv)
                post(b, g0 + NT - 1, conv)

            def transpose8(src, done):
                for i in range(NT):
                    last = tr((TA if i < 4 else TB)[:, tile(i % 4)], src[:, i, :], ident[:, :])
                last.then_inc(done, 1)

            def image(b):
                pe.wait_ge(s["l_dve"], b)
                pe.wait_ge(s["x2T_dve"], b)
                pe.wait_ge(s["post_used"], b * 16)
                xb = xn_b[:, :]
                pe.wait_ge(s["xb_ready"], b + 1)
                for j in range(NT):
                    last = mm(S[0][:, tile(j)], xb[:, tile(j)], wK_T[:, :], start=True, stop=True)
                last.then_inc(s["kT_pe"], 1)
                pe.wait_ge(s["taps_ready"], b + 1)
                for jj in range(2):
                    for tap in range(4):
                        last = mm(TA[:, jj * 2 * C:(jj + 1) * 2 * C], taps[:, tap, jj * P:(jj + 1) * P],
                                  wQV_T[:, tap, :, :].rearrange("p m c -> p (m c)"), start=(tap == 0), stop=(tap == 3))
                last.then_inc(s["qv_pe"], 1)
                pe.wait_ge(s["kT_act"], b + 1)
                pe.wait_ge(s["kT_dve"], b + 1)
                for half in range(2):
                    r = slice(half * 512, (half + 1) * 512)
                    last = mm(S[1][:, r], q_wT[:, :], kT[:, r], start=True, stop=True)
                last.then_inc(s["q_pe"], 1)
                pe.wait_ge(s["qv_act"], b + 1)
                mm(TB[:, 0:KEYS], k_wT[:, :], qvT[:, :, 0, :], start=True, stop=True).then_inc(s["k_pe"], 1)
                for jj in range(2):
                    last = mm(OB[:, tile(jj)], qvT[:, jj, 1, :], v_wT[:, :], start=True, stop=True)
                last.then_inc(s["v_pe"], 1)
                for n in ("q_lo", "k_lo", "v_dve"):
                    pe.wait_ge(s[n], b + 1)
                attention(b, 0, True)
                pe.wait_ge(s["cln_ready"], b + 1)
                transpose8(conv_out, s["clnT_pe"])
                pe.wait_ge(s["clnT_act"], b + 1)
                pe.wait_ge(s["clnT_dve"], b + 1)
                for j in range(NT):
                    last = mm(S[0][:, tile(j)], conv_lnT[:, tile(j)], o_wTg[:, :], start=True, stop=True)
                last.then_inc(s["o_pe"], 1)
                pe.wait_ge(s["xnew_ready"], b + 1)
                for i in range(NT):
                    last = tr(S[1][:, tile(i)], x_new[:, tile(i)], ident[:, :])
                last.then_inc(s["t_pe"], 1)
                pe.wait_ge(s["tln_ready"], b + 1)
                transpose8(tok_ln, s["tlnT_pe"])
                pe.wait_ge(s["tlnT_act"], b + 1)
                pe.wait_ge(s["tlnT_dve"], b + 1)
                for dst, w, done in ((S[0], Wq2, "Q_pe"), (S[1], Wk2, "K_pe")):
                    for half in range(2):
                        r = slice(half * 512, (half + 1) * 512)
                        last = mm(dst[:, r], w[:, :], tok_lnT[:, r], start=True, stop=True)
                    last.then_inc(s[done], 1)
                for i in range(NT):
                    last = mm((TA if i < 4 else TB)[:, tile(i % 4)], tok_lnT[:, tile(i)], Wv2[:, :], start=True, stop=True)
                last.then_inc(s["V_pe"], 1)
                for n in ("Q_lo", "K_lo", "V_act", "V_dve"):
                    pe.wait_ge(s[n], b + 1)
                attention(b, NT, False)
                pe.wait_ge(s["x2_ready"], b + 1)
                transpose8(x2, s["x2T_pe"])
                pe.wait_ge(s["x2T_act"], b + 1)
                pe.wait_ge(s["x2T_dve"], b + 1)
                for i in range(NT):
                    last = mm(S[0][:, tile(i)], x2T[:, tile(i)], router_T[:, :], start=True, stop=True)
                last.then_inc(s["l_pe"], 1)

            for half in range(2):
                with pe.Fori(half * HALF_B, (half + 1) * HALF_B) as b:
                    image(b)
                pe.wait_ge(s["r_cnt_in"], half + 1)
                mm(MB[:, 0:TT * E], before[:, :], r8["a"][:, :, :].rearrange("p i e -> p (i e)"), start=True, stop=False)
                mm(MB[:, 0:TT * E], ones[:, :], r8["c0"][:, :, :].rearrange("p i e -> p (i e)"), start=False, stop=True)
                mm(MB[:, P:P + E], ones[:, :], r8["c1"][:, TT - 1, :], start=True, stop=True).then_inc(s["r_pe"], 1)

            def token_T(n, q, k):
                pe.wait_ge(xs_in[k], q * 16 + 16)
                wait_if(pe, s["xsT_act"], n)
                tr(OB[:, 0:P], xs[:, k, 0:C], ident[:, :]).then_inc(s["xsT_pe"], 1)

            def hidden(n, q, k):
                e = expert_of(n)
                pe.wait_ge(s["xsT_act"], n + 1)
                wait_if(pe, s["hid_ready"], n - 1)
                for m in range(2):
                    last = mm(S[k % 2][:, m * 512:m * 512 + H], xsT[:, k % NC, :],
                              w13_T[:, bass.ds(e, 1), m * H:(m + 1) * H].rearrange("p a h -> p (a h)"), start=True, stop=True)
                last.then_inc(s["h_pe"], 1)

            def hidden_T(n, q, k):
                pe.wait_ge(s["hid_ready"], n + 1)
                wait_if(pe, s["hT_dve"], n)
                for c in range(CHUNKS):
                    last = tr(TA[0:HC, tile(c)], hid[:, k % NC, c * HC:(c + 1) * HC], ident[:, :])
                last.then_inc(s["hT_pe"], 1)

            def output(n, q, k):
                e = expert_of(n)
                pe.wait_ge(s["hT_dve"], n + 1)
                wait_if(pe, s["ys_ready"], n)
                for c in range(CHUNKS):
                    last = mm(MB[:, 0:P], hidT[0:HC, k % NC, tile(c)],
                              w2_T[0:HC, bass.ds(e, 1), tile(c)].rearrange("p a c -> p (a c)"), start=(c == 0), stop=(c == CHUNKS - 1))
                last.then_inc(s["y_pe"], 1)

            def expert_of(n):
                te = tile_expert[0:1, :, :].rearrange("p h i -> p (h i)")
                i = bass.ds(n, 1) if not isinstance(n, int) else slice(n, n + 1)
                return pe.value_load(te[:, i], min_val=0, max_val=E - 1)

            for half in range(2):
                pe.wait_ge(s["route_done"], half + 1)
                schedule(pe, half, (("B", hidden), ("T", token_T), ("D", output), ("C", hidden_T)))
            for q in range(2 * TT // 4):
                pe.wait_ge(s["sum_ready"], q + 1)
                if q >= 2:
                    pe.wait_ge(s["fin_act"], q - 1)
                T = TA if q % 2 == 0 else TB
                for i in range(4):
                    last = tr(T[:, tile(i)], t1[:, 4 * q + i, :], ident[:, :])
                last.then_inc(s["fin_pe"], 1)


INPUTS = ["x"] + ["L0_conv_" + n for n in "wK wQ wV q_w q_b k_w k_b v_w v_b ln_g ln_b o_w o_b".split()] + \
    ["L1_attn_" + n for n in "W_q W_k W_v W_o b_o".split()] + ["L1_ffn_" + n for n in "router_w w1 w2 w3".split()]


def kernel(**inputs):
    import numpy as np
    from concourse import bacc
    from concourse.bass_utils import run_bass_kernel_spmd

    nc = bacc.Bacc("TRN2", target_bir_lowering=False, num_devices=1)
    arrays, aps = {}, {}
    for name in INPUTS:
        v = np.ascontiguousarray(inputs[name])
        arrays["in_" + name] = v
        aps[name] = nc.dram_tensor("in_" + name, v.shape, mybir.dt.from_np(v.dtype), kind="ExternalInput").ap()
    out = nc.dram_tensor("out", (B, C, 32, 32), F32, kind="ExternalOutput").ap()
    build(nc, aps, out)
    r = run_bass_kernel_spmd(nc, [arrays], core_ids=[0])
    return r.results[0]["out"]
```

```python
from contextlib import ExitStack

import concourse.bass as bass
from concourse import mybir

F32 = mybir.dt.float32
F32R = mybir.dt.float32r
I32 = mybir.dt.int32
ALU = mybir.AluOpType
ACT = mybir.ActivationFunctionType
AX = mybir.AxisListType

P = 128
B, C, HW = 4, 128, 1024
NT = HW // P
HEADS, HD, KEYS = 4, 32, 256
U = 64
E, H = 8, 341
HC = 114
CHUNKS = 3
HALF_B = 2
TT = HALF_B * NT
HALF_TOK = TT * P
NB = 8
NC = 4
SLOT_TILES = -(-(2 * HALF_TOK // P + E - 1) // NB) * NB
TURNS = SLOT_TILES // NB
SLOTS = SLOT_TILES * P
ROW = C + 2
Y_ROWS = 2 * HALF_TOK + SLOTS
CONV_SCALE = float(HD) ** -0.5
TOK_SCALE = float(U) ** -0.5
GROUP = 4
DISPATCH_FROM = 10
MAGIC = 0x5F3759DF
BIG = -3.0e38
CUT = 512
NEWTON = 3

SLOTS_OF_STEP = 3
PRE_A = "xn kT0 kT1 qv0 qv1 V"
PRE_Q = "K Q0 Q1"
EARLY = "cs0 cs1 - ca0 ca1+c0 c1 o0 o1+t0 t1 ts0 ts1 - ta0 ta1"
MID = "l0 l1 v0 v1 q0 k0 k1 q1"
POST = "ps0 ps1 - pa0 pa1+pc+r0 r1 g0 g1"
ROUTE = "ra rb rc rank rd re rf"


def units(text, b):
    return [[(u, b) for u in slot.split("+") if u != "-"] for slot in text.split()]


def overlay(base, *others):
    slots = base + [[] for _ in range(max(at + len(more) for at, more in others) - len(base))]
    for at, more in others:
        for i, slot in enumerate(more):
            slots[at + i] = slots[at + i] + slot
    return slots


W = "- "
PHASES = [
    ("conv", 0, units(W * 5 + PRE_A, 1), units(PRE_Q, 1)),
    ("conv", 1, units(W * 3 + EARLY, 0) + units(PRE_A, 2), units(PRE_Q, 2)),
    ("conv", 2, units(MID, 0) + units(EARLY, 1), []),
    ("tok", 0, units(W * 4 + PRE_A + " " + PRE_Q, 3), []),
    ("conv", 3, overlay(units(MID, 1), (4, units(POST, 0)), (10, units(EARLY, 2))), []),
    ("tok", 1, units(MID, 2) + units(EARLY, 3), []),
    ("tok", 2, units(MID, 3) + units(POST, 1) + units(ROUTE, 0), []),
    ("tok", 3, units(W * 4 + POST.replace("+pc", ""), 2), []),
]
FIRST = units(PRE_A + " " + PRE_Q, 0)
LAST = units("ps0+ps1 pa0+pa1+pc r0 r1 g0+g1", 3) + units("ra rb rc rank rd re rf", 1)
LAST[0].append(("pc", 2))
STEPS = NT * len(PHASES)


def flat(slots):
    return [f for slot in slots for f in slot]


LAST_UNITS = flat(LAST)
FILLERS = flat(FIRST) + [f for _, _, inner, behind in PHASES for f in flat(inner + behind)] + LAST_UNITS
BANKED = [f for f in FILLERS if f[0] in "kT0 kT1 qv0 qv1 Q0 Q1 K V c0 c1 o0 o1 t0 t1 l0 l1 q0 q1 k0 k1 v0 v1 r0 r1 g0 g1 rank".split()]
NORMS = [f for f in FILLERS if f[0] in ("cs1", "ts1", "ps1")]
TOK_SET = [0, 0, 1, 0]


def build(nc, a, out):
    ctx = ExitStack()
    with ctx:
        def sb(name, shape, dt=F32):
            return ctx.enter_context(nc.sbuf_tensor(name, shape, dt))

        def ps(name, shape, dt=F32):
            return ctx.enter_context(nc.psum_tensor(name, shape, dt))

        def sem(name):
            return ctx.enter_context(nc.semaphore(name))

        ident = sb("ident", [P, P])
        ones = sb("ones", [P, P])
        spare = sb("spare", [P, 2])
        before = sb("before", [P, P])
        groups = sb("groups", [P, P])
        rev = sb("rev", [P, TT, E])
        tile_no = sb("tile_no", [P, SLOT_TILES, E])
        router_in = sb("router_in", [E, C])
        rows_in = sb("rows_in", [1, 3, P])
        q_b = sb("q_b", [P, 1])
        k_b = sb("k_b", [P, 1])
        ln_g = sb("ln_g", [P, 1])
        ln_b = sb("ln_b", [P, 1])
        wK_T = sb("wK_T", [P, C])
        wQV_T = sb("wQV_T", [P, 4, 2, C])
        q_wT = sb("q_wT", [P, P])
        k_wT = sb("k_wT", [P, P])
        v_wT = sb("v_wT", [P, P])
        o_wT = sb("o_wT", [P, P])
        o_wTg = sb("o_wTg", [P, P])
        Wq2 = sb("Wq2", [P, P])
        Wk2 = sb("Wk2", [P, P])
        Wv2 = sb("Wv2", [P, P])
        Wo2 = sb("Wo2", [P, C])
        router_T = sb("router_T", [P, P])
        v_b_rows = sb("v_b_rows", [P, P])
        o_b_rows = sb("o_b_rows", [P, P])
        b_o_rows = sb("b_o_rows", [P, P])
        w13_T = sb("w13_T", [P, E, 2 * H])
        w2_T = sb("w2_T", [P, E, CHUNKS * C])
        x = sb("x", [P, B, HW])
        chan = sb("chan", [P, B, 2, 6])
        chan_mv = sb("chan_mv", [P, B, 2])
        grp = sb("grp", [P, B, 2])
        dev = sb("dev", [P, B])
        gvar = sb("gvar", [P, 8])
        operandT = sb("operandT", [P, HW])
        wK_in, qw_in, kw_in, vw_in, ow_in = (operandT[:, k * P:(k + 1) * P] for k in range(5))
        qvT = sb("qvT", [P, 2, 2, C])
        Qhi = sb("Qhi", [P, HW], F32R)
        Qlo = sb("Qlo", [P, HW], F32R)
        Khi = sb("Khi", [P, HEADS, KEYS], F32R)
        Klo = sb("Klo", [P, HEADS, KEYS], F32R)
        QS = [sb("QS", [P, HW], F32R)[:, :], Qhi[:, :]]
        KH = [sb("KH", [P, HW], F32R)[:, :], Qlo[:, :]]
        KL = [sb("KL", [P, HW], F32R)[:, :], Khi[:, :, :].rearrange("p h k -> p (h k)")]
        V4 = sb("V4", [P, 2, 2, P])
        Vt = sb("Vt", [P, 2, NT, U])
        shared = sb("shared", [P, 4 * HW])
        probs = shared[:, 0:2 * HW].rearrange("p (i n) -> p i n", i=2)
        probsT = shared[:, 2 * HW:4 * HW].rearrange("p (i n) -> p i n", i=2)
        w1stage = shared[:, 0:CHUNKS * E * C].rearrange("p (c e n) -> p c e n", c=CHUNKS, e=E)
        outT = sb("outT", [P, 2, P])
        late = sb("late", [P, 6 * HW])
        piece = lambda i: late[:, i * HW:(i + 1) * HW].rearrange("p (i c) -> p i c", i=NT)
        normed = piece(0)
        conv_out = [piece(1), piece(2)]
        tok = [piece(3), piece(4), piece(5)]
        lnb_rep = sb("lnb_rep", [P, P])
        pixels = sb("pixels", [P, HW])
        xn_b = x_new = pixels
        taps = sb("taps", [P, 4, 256])
        wQ_in, wV_in = (taps[:, 2 * k:2 * k + 2, :].rearrange("p t n -> p (t n)") for k in range(2))
        t1 = sb("t1", [P, B * NT, C])
        w3stage = t1[:, 0:CHUNKS * E, :].rearrange("p (c e) n -> p c e n", c=CHUNKS)
        rows_both = sb("rows_both", [P, 2 * TT * ROW])
        rows = [rows_both[:, k * TT * ROW:(k + 1) * TT * ROW].rearrange("p (i c) -> p i c", i=TT) for k in range(2)]
        w2stage = rows_both[:, 0:E * H].rearrange("p (e h) -> p e h", e=E)
        logits = sb("logits", [P, 2 * TT, E])
        stats = sb("stats", [P, NT, 6])
        mv = sb("mv", [P, NT, 2])
        rs_v = sb("rs_v", [P, NT])
        rs_a = sb("rs_a", [P, NT])
        rs_y = sb("rs_y", [P, NT])
        minus_half = sb("minus_half", [P, NT])
        rs_i = sb("rs_i", [P, NT], I32)
        rowmax = sb("rowmax", [P, 2, HEADS])
        negmax = sb("negmax", [P, 2, HEADS])
        rowsum = sb("rowsum", [P, 4, HEADS])
        rowinv = sb("rowinv", [P, 4, HEADS])
        r8 = {n: sb("r_" + n, [P, TT, E]) for n in ("eq", "w", "oh1", "oh2", "l2", "ex", "a", "c0", "c1", "rank", "tmp")}
        r1 = {n: sb("r1_" + n, [P, TT]) for n in ("m1", "m2", "mw", "z", "e2", "p1", "p2", "g1", "g2", "s", "pos")}
        pos_i = sb("pos_i", [P, 2, 2, TT], I32)
        cnt = sb("cnt", [P, E])
        cnt_i = sb("cnt_i", [P, E], I32)
        cum = [sb(f"cum{k}", [P, E]) for k in range(2)]
        tile_cmp = sb("tile_cmp", [P, SLOT_TILES, E])
        tile_sum = sb("tile_sum", [P, SLOT_TILES])
        tile_expert = sb("tile_expert", [P, 2, SLOT_TILES], I32)
        empty = late[:, 0:SLOT_TILES * ROW].rearrange("p (k c) -> p k c", c=ROW)

        def carve(base, at, n, width):
            return base[:, at:at + n * width].rearrange("p (i n) -> p i n", i=n), at + n * width

        xs = sb("xs", [P, NB, ROW])
        hid, at = carve(late, 0, NC, CHUNKS * HC)
        y12, at = carve(late, at, 2, 4 * 2 * C)
        y12 = y12.rearrange("p i (t n) -> p i t n", t=4)
        res = x[:, 0, :].rearrange("p (i n) -> p i n", i=2)
        assert at <= SLOT_TILES * ROW
        hidT, at = carve(shared, 0, NC, CHUNKS * P)
        act_h, at = carve(shared, at, NC, H)
        xsT, at = carve(shared, at, NC, P)
        ys, at = carve(shared, at, NC, C)
        assert at <= 4 * HW

        slots = [nc.dram_tensor(f"slots{h}", [SLOTS, ROW], F32).ap() for h in range(2)]
        y_rows = [nc.dram_tensor(f"y_rows{h}", [Y_ROWS, C], F32).ap() for h in range(2)]

        S = [ps(f"S{i}", [P, HW]) for i in range(2)]
        OM, PO, TA, TB = (ps(n, [P, 512]) for n in ("OM", "PO", "TA", "TB"))

        names = """x_in w_in const_z const_set pad_z wt_done wt_used bias_done bias_used
            gn_pe gn_dve w1_in w3_in w2stage_in small_in w2_pe w2_copied wexp_pe wexp_copied dve_pre
            scores_done neg_ready exp_done pt_done ptA_copied ptB_copied pv_done ot_copied post_done post_used
            dve_step fill_done fill_copied0 fill_copied1 xn_ready taps_ready hi_done x_added lo_ready norm_stats norm_step norm_rstd normed_ready
            tok_ready rows_set
            r_exp_in r_exp r_cnt_in route_done pool_step init_z init_done dispatched0 dispatched1
            xs_in0 xs_in1 xs_in2 xs_in3 xs_in4 xs_in5 xs_in6 xs_in7 xsT_pe xsT_act h_pe silu_done hid_ready hT_pe hT_dve y_pe ys_ready
            ys_out0 ys_out1 ys_out2 ys_out3 ys_out4 ys_out5 ys_out6 ys_out7
            y12_in0 y12_in1 sum_step sum_ready fin_pe fin_act out_done0 out_done1""".split()
        s = {n: sem(n) for n in names}
        xs_in = [s[f"xs_in{k}"] for k in range(NB)]
        ys_out = [s[f"ys_out{k}"] for k in range(NB)]
        y12_in = [s[f"y12_in{k}"] for k in range(2)]

        N_W = 21
        SMALL_T = [
            (wK_in[:, :], wK_T[:, :]),
            *[(wQ_in[:, tap:C * 4:4], wQV_T[:, tap, 0, :]) for tap in range(4)],
            *[(wV_in[:, tap:C * 4:4], wQV_T[:, tap, 1, :]) for tap in range(4)],
            (qw_in[:, :], q_wT[:, :]), (kw_in[:, :], k_wT[:, :]), (vw_in[:, :], v_wT[:, :]), (ow_in[:, :], o_wT[:, :]),
        ]
        SMALL_BANK = [OM, PO, TA, TB]
        BANKS = [TA, TB]
        out_r = out.rearrange("b c h w -> c b (h w)")
        block = ctx.enter_context(nc.Block())

        def tile(i):
            return slice(i * P, (i + 1) * P)

        def wait_if(eng, semaphore, value):
            if not (isinstance(value, int) and value <= 0):
                eng.wait_ge(semaphore, value)

        def nth(f):
            return BANKED.index(f) + 1

        def banked_before(f):
            return sum(g in BANKED for g in FILLERS[:FILLERS.index(f)])

        def before_it(f, *names):
            return sum(g[0] in names for g in FILLERS[:FILLERS.index(f)])

        def bank_of(f):
            return 1 if f in LAST_UNITS else BANKED.index(f) % 2

        def turn_of(f):
            return sum(bank_of(g) == bank_of(f) for g in BANKED[:BANKED.index(f) + 1])

        def wait_copied(eng, *fs):
            for f in fs:
                eng.wait_ge(s[f"fill_copied{bank_of(f)}"], turn_of(f))

        def norm_of(f):
            return NORMS.index(({"c": "cs1", "l": "ts1", "r": "ps1"}.get(f[0][0]) if f[0][1] in "01" else f[0][0] + "s1", f[1]))

        def normed_of(f):
            return {len(NORMS) - 2: taps[:, :, :].rearrange("p t n -> p (t n)").rearrange("p (i c) -> p i c", i=NT),
                    len(NORMS) - 1: pixels[:, :].rearrange("p (i c) -> p i c", i=NT)}.get(norm_of(f), normed)

        def run_phases(step, fill, tail):
            for f in flat(FIRST):
                fill(*f)
            for p, (kind, b, inner, behind) in enumerate(PHASES):
                assert len(inner) <= SLOTS_OF_STEP * NT, (p, len(inner))
                for j in range(NT):
                    def slot(i):
                        n = SLOTS_OF_STEP * j + i
                        for f in inner[n] if n < len(inner) else []:
                            fill(*f)
                        if n == SLOTS_OF_STEP * NT - 1:
                            for f in flat(behind):
                                fill(*f)
                    step(NT * p + j, slot)
            tail()

        def phase_of(g):
            return PHASES[g // NT][0], PHASES[g // NT][1], g % NT

        OFFSET = {"B": 0, "T": 1, "D": -2, "C": -1}

        def schedule(eng, half, stages, fill):
            def step(q, k, i=None):
                for name, stage in stages:
                    d = OFFSET[name]
                    if i is not None and not 0 <= i + d < SLOT_TILES:
                        continue
                    qq = q + (k + d) // NB
                    stage(qq * NB + (k + d) % NB, qq, (k + d) % NB)

            if any(name == "T" for name, _ in stages):
                dict(stages)["T"](half * SLOT_TILES, half * TURNS, 0)
            for i in range(NB):
                step(half * TURNS, i, i)
                if half == 0:
                    for f in flat(LAST[2 * i:2 * i + 2] if i < NB - 1 else LAST[2 * i:]):
                        fill(*f)
            with eng.Fori(half * TURNS + 1, half * TURNS + TURNS - 1) as t:
                for k in range(NB):
                    step(t, k)
            for i in range(SLOT_TILES - NB, SLOT_TILES + 2):
                step(half * TURNS + i // NB, i % NB, i)

        @block.sync
        def _(sp):
            xr = a["x"].rearrange("b c h w -> c b (h w)")
            for b in range(B):
                sp.dma_start(x[:, b, :], xr[:, b, :]).then_inc(s["x_in"], 16)
            sp.dma_start(wK_in[:, :], a["L0_conv_wK"].rearrange("o c h w -> o (c h w)")).then_inc(s["w_in"], 16)
            sp.dma_start(wQ_in[:, :], a["L0_conv_wQ"].rearrange("o c h w -> o (c h w)")).then_inc(s["w_in"], 16)
            sp.dma_start(wV_in[:, :], a["L0_conv_wV"].rearrange("o c h w -> o (c h w)")).then_inc(s["w_in"], 16)
            sp.dma_start(qw_in[:, :], a["L0_conv_q_w"]).then_inc(s["w_in"], 16)
            sp.dma_start(ow_in[:, :], a["L0_conv_o_w"]).then_inc(s["w_in"], 16)
            kv = lambda w: w.rearrange("(k d) e -> k d e", k=2)
            for k in range(2):
                for src, dst in ((a["L0_conv_k_w"], kw_in), (a["L0_conv_v_w"], vw_in)):
                    for g in range(2):
                        sp.dma_start(dst[(2 * k + g) * HD:(2 * k + g + 1) * HD, :], kv(src)[k]).then_inc(s["w_in"], 16)
            col = lambda v: v.rearrange("(p a) -> p a", a=1)
            sp.dma_start(q_b[:, :], col(a["L0_conv_q_b"])).then_inc(s["w_in"], 16)
            sp.dma_start(ln_g[:, :], col(a["L0_conv_ln_g"])).then_inc(s["w_in"], 16)
            sp.dma_start(ln_b[:, :], col(a["L0_conv_ln_b"])).then_inc(s["w_in"], 16)
            for k in range(2):
                for g in range(2):
                    h = 2 * k + g
                    sp.dma_start(k_b[h * HD:(h + 1) * HD, :],
                                 col(a["L0_conv_k_b"])[k * HD:(k + 1) * HD, :]).then_inc(s["w_in"], 16)

            def experts_tiles(half):
                sp.wait_ge(s["init_done"], 32)
                for b in range(HALF_B):
                    sp.wait_ge(s[f"dispatched{b}"], 16 * 2 * NT * (half + 1))

                def load(i, q, k):
                    wait_if(sp, ys_out[k], q * 16)
                    row = bass.ds(i * P, P) if not isinstance(i, int) else slice(i * P, i * P + P)
                    sp.dma_start(xs[:, k, :], slots[half][row, :]).then_inc(xs_in[k], 16)

                for k in range(NB):
                    load(k, half * TURNS, k)
                with sp.Fori(1, TURNS) as t:
                    for k in range(NB):
                        load(t * NB + k, t + half * TURNS, k)

            for half in range(2):
                experts_tiles(half)
            for k in range(NB):
                sp.wait_ge(ys_out[k], 16 * 2 * TURNS)
            y_view = [y_rows[h][0:2 * HALF_TOK, :].rearrange("(i p r) c -> p i (r c)", p=P, r=2) for h in range(2)]
            for q in range(2 * TT // 4 + 2):
                if q < 2 * TT // 4:
                    if q >= 2:
                        sp.wait_ge(s["sum_ready"], q - 1)
                    h, r = q // (TT // 4), q % (TT // 4)
                    sp.dma_start(y12[:, q % 2, :, :], y_view[h][:, r * 4:r * 4 + 4, :]).then_inc(y12_in[q % 2], 16)
                if q >= 2:
                    m = q - 2
                    sp.wait_ge(s["fin_act"], m + 1)
                    sp.dma_start(out_r[:, m // 2, (m % 2) * 512:(m % 2) * 512 + 512],
                                 res[:, m % 2, :]).then_inc(s[f"out_done{m % 2}"], 16)
            for k in range(2):
                sp.wait_ge(s[f"out_done{k}"], 16 * TT // 4)

        @block.gpsimd
        def _(pool):
            for k, (m, v) in enumerate(((ident, 0.0), (ones, 1.0), (before, 1.0), (groups, 1.0 / GROUP), (router_T, 0.0),
                                        (w2_T, 0.0), (empty, 0.0))):
                nc.gpsimd.memset(m if m is empty else m[:], v).then_inc(s["const_z"], 1)
            nc.gpsimd.memset(minus_half[:], -0.5)
            pool.wait_ge(s["const_z"], 7)
            nc.gpsimd.affine_select(out=ident[:, :], in_=ident[:, :], compare_op=ALU.not_equal, fill=1.0, base=0,
                                    pattern=[[-1, P]], channel_multiplier=1).then_inc(s["const_set"], 1)
            nc.gpsimd.affine_select(out=before[:, :], in_=before[:, :], compare_op=ALU.is_gt, fill=0.0, base=0,
                                    pattern=[[1, P]], channel_multiplier=-1).then_inc(s["const_set"], 1)
            gv = groups[:, :].rearrange("p (g r) -> p g r", r=GROUP)
            nc.gpsimd.affine_select(out=gv, in_=gv, compare_op=ALU.is_ge, fill=0.0, base=0,
                                    pattern=[[-GROUP, P // GROUP], [0, GROUP]], channel_multiplier=1).then_inc(s["const_z"], 1)
            pool.wait_ge(s["const_z"], 8)
            nc.gpsimd.affine_select(out=gv, in_=gv, compare_op=ALU.is_ge, fill=0.0, base=GROUP - 1,
                                    pattern=[[GROUP, P // GROUP], [0, GROUP]], channel_multiplier=-1).then_inc(s["const_set"], 1)
            nc.gpsimd.iota(rev[:, :, :], pattern=[[0, TT], [-1, E]], base=E, channel_multiplier=0,
                           allow_small_or_imprecise_dtypes=True).then_inc(s["const_set"], 1)
            nc.gpsimd.iota(tile_no[:, :, :], pattern=[[1, SLOT_TILES], [0, E]], base=0, channel_multiplier=0,
                           allow_small_or_imprecise_dtypes=True).then_inc(s["const_set"], 1)
            nc.gpsimd.iota(empty[:, :, C:C + 1].bitcast(I32), pattern=[[1, SLOT_TILES]], base=2 * HALF_TOK,
                           channel_multiplier=SLOT_TILES).then_inc(s["init_z"], 1)
            pool.wait_ge(s["init_z"], 1)
            for half in range(2):
                pool.dma_start(slots[half].rearrange("(p k) c -> p (k c)", k=SLOT_TILES),
                               empty[:, :, :].rearrange("p k c -> p (k c)")).then_inc(s["init_done"], 16)
            pool.wait_ge(s["w2_copied"], E)
            for k in range(2):
                nc.gpsimd.iota(rows[k][:, :, C:C + 1].bitcast(I32), pattern=[[2 * P, TT]], base=k,
                               channel_multiplier=2).then_inc(s["init_z"], 1)
            def dispatch(half, j):
                pool.indirect_dma_start(
                    slots[half], bass.IndirectOffsetOnAxis(pos_i[:, half, j % 2, j // 2:j // 2 + 1], 0),
                    rows[j % 2][:, j // 2, :], None).then_inc(s[f"dispatched{j // (2 * NT)}"], 16)

            def scatter(half, k):
                pool.indirect_dma_start(
                    y_rows[half], bass.IndirectOffsetOnAxis(xs[:, k, C:C + 1].bitcast(I32), 0),
                    ys[:, k % NC, :], None).then_inc(ys_out[k], 16)

            def fill(u, b):
                f = (u, b)
                if u == "xn":
                    pool.wait_ge(s["xn_ready"], b + 1)
                    xv = x[:, b, :].rearrange("p (j f) -> p j f", j=NT)
                    nc.gpsimd.tensor_tensor(xv, xv, o_b_rows[:, :].unsqueeze(1).broadcast_to((P, NT, P)), ALU.add).then_inc(s["x_added"], 1)
                elif f in NORMS:
                    n = NORMS.index(f)
                    pool.wait_ge(s["norm_stats"], n + 1)
                    nc.gpsimd.tensor_scalar(rs_v[:, :], mv[:, :, 1], 1e-5, None, ALU.add).then_inc(s["norm_step"], 1)
                    pool.wait_ge(s["norm_step"], n + 1)
                    nc.gpsimd.tensor_tensor(rs_y[:, :], rs_v[:, :], minus_half[:, :], ALU.pow).then_inc(s["norm_rstd"], 1)
                elif u == "ta1":
                    pool.wait_ge(s["normed_ready"], 2 * norm_of(f) + 2)
                    t = tok[b % 3][:, :, :]
                    nc.gpsimd.tensor_tensor(t, t, normed[:, :, :], ALU.add).then_inc(s["tok_ready"], 1)
                    pool.wait_ge(s["tok_ready"], 2 * before_it(f, "ta1") + 1)
                    nc.gpsimd.tensor_tensor(t, t, b_o_rows[:, :].unsqueeze(1).broadcast_to((P, NT, C)), ALU.add).then_inc(s["tok_ready"], 1)
                elif u == "pc":
                    pool.wait_ge(s["normed_ready"], 2 * norm_of(f) + 2)
                    wait_if(pool, s[f"dispatched{b % HALF_B}"], 16 * 2 * NT * (b // HALF_B))
                    i = (b % HALF_B) * NT
                    for k in range(2):
                        nc.gpsimd.tensor_copy(rows[k][:, i:i + NT, 0:C], normed_of(f)).then_inc(s["rows_set"], 1)

            pool.wait_ge(s["bias_used"], 2)
            for f in FILLERS:
                fill(*f)
                if f == ("rf", 0):
                    pool.wait_ge(s["init_done"], 32)
                    pool.wait_ge(s["rows_set"], 2 * HALF_B)
                    pool.wait_ge(s["route_done"], 1)
                    for j in range(4):
                        dispatch(0, j)
                if f == ("ps1", 2):
                    for j in range(4, 2 * TT):
                        dispatch(0, j)
            for n in range(SLOT_TILES):
                if n == DISPATCH_FROM:
                    pool.wait_ge(s["rows_set"], 2 * B)
                    pool.wait_ge(s["route_done"], 2)
                if DISPATCH_FROM <= n < DISPATCH_FROM + TT:
                    for j in range(2):
                        dispatch(1, 2 * (n - DISPATCH_FROM) + j)
                pool.wait_ge(s["ys_ready"], n + 1)
                scatter(0, n % NB)
            carry = lambda: nc.gpsimd.tensor_tensor(spare[:, 1:2], ones[:, 0:1], ones[:, 1:2], ALU.mult).then_inc(s["pool_step"], 1)
            carry()
            with pool.Fori(TURNS, 2 * TURNS) as t:
                for k in range(NB):
                    pool.wait_ge(s["ys_ready"], t * NB + (k + 1))
                    pool.wait_ge(s["pool_step"], t * NB + (k - SLOT_TILES + 1))
                    carry()
                    scatter(1, k)

        @block.scalar
        def _(act):
            act.dma_start(router_in[:, :], a["L1_ffn_router_w"]).then_inc(s["w_in"], 16)
            for dst, w in ((Wq2, "L1_attn_W_q"), (Wk2, "L1_attn_W_k"), (Wv2, "L1_attn_W_v")):
                for k in range(2):
                    act.dma_start(dst[:, k * U:(k + 1) * U], a[w]).then_inc(s["small_in"], 16)
            for k in range(2):
                act.dma_start(Wo2[k * U:(k + 1) * U, :], a["L1_attn_W_o"]).then_inc(s["small_in"], 16)
            row = lambda v: v.rearrange("(a n) -> a n", a=1)
            for h in range(HEADS):
                act.dma_start(rows_in[0:1, 0, h * HD:(h + 1) * HD],
                              row(a["L0_conv_v_b"])[:, (h // 2) * HD:(h // 2 + 1) * HD]).then_inc(s["small_in"], 16)
            act.dma_start(rows_in[0:1, 1, :], row(a["L0_conv_o_b"])).then_inc(s["small_in"], 16)
            act.dma_start(rows_in[0:1, 2, :], row(a["L1_attn_b_o"])).then_inc(s["small_in"], 16)
            act.dma_start(w2stage[:, :, :], a["L1_ffn_w2"].rearrange("e c h -> c e h")).then_inc(s["w2stage_in"], 16)

            for w, stage, done in (("L1_ffn_w1", w1stage, "w1_in"), ("L1_ffn_w3", w3stage, "w3_in")):
                for c in range(CHUNKS):
                    n = min(HC, H - c * HC)
                    act.dma_start(stage[0:n, c, :, :], a[w][:, c * HC:c * HC + n, :].rearrange("e h c -> h e c")).then_inc(s[done], 16)
            for e in range(E):
                act.wait_ge(s["wexp_pe"], e + 1)
                act.activation(w13_T[:, e, :].rearrange("p (m h) -> p m h", m=2)[:, :, 0:H],
                               S[e % 2][:, :].rearrange("p (m h) -> p m h", m=2)[:, :, 0:H],
                               ACT.Copy).then_inc(s["wexp_copied"], 1)

            def exps(g):
                kind, b, j = phase_of(g)
                act.wait_ge(s["neg_ready"], g + 1)
                wait_if(act, s["pt_done"], g - 1)
                wait_if(act, s["post_used"], g - 3)
                if kind == "conv":
                    for h in range(HEADS):
                        ins = act.activation(probs[:, g % 2, h * KEYS:(h + 1) * KEYS],
                                             S[g % 2][:, h * KEYS:(h + 1) * KEYS], ACT.Exp,
                                             bias=negmax[:, g % 2, h:h + 1], scale=CONV_SCALE,
                                             accum_out=rowsum[:, g % 4, h:h + 1])
                else:
                    ins = act.activation(probs[:, g % 2, :], S[g % 2][:, :], ACT.Exp, bias=negmax[:, g % 2, 0:1],
                                         scale=TOK_SCALE, accum_out=rowsum[:, g % 4, 0:1])
                ins.then_inc(s["exp_done"], 1)

            def probs_copy(g):
                act.wait_ge(s["pt_done"], g + 1)
                wait_if(act, s["pv_done"], g - 1)
                act.activation(probsT[:, g % 2, CUT:HW], S[g % 2][:, CUT:HW], ACT.Copy).then_inc(s["ptB_copied"], 1)

            def out_copy(g):
                act.wait_ge(s["pv_done"], g + 1)
                wait_if(act, s["post_done"], g - 1)
                act.activation(outT[:, g % 2, :], OM[:, 0:P], ACT.Copy).then_inc(s["ot_copied"], 1)

            def step(g, slot):
                if g == 0:
                    exps(0)
                slot(0)
                if g % NT < NT - 1:
                    exps(g + 1)
                probs_copy(g)
                slot(1)
                if g >= 1:
                    out_copy(g - 1)
                slot(2)
                if g % NT == NT - 1 and g + 1 < STEPS:
                    exps(g + 1)

            def tail():
                out_copy(STEPS - 1)

            def fill(u, b):
                f = (u, b)
                if f in BANKED and u not in ("V", "o0", "o1", "g0", "g1", "rank"):
                    act.wait_ge(s["fill_done"], nth(f))
                bank = BANKS[bank_of(f)] if f in BANKED else None
                half = int(u[-1]) if u[-1] in "01" else 0
                r = slice(half * 512, (half + 1) * 512)
                copied = lambda ins: ins.then_inc(s[f"fill_copied{bank_of(f)}"], 1)
                T = TOK_SET[b] if b < B else 0
                if u == "xn":
                    act.wait_ge(s["xn_ready"], b + 1)
                    wait_if(act, s["fill_done"], banked_before(f))
                    grid = pixels[:, :].rearrange("p (oy dy ox dx) -> p dy dx oy ox", oy=16, dy=2, ox=16, dx=2)
                    for dy in range(2):
                        ins = act.activation(taps[:, 2 * dy:2 * dy + 2, :].rearrange("p x (oy ox) -> p x oy ox", oy=16),
                                             grid[:, dy], ACT.Copy)
                    ins.then_inc(s["taps_ready"], 1)
                elif u in ("kT0", "kT1", "c0", "c1", "l0", "l1", "r0", "r1"):
                    copied(act.activation(operandT[:, r], bank[:, :], ACT.Copy))
                elif u in ("qv0", "qv1"):
                    copied(act.activation(qvT[:, half, :, :].rearrange("p m c -> p (m c)"), bank[:, 0:2 * C], ACT.Copy))
                elif u in ("Q0", "Q1"):
                    act.activation(Qhi[:, r], bank[:, :], ACT.Identity, bias=q_b[:, 0:1]).then_inc(s["hi_done"], 1)
                elif u == "K":
                    for h in range(HEADS):
                        p = slice(h * HD, (h + 1) * HD)
                        ins = act.activation(Khi[p, h, :], bank[p, 0:KEYS], ACT.Identity, bias=k_b[p, 0:1])
                    ins.then_inc(s["hi_done"], 1)
                elif u in ("t0", "t1"):
                    if b >= 3:
                        act.wait_ge(s["post_used"], NT * [p[:2] for p in PHASES].index(("tok", b - 3)) + NT)
                    copied(act.activation(tok[b % 3][:, 4 * half:4 * half + 4, :].rearrange("p i c -> p (i c)"), bank[:, :], ACT.Copy))
                elif u in ("q0", "q1"):
                    act.activation(QS[T][:, r], bank[:, :], ACT.Copy).then_inc(s["hi_done"], 1)
                elif u in ("k0", "k1"):
                    act.activation(KH[T][:, r], bank[:, :], ACT.Copy).then_inc(s["hi_done"], 1)
                elif u in ("v0", "v1"):
                    copied(act.activation(Vt[:, b % 2, 4 * half:4 * half + 4, :],
                                          bank[:, :].rearrange("p (i u) -> p i u", i=4)[:, :, 0:U], ACT.Copy))
                elif u == "rb":
                    act.wait_ge(s["r_exp_in"], b + 1)
                    act.activation(r8["ex"][:, :, :], r8["ex"][:, :, :], ACT.Exp).then_inc(s["r_exp"], 1)

            act.wait_ge(s["w_in"], 16 * N_W)
            run_phases(step, fill, tail)

            def x_copy(n, q, k):
                act.wait_ge(s["xsT_pe"], n + 1)
                wait_if(act, s["h_pe"], n - (NC - 1))
                act.activation(xsT[:, k % NC, :], OM[:, 0:P], ACT.Copy).then_inc(s["xsT_act"], 1)

            def silu(n, q, k):
                act.wait_ge(s["h_pe"], n + 1)
                wait_if(act, s["hid_ready"], n - (NC - 1))
                act.activation(act_h[:, k % NC, :], S[k % 2][:, 0:H], ACT.Silu).then_inc(s["silu_done"], 1)

            def gate(n, q, k):
                act.wait_ge(s["y_pe"], n + 1)
                wait_if(act, ys_out[(k - NC) % NB], (q + (k - NC) // NB + 1) * 16)
                act.activation(ys[:, k % NC, :], PO[:, 0:P], ACT.Copy, scale=xs[:, k, C + 1:C + 2]).then_inc(s["ys_ready"], 1)

            for half in range(2):
                schedule(act, half, (("B", silu), ("T", x_copy), ("D", gate)), fill)

            for q in range(2 * TT // 4):
                act.wait_ge(s["fin_pe"], q + 1)
                if q >= 2:
                    act.wait_ge(s[f"out_done{q % 2}"], 16 * (q // 2))
                act.activation(res[:, q % 2, :], (TA if q % 2 == 0 else TB)[:, :], ACT.Copy).then_inc(s["fin_act"], 1)

        @block.vector
        def _(dve):
            class Steps:
                def __init__(self, semaphore, base):
                    self.semaphore, self.base, self.n = semaphore, base, 0

                def __call__(self, ins):
                    ins.then_inc(self.semaphore, 1)
                    self.n += 1
                    dve.wait_ge(self.semaphore, self.base + self.n)

            def rsqrt(link, y, v, n, eps):
                h, t = rs_v[:, 0:n], rs_a[:, 0:n]
                link(nc.vector.tensor_scalar(h, v, eps, None, ALU.add))
                link(nc.vector.tensor_scalar(rs_i[:, 0:n], h.bitcast(I32), 1, None, ALU.logical_shift_right))
                link(nc.vector.tensor_scalar(y.bitcast(I32), rs_i[:, 0:n], -1.0, float(MAGIC), ALU.mult, ALU.add))
                for _ in range(NEWTON):
                    link(nc.vector.tensor_tensor(t, y, y, ALU.mult))
                    link(nc.vector.scalar_tensor_tensor(out=t, in0=t, scalar=-0.5, in1=h, op0=ALU.mult, op1=ALU.mult))
                    link(nc.vector.scalar_tensor_tensor(out=y, in0=t, scalar=1.5, in1=y, op0=ALU.add, op1=ALU.mult))

            pre = Steps(s["dve_pre"], 0)
            dve.wait_ge(s["x_in"], 16 * B)
            for b in range(B):
                for i in range(2):
                    last = nc.vector.bn_stats(chan[:, b, i, :], x[:, b, i * 512:(i + 1) * 512])
            pre(last)
            for b in range(B):
                last = nc.vector.bn_aggr(chan_mv[:, b, :], chan[:, b, :, :].rearrange("p i s -> p (i s)"))
            last.then_inc(s["gn_dve"], 1)
            dve.wait_ge(s["gn_dve"], 1)
            dve.wait_ge(s["gn_pe"], 1)
            pre(nc.vector.tensor_copy(grp[:, :, :].rearrange("p b s -> p (b s)"), S[0][:, 0:2 * B]))
            pre(nc.vector.tensor_tensor(dev[:, :], chan_mv[:, :, 0], grp[:, :, 0], ALU.subtract))
            nc.vector.tensor_tensor(dev[:, :], dev[:, :], dev[:, :], ALU.mult).then_inc(s["gn_dve"], 1)
            dve.wait_ge(s["gn_pe"], 2)
            pre(nc.vector.tensor_tensor(gvar[:, 0:B], S[0][:, 0:B], grp[:, :, 1], ALU.add))
            rsqrt(pre, gvar[:, 4:4 + B], gvar[:, 0:B], B, 1e-5)
            nc.vector.memset(Khi[:, :, :].bitcast(F32), 0.0)
            nc.vector.memset(Klo[:, :, :].bitcast(F32), 0.0).then_inc(s["pad_z"], 1)
            for i, (_, dst) in enumerate(SMALL_T):
                if i % 4 == 0:
                    dve.wait_ge(s["wt_done"], i // 4 + 1)
                last = nc.vector.tensor_copy(dst, SMALL_BANK[i // 4][:, tile(i % 4)])
                if i % 4 == 3 or i == len(SMALL_T) - 1:
                    if i == len(SMALL_T) - 1:
                        dve.wait_ge(s["const_z"], 7)
                        last = nc.vector.tensor_copy(router_T[:, 0:E], TB[:, P:P + E])
                    last.then_inc(s["wt_used"], 1)
            dve.wait_ge(s["wt_used"], 4)
            nc.vector.tensor_scalar(o_wTg[:, :], o_wT[:, :], ln_g[:, 0:1], None, ALU.mult)
            dve.wait_ge(s["const_z"], 7)
            nc.vector.tensor_scalar(lnb_rep[:, :], ones[:, :], ln_b[:, 0:1], None, ALU.mult).then_inc(s["bias_used"], 1)
            dve.wait_ge(s["bias_done"], 1)
            nc.vector.tensor_copy(v_b_rows[:, :], OM[:, tile(0)])
            nc.vector.tensor_copy(o_b_rows[:, :], OM[:, tile(1)])
            nc.vector.tensor_copy(b_o_rows[:, :], OM[:, tile(2)]).then_inc(s["bias_used"], 1)
            dve.wait_ge(s["bias_used"], 2)
            for e in range(E):
                dve.wait_ge(s["w2_pe"], e + 1)
                T = TA if e % 2 == 0 else TB
                nc.vector.tensor_copy(w2_T[0:HC, e, 0:2 * C], T[0:HC, 0:2 * C])
                nc.vector.tensor_copy(w2_T[0:HC - 1, e, 2 * C:3 * C], T[0:HC - 1, 2 * C:3 * C]).then_inc(s["w2_copied"], 1)

            link = Steps(s["dve_step"], 0)

            def row_max(g):
                kind, b, j = phase_of(g)
                dve.wait_ge(s["scores_done"], g + 1)
                wait_if(dve, s["exp_done"], g - 1)
                n = HEADS if kind == "conv" else 1
                link(nc.vector.tensor_reduce(rowmax[:, g % 2, 0:n], S[g % 2][:, :].rearrange("p (h k) -> p h k", h=n),
                                             AX.X, ALU.max))
                nc.vector.tensor_scalar(negmax[:, g % 2, 0:n], rowmax[:, g % 2, 0:n],
                                        -(CONV_SCALE if kind == "conv" else TOK_SCALE), None, ALU.mult).then_inc(s["neg_ready"], 1)

            def probs_copy(g):
                dve.wait_ge(s["pt_done"], g + 1)
                wait_if(dve, s["pv_done"], g - 1)
                nc.vector.tensor_copy(probsT[:, g % 2, 0:CUT], S[g % 2][:, 0:CUT]).then_inc(s["ptA_copied"], 1)

            def normalise(g):
                kind, b, j = phase_of(g)
                n = HEADS if kind == "conv" else 1
                link(nc.vector.reciprocal(rowinv[:, g % 4, 0:n], rowsum[:, g % 4, 0:n]))
                dve.wait_ge(s["post_done"], g + 1)
                post = PO[:, 0:P]
                if kind == "conv":
                    nc.vector.tensor_tensor(conv_out[b % 2][:, j, :].rearrange("p (h d) -> p h d", h=HEADS),
                                            post.rearrange("p (h d) -> p h d", h=HEADS),
                                            rowinv[:, g % 4, :].unsqueeze(2).broadcast_to((P, HEADS, HD)),
                                            ALU.mult).then_inc(s["post_used"], 1)
                else:
                    dve.wait_ge(s["tok_ready"], 2 * b + 2)
                    nc.vector.scalar_tensor_tensor(out=t1[:, b * NT + j, :], in0=post, scalar=rowinv[:, g % 4, 0:1],
                                                   in1=tok[b % 3][:, j, :], op0=ALU.mult, op1=ALU.add).then_inc(s["post_used"], 1)

            def step(g, slot):
                if g == 0:
                    row_max(0)
                if g % NT < NT - 1:
                    row_max(g + 1)
                if g >= 2:
                    normalise(g - 2)
                slot(0)
                probs_copy(g)
                slot(1)
                slot(2)
                if g % NT == NT - 1 and g + 1 < STEPS:
                    row_max(g + 1)

            def tail():
                normalise(STEPS - 2)
                normalise(STEPS - 1)

            def statistics(f, src, half):
                tiles = range(4 * half, 4 * half + 4)
                for i in tiles:
                    last = nc.vector.bn_stats(stats[:, i, :], src[:, i, :])
                link(last)
                for i in tiles:
                    last = nc.vector.bn_aggr(mv[:, i, :], stats[:, i, :])
                if half == 1:
                    last.then_inc(s["norm_stats"], 1)

            def apply_norm(f, src, half):
                n = norm_of(f)
                dve.wait_ge(s["norm_rstd"], n + 1)
                wait_if(dve, s["fill_done"], banked_before(f))
                wait_if(dve, s["tok_ready"], 2 * before_it(f, "ta1"))
                wait_if(dve, s["rows_set"], 2 * before_it(f, "pc") - (2 if f in LAST_UNITS else 0))
                for i in range(4 * half, 4 * half + 4):
                    last = nc.vector.tensor_scalar(normed_of(f)[:, i, :], src[:, i, :], mv[:, i, 0:1], rs_y[:, i:i + 1],
                                                   ALU.subtract, ALU.mult)
                last.then_inc(s["normed_ready"], 1)

            def fill(u, b):
                f = (u, b)
                V = nc.vector
                if u in ("Q0", "Q1", "K", "q0", "q1", "k0", "k1"):
                    dve.wait_ge(s["hi_done"], sum(g[0] in ("Q0", "Q1", "K", "q0", "q1", "k0", "k1") for g in FILLERS[:FILLERS.index(f) + 1]))
                elif u in ("V", "o0", "o1", "g0", "g1", "re"):
                    dve.wait_ge(s["fill_done"], nth(f if u != "re" else ("rank", b)))
                bank = BANKS[bank_of(f)] if f in BANKED else None
                half = int(u[-1]) if u[-1] in "01" else 0
                r = slice(half * 512, (half + 1) * 512)
                copied = lambda ins: ins.then_inc(s[f"fill_copied{bank_of(f)}"], 1)
                T = TOK_SET[b] if b < B else 0
                V = nc.vector
                if u == "xn":
                    wait_if(dve, s["fill_done"], banked_before(f))
                    V.tensor_scalar(pixels[:, :], x[:, b, :], grp[:, b, 0:1], gvar[:, b + 4:b + 5],
                                    ALU.subtract, ALU.mult).then_inc(s["xn_ready"], 1)
                elif u in ("Q0", "Q1"):
                    copied(V.scalar_tensor_tensor(out=Qlo[:, r], in0=bank[:, :], scalar=q_b[:, 0:1], in1=Qhi[:, r].bitcast(F32),
                                                  op0=ALU.add, op1=ALU.subtract))
                elif u == "K":
                    for h in range(HEADS):
                        p = slice(h * HD, (h + 1) * HD)
                        last = V.scalar_tensor_tensor(out=Klo[p, h, :], in0=bank[p, 0:KEYS], scalar=k_b[p, 0:1],
                                                      in1=Khi[p, h, :].bitcast(F32), op0=ALU.add, op1=ALU.subtract)
                    copied(last)
                elif u == "V":
                    copied(V.tensor_tensor(V4[:, b % 2, :, :], bank[:, 0:2 * P].rearrange("p (j v) -> p j v", j=2),
                                           v_b_rows[:, :].unsqueeze(1).broadcast_to((P, 2, P)), ALU.add))
                elif u in ("cs0", "cs1"):
                    g = NT * [p[:2] for p in PHASES].index(("conv", b)) + 4 * half + 4
                    dve.wait_ge(s["post_used"], g)
                    statistics(f, conv_out[b % 2], half)
                elif u in ("ca0", "ca1"):
                    apply_norm(f, conv_out[b % 2], half)
                elif u in ("o0", "o1"):
                    dve.wait_ge(s["x_added"], b + 1)
                    dve.wait_ge(s["taps_ready"], before_it(f, "xn"))
                    copied(V.tensor_tensor(pixels[:, r], bank[:, :], x[:, b, r], ALU.add))
                elif u in ("ts0", "ts1"):
                    wait_copied(dve, (f"t{half}", b))
                    statistics(f, tok[b % 3], half)
                elif u in ("ta0", "ta1"):
                    apply_norm(f, tok[b % 3], half)
                elif u in ("q0", "q1"):
                    copied(V.tensor_tensor(QS[T][U:P, r], bank[U:P, :], QS[T][U:P, r].bitcast(F32), ALU.subtract))
                elif u in ("k0", "k1"):
                    copied(V.tensor_tensor(KL[T][:, r], bank[:, :], KH[T][:, r].bitcast(F32), ALU.subtract))
                elif u in ("ps0", "ps1"):
                    g = NT * [p[:2] for p in PHASES].index(("tok", b)) + 4 * half + 4
                    dve.wait_ge(s["post_used"], g)
                    statistics(f, t1[:, b * NT:(b + 1) * NT, :], half)
                elif u in ("pa0", "pa1"):
                    apply_norm(f, t1[:, b * NT:(b + 1) * NT, :], half)
                elif u in ("g0", "g1"):
                    i = b * NT + 4 * half
                    copied(V.tensor_copy(logits[:, i:i + 4, :], bank[:, :].rearrange("p (i e) -> p i e", i=4)[:, :, 0:E]))
                elif u in ("ra", "rb", "rc", "rd", "re", "rf"):
                    route(u, b)

            def route(part, half):
                step = link
                V = nc.vector
                f = ("rank", half)
                bank = BANKS[bank_of(f)]
                copied = lambda ins: ins.then_inc(s[f"fill_copied{bank_of(f)}"], 1)
                L = logits[:, half * TT:(half + 1) * TT, :]
                wide = lambda t: t[:, :].unsqueeze(2).broadcast_to((P, TT, E))
                R, r = r8, r1

                def first_of(values, m, onehot):
                    step(V.tensor_reduce(r[m][:, :], values, AX.X, ALU.max))
                    step(V.tensor_tensor(R["eq"][:, :, :], values, wide(r[m]), ALU.is_equal))
                    step(V.tensor_tensor(R["w"][:, :, :], R["eq"][:, :, :], rev[:, :, :], ALU.mult))
                    step(V.tensor_reduce(r["mw"][:, :], R["w"][:, :, :], AX.X, ALU.max))
                    step(V.tensor_tensor(R[onehot][:, :, :], R["w"][:, :, :], wide(r["mw"]), ALU.is_equal))

                if part == "ra":
                    wait_copied(dve, *((g, HALF_B * half + k) for g in ("g0", "g1") for k in range(HALF_B)))
                    first_of(L, "m1", "oh1")
                    V.tensor_tensor(R["ex"][:, :, :], L, wide(r["m1"]), ALU.subtract).then_inc(s["r_exp_in"], 1)
                    step(V.scalar_tensor_tensor(out=R["l2"][:, :, :], in0=R["oh1"][:, :, :], scalar=BIG, in1=L,
                                                op0=ALU.mult, op1=ALU.add))
                if part == "rb":
                    first_of(R["l2"][:, :, :], "m2", "oh2")
                    step(V.tensor_tensor(R["a"][:, :, :], R["oh1"][:, :, :], R["oh2"][:, :, :], ALU.add))
                if part == "rc":
                    src = "a"
                    for n, d in enumerate((1, 2, 4, 8)):
                        dst = ("c0", "c1")[n % 2]
                        V.tensor_copy(R[dst][:, 0:d, :], R[src][:, 0:d, :])
                        step(V.tensor_tensor(R[dst][:, d:TT, :], R[src][:, d:TT, :], R[src][:, 0:TT - d, :], ALU.add))
                        src = dst
                    V.tensor_tensor(R["c0"][:, :, :], R["c1"][:, :, :], R["a"][:, :, :], ALU.subtract).then_inc(s["r_cnt_in"], 1)
                if part == "rd":
                    dve.wait_ge(s["r_exp"], half + 1)
                    step(V.tensor_reduce(r["z"][:, :], R["ex"][:, :, :], AX.X, ALU.add))
                    step(V.tensor_tensor(R["tmp"][:, :, :], R["ex"][:, :, :], R["oh2"][:, :, :], ALU.mult))
                    step(V.tensor_reduce(r["e2"][:, :], R["tmp"][:, :, :], AX.X, ALU.add))
                    step(V.reciprocal(r["p1"][:, :], r["z"][:, :]))
                    step(V.tensor_tensor(r["p2"][:, :], r["e2"][:, :], r["p1"][:, :], ALU.mult))
                    step(V.scalar_tensor_tensor(out=r["s"][:, :], in0=r["p1"][:, :], scalar=1e-9, in1=r["p2"][:, :],
                                                op0=ALU.add, op1=ALU.add))
                    step(V.reciprocal(r["z"][:, :], r["s"][:, :]))
                    dve.wait_ge(s["init_z"], 3)
                    if half == 1:
                        for b in range(HALF_B):
                            dve.wait_ge(s[f"dispatched{b}"], 16 * 2 * NT)
                    for k, p in enumerate(("p1", "p2")):
                        step(V.tensor_tensor(rows[k][:, :, C + 1], r[p][:, :], r["z"][:, :], ALU.mult))
                if part == "re":
                    step(V.tensor_scalar(cnt_i[:, :], bank[:, 128:128 + E], float(P - 1), None, ALU.add))
                    step(V.tensor_scalar(cnt_i[:, :], cnt_i[:, :], 7, None, ALU.logical_shift_right))
                    step(V.tensor_copy(cnt[:, :], cnt_i[:, :]))
                    src = cnt
                    for n, d in enumerate((1, 2, 4)):
                        V.tensor_copy(cum[n % 2][:, 0:d], src[:, 0:d])
                        step(V.tensor_tensor(cum[n % 2][:, d:E], src[:, d:E], src[:, 0:E - d], ALU.add))
                        src = cum[n % 2]
                    step(V.tensor_tensor(tile_cmp[:, :, :], tile_no[:, :, :],
                                         cum[0][:, :].unsqueeze(1).broadcast_to((P, SLOT_TILES, E)), ALU.is_ge))
                    step(V.tensor_reduce(tile_sum[:, :], tile_cmp[:, :, :], AX.X, ALU.add))
                    step(V.tensor_scalar(tile_expert[:, half, :], tile_sum[:, :], float(E - 1), None, ALU.min))
                    step(V.tensor_tensor(cum[1][:, :], cum[0][:, :], cnt[:, :], ALU.subtract))
                    step(V.tensor_scalar(cum[1][:, :], cum[1][:, :], float(P), None, ALU.mult))
                    copied(V.tensor_tensor(R["rank"][:, :, :], bank[:, 0:TT * E].rearrange("p (i e) -> p i e", e=E),
                                           cum[1][:, :].unsqueeze(1).broadcast_to((P, TT, E)), ALU.add))
                    wait_copied(dve, f)
                if part == "rf":
                    for k, oh in enumerate(("oh1", "oh2")):
                        step(V.tensor_tensor(R["tmp"][:, :, :], R["rank"][:, :, :], R[oh][:, :, :], ALU.mult))
                        step(V.tensor_reduce(r["pos"][:, :], R["tmp"][:, :, :], AX.X, ALU.add))
                        last = V.tensor_copy(pos_i[:, half, k, :], r["pos"][:, :])
                        if k == 0:
                            step(last)
                    last.then_inc(s["route_done"], 1)

            dve.wait_ge(s["w_in"], 16 * N_W)
            dve.wait_ge(s["init_done"], 32)
            run_phases(step, fill, tail)

            def hidden(n, q, k):
                dve.wait_ge(s["silu_done"], n + 1)
                wait_if(dve, s["hT_pe"], n - (NC - 1))
                nc.vector.tensor_tensor(hid[:, k % NC, 0:H], S[k % 2][:, 512:512 + H], act_h[:, k % NC, :], ALU.mult).then_inc(s["hid_ready"], 1)

            def hidden_copy(n, q, k):
                dve.wait_ge(s["hT_pe"], n + 1)
                wait_if(dve, s["y_pe"], n - (NC - 1))
                nc.vector.tensor_copy(hidT[0:HC, k % NC, :], TA[0:HC, 0:CHUNKS * P]).then_inc(s["hT_dve"], 1)

            nc.vector.memset(hid[:, :, :], 0.0).then_inc(s["pad_z"], 1)
            dve.wait_ge(s["pad_z"], 2)
            for half in range(2):
                schedule(dve, half, (("B", hidden), ("C", hidden_copy)), fill)
            for q in range(2 * TT // 4):
                dve.wait_ge(y12_in[q % 2], 16 * (q // 2 + 1))
                t = t1[:, 4 * q:4 * q + 4, :]
                nc.vector.tensor_tensor(t, t, y12[:, q % 2, :, 0:C], ALU.add).then_inc(s["sum_step"], 1)
                dve.wait_ge(s["sum_step"], q + 1)
                nc.vector.tensor_tensor(t, t, y12[:, q % 2, :, C:2 * C], ALU.add).then_inc(s["sum_ready"], 1)

        @block.tensor
        def _(pe):
            mm, tr = nc.tensor.matmul, nc.tensor.transpose

            pe.wait_ge(s["const_set"], 5)
            pe.wait_ge(s["gn_dve"], 1)
            mm(S[0][:, 0:2 * B], groups[:, :], chan_mv[:, :, :].rearrange("p b s -> p (b s)"), start=True, stop=True).then_inc(s["gn_pe"], 1)
            pe.wait_ge(s["gn_dve"], 2)
            mm(S[0][:, 0:B], groups[:, :], dev[:, :], start=True, stop=True).then_inc(s["gn_pe"], 1)
            pe.wait_ge(s["w_in"], 16 * N_W)
            for i, (src, _) in enumerate(SMALL_T):
                last = tr(SMALL_BANK[i // 4][:, tile(i % 4)], src, ident[:, :])
                if i == len(SMALL_T) - 1:
                    last = tr(TB[:, P:P + E], router_in[:, :], ident[0:E, 0:E])
                if i % 4 == 3 or i == len(SMALL_T) - 1:
                    last.then_inc(s["wt_done"], 1)
            pe.wait_ge(s["small_in"], 16 * 14)
            pe.wait_ge(s["bias_used"], 1)
            mm(OM[:, tile(0)], ones[0:1, :], rows_in[0:1, 0, :], start=True, stop=True)
            mm(OM[:, tile(1)], lnb_rep[:, :], o_wT[:, :], start=True, stop=False)
            mm(OM[:, tile(1)], ones[0:1, :], rows_in[0:1, 1, :], start=False, stop=True)
            mm(OM[:, tile(2)], ones[0:1, :], rows_in[0:1, 2, :], start=True, stop=True).then_inc(s["bias_done"], 1)
            pe.wait_ge(s["w2stage_in"], 16)
            pe.wait_ge(s["w1_in"], 16 * CHUNKS)
            pe.wait_ge(s["w3_in"], 16 * CHUNKS)
            for e in range(E):
                if e >= 2:
                    pe.wait_ge(s["wexp_copied"], e - 1)
                for m, stage in enumerate((w1stage, w3stage)):
                    for c in range(CHUNKS):
                        n = min(HC, H - c * HC)
                        last = tr(S[e % 2][:, m * 512 + c * HC:m * 512 + c * HC + n], stage[0:n, c, e, :], ident[0:n, 0:n])
                last.then_inc(s["wexp_pe"], 1)
                T = TA if e % 2 == 0 else TB
                if e >= 2:
                    pe.wait_ge(s["w2_copied"], e - 1)
                else:
                    pe.wait_ge(s["wt_used"], 4)
                for c in range(CHUNKS):
                    n = min(HC, H - c * HC)
                    last = tr(T[0:n, tile(c)], w2stage[:, e, c * HC:c * HC + n], ident[:, :])
                last.then_inc(s["w2_pe"], 1)
            pe.wait_ge(s["wexp_copied"], E)
            pe.wait_ge(s["w2_copied"], E)
            pe.wait_ge(s["pad_z"], 1)
            pe.wait_ge(s["bias_used"], 2)

            def scores(g):
                kind, b, j = phase_of(g)
                wait_if(pe, s["ptA_copied"], g - 1)
                wait_if(pe, s["ptB_copied"], g - 1)
                if j == 0:
                    wait_copied(pe, *((u, b) for u in (("Q0", "Q1", "K", "V") if kind == "conv" else ("q0", "q1", "k0", "k1", "v0", "v1"))))
                for half in range(2):
                    r = slice(half * 512, (half + 1) * 512)
                    dst = S[g % 2][:, r]
                    if kind == "conv":
                        kh = Khi[:, 2 * half:2 * half + 2, :].rearrange("p h k -> p (h k)")
                        kl = Klo[:, 2 * half:2 * half + 2, :].rearrange("p h k -> p (h k)")
                        mm(dst, Qhi[:, tile(j)], kh, start=True, stop=False)
                        mm(dst, Qhi[:, tile(j)], kl, start=False, stop=False)
                        last = mm(dst, Qlo[:, tile(j)], kh, start=False, stop=True)
                    else:
                        T = TOK_SET[b]
                        mm(dst, QS[T][:, tile(j)], KH[T][:, r], start=True, stop=False)
                        last = mm(dst, QS[T][:, tile(j)], KL[T][:, r], start=False, stop=True)
                last.then_inc(s["scores_done"], 1)

            def probs_T(g):
                pe.wait_ge(s["exp_done"], g + 1)
                for k in range(8):
                    last = tr(S[g % 2][:, tile(k)], probs[:, g % 2, tile(k)], ident[:, :])
                last.then_inc(s["pt_done"], 1)

            def values(g):
                kind, b, j = phase_of(g)
                pe.wait_ge(s["ptA_copied"], g + 1)
                pe.wait_ge(s["ptB_copied"], g + 1)
                wait_if(pe, s["ot_copied"], g)
                out_ = OM[:, 0:P]
                pT = probsT[:, g % 2, :]
                if kind == "conv":
                    for st in range(2):
                        for h in range(HEADS):
                            last = mm(out_[h * HD:(h + 1) * HD, :], V4[:, b % 2, st, h * HD:(h + 1) * HD],
                                      pT[:, tile(2 * h + st)], start=(st == 0), stop=(st == 1))
                else:
                    for kt in range(NT):
                        r = slice((kt % 2) * U, (kt % 2 + 1) * U)
                        last = mm(out_[r, :], Vt[:, b % 2, kt, :], pT[:, tile(kt)], start=(kt < 2), stop=(kt >= NT - 2))
                last.then_inc(s["pv_done"], 1)

            def post_of(g):
                kind, b, j = phase_of(g)
                pe.wait_ge(s["ot_copied"], g + 1)
                wait_if(pe, s["post_used"], g)
                out_ = PO[:, 0:P]
                if kind == "conv":
                    last = tr(out_, outT[:, g % 2, :], ident[:, :])
                else:
                    last = mm(out_, outT[:, g % 2, :], Wo2[:, :], start=True, stop=True)
                last.then_inc(s["post_done"], 1)

            def step(g, slot):
                if g == 0:
                    scores(0)
                if g % NT < NT - 1:
                    scores(g + 1)
                if g >= 2:
                    post_of(g - 2)
                slot(0)
                probs_T(g)
                slot(1)
                if g >= 1:
                    values(g - 1)
                slot(2)
                if g % NT == NT - 1 and g + 1 < STEPS:
                    scores(g + 1)

            def tail():
                post_of(STEPS - 2)
                values(STEPS - 1)
                post_of(STEPS - 1)

            def fill(u, b):
                f = (u, b)
                if f not in BANKED:
                    return
                n = nth(f)
                half = int(u[-1]) if u[-1] in "01" else 0
                r = slice(half * 512, (half + 1) * 512)
                if u in ("kT0", "kT1"):
                    pe.wait_ge(s["xn_ready"], b + 1)
                elif u in ("qv0", "qv1"):
                    pe.wait_ge(s["taps_ready"], b + 1)
                elif u in ("c0", "l0", "r0", "c1", "l1", "r1"):
                    pe.wait_ge(s["normed_ready"], 2 * norm_of(f) + 1 + half)
                elif u == "rank":
                    pe.wait_ge(s["r_cnt_in"], b + 1)
                for k, sources in {"Q": ("kT",), "K": ("qv0", "qv1"), "V": ("qv0", "qv1"), "o": ("c",), "t": ("o",),
                                   "v": ("l",), "q": ("l",) if u[:2] != "qv" else (), "k": ("l",) if u[:2] != "kT" else (),
                                   "g": ("r",)}.items():
                    if u[0] == k:
                        wait_copied(pe, *((src if src[-1] in "01" else f"{src}{half}", b) for src in sources))
                wait_if(pe, s[f"fill_copied{bank_of(f)}"], turn_of(f) - 1)
                bank = BANKS[bank_of(f)]
                if u in ("kT0", "kT1"):
                    for j in range(4):
                        last = mm(bank[:, tile(j)], pixels[:, tile(4 * half + j)], wK_T[:, :], start=True, stop=True)
                elif u in ("qv0", "qv1"):
                    for tap in range(4):
                        last = mm(bank[:, 0:2 * C], taps[:, tap, tile(half)], wQV_T[:, tap, :, :].rearrange("p m c -> p (m c)"),
                                  start=(tap == 0), stop=(tap == 3))
                elif u in ("Q0", "Q1"):
                    last = mm(bank[:, :], q_wT[:, :], operandT[:, r], start=True, stop=True)
                elif u == "K":
                    last = mm(bank[:, 0:KEYS], k_wT[:, :], qvT[:, :, 0, :], start=True, stop=True)
                elif u == "V":
                    for j in range(2):
                        last = mm(bank[:, tile(j)], qvT[:, j, 1, :], v_wT[:, :], start=True, stop=True)
                elif u in ("c0", "c1", "l0", "l1", "r0", "r1"):
                    for i in range(4):
                        last = tr(bank[:, tile(i)], normed_of(f)[:, 4 * half + i, :], ident[:, :])
                elif u in ("o0", "o1"):
                    for j in range(4):
                        last = mm(bank[:, tile(j)], operandT[:, tile(4 * half + j)], o_wTg[:, :], start=True, stop=True)
                elif u in ("t0", "t1"):
                    for i in range(4):
                        last = tr(bank[:, tile(i)], pixels[:, tile(4 * half + i)], ident[:, :])
                elif u in ("q0", "q1"):
                    last = mm(bank[:, :], Wq2[:, :], operandT[:, r], start=True, stop=True)
                elif u in ("k0", "k1"):
                    last = mm(bank[:, :], Wk2[:, :], operandT[:, r], start=True, stop=True)
                elif u in ("v0", "v1"):
                    for i in range(4):
                        last = mm(bank[:, tile(i)], operandT[:, tile(4 * half + i)], Wv2[:, :], start=True, stop=True)
                elif u in ("g0", "g1"):
                    for i in range(4):
                        last = mm(bank[:, tile(i)], operandT[:, tile(4 * half + i)], router_T[:, :], start=True, stop=True)
                elif u == "rank":
                    mm(bank[:, 0:TT * E], before[:, :], r8["a"][:, :, :].rearrange("p i e -> p (i e)"), start=True, stop=False)
                    mm(bank[:, 0:TT * E], ones[:, :], r8["c0"][:, :, :].rearrange("p i e -> p (i e)"), start=False, stop=True)
                    last = mm(bank[:, P:P + E], ones[:, :], r8["c1"][:, TT - 1, :], start=True, stop=True)
                last.then_inc(s["fill_done"], 1)

            run_phases(step, fill, tail)

            def token_T(n, q, k):
                pe.wait_ge(xs_in[k], q * 16 + 16)
                wait_if(pe, s["xsT_act"], n)
                tr(OM[:, 0:P], xs[:, k, 0:C], ident[:, :]).then_inc(s["xsT_pe"], 1)

            def hidden(n, q, k):
                e = expert_of(n)
                pe.wait_ge(s["xsT_act"], n + 1)
                wait_if(pe, s["hid_ready"], n - 1)
                for m in range(2):
                    last = mm(S[k % 2][:, m * 512:m * 512 + H], xsT[:, k % NC, :],
                              w13_T[:, bass.ds(e, 1), m * H:(m + 1) * H].rearrange("p a h -> p (a h)"), start=True, stop=True)
                last.then_inc(s["h_pe"], 1)

            def hidden_T(n, q, k):
                pe.wait_ge(s["hid_ready"], n + 1)
                wait_if(pe, s["hT_dve"], n)
                for c in range(CHUNKS):
                    last = tr(TA[0:HC, tile(c)], hid[:, k % NC, c * HC:(c + 1) * HC], ident[:, :])
                last.then_inc(s["hT_pe"], 1)

            def output(n, q, k):
                e = expert_of(n)
                pe.wait_ge(s["hT_dve"], n + 1)
                wait_if(pe, s["ys_ready"], n)
                for c in range(CHUNKS):
                    last = mm(PO[:, 0:P], hidT[0:HC, k % NC, tile(c)],
                              w2_T[0:HC, bass.ds(e, 1), tile(c)].rearrange("p a c -> p (a c)"), start=(c == 0), stop=(c == CHUNKS - 1))
                last.then_inc(s["y_pe"], 1)

            def expert_of(n):
                te = tile_expert[0:1, :, :].rearrange("p h i -> p (h i)")
                i = bass.ds(n, 1) if not isinstance(n, int) else slice(n, n + 1)
                return pe.value_load(te[:, i], min_val=0, max_val=E - 1)

            wait_copied(pe, [f for f in BANKED if bank_of(f) == 0][-1])
            for half in range(2):
                pe.wait_ge(s["route_done"], half + 1)
                schedule(pe, half, (("B", hidden), ("T", token_T), ("D", output), ("C", hidden_T)), fill)
            for q in range(2 * TT // 4):
                pe.wait_ge(s["sum_ready"], q + 1)
                if q >= 2:
                    pe.wait_ge(s["fin_act"], q - 1)
                T = TA if q % 2 == 0 else TB
                for i in range(4):
                    last = tr(T[:, tile(i)], t1[:, 4 * q + i, :], ident[:, :])
                last.then_inc(s["fin_pe"], 1)


INPUTS = ["x"] + ["L0_conv_" + n for n in "wK wQ wV q_w q_b k_w k_b v_w v_b ln_g ln_b o_w o_b".split()] + \
    ["L1_attn_" + n for n in "W_q W_k W_v W_o b_o".split()] + ["L1_ffn_" + n for n in "router_w w1 w2 w3".split()]


def kernel(**inputs):
    import numpy as np
    from concourse import bacc
    from concourse.bass_utils import run_bass_kernel_spmd

    nc = bacc.Bacc("TRN2", target_bir_lowering=False, num_devices=1)
    arrays, aps = {}, {}
    for name in INPUTS:
        v = np.ascontiguousarray(inputs[name])
        arrays["in_" + name] = v
        aps[name] = nc.dram_tensor("in_" + name, v.shape, mybir.dt.from_np(v.dtype), kind="ExternalInput").ap()
    out = nc.dram_tensor("out", (B, C, 32, 32), F32, kind="ExternalOutput").ap()
    build(nc, aps, out)
    r = run_bass_kernel_spmd(nc, [arrays], core_ids=[0])
    return r.results[0]["out"]
```

```python
from contextlib import ExitStack

import concourse.bass as bass
from concourse import mybir

F32 = mybir.dt.float32
F32R = mybir.dt.float32r
I32 = mybir.dt.int32
ALU = mybir.AluOpType
ACT = mybir.ActivationFunctionType
AX = mybir.AxisListType

P = 128
B, C, HW = 4, 128, 1024
NT = HW // P
HEADS, HD, KEYS = 4, 32, 256
U = 64
E, H = 8, 341
HC = 114
CHUNKS = 3
HALF_B = 2
TT = HALF_B * NT
HALF_TOK = TT * P
NB = 8
NC = 4
NS = 4
SLOT_TILES = -(-(2 * HALF_TOK // P + E - 1) // NB) * NB
TURNS = SLOT_TILES // NB
SLOTS = SLOT_TILES * P
ROW = C + 2
Y_ROWS = 2 * HALF_TOK + SLOTS
CONV_SCALE = float(HD) ** -0.5
TOK_SCALE = float(U) ** -0.5
GROUP = 4
DISPATCH_FROM = 8
MAGIC = 0x5F3759DF
BIG = -3.0e38
CUT = 512
NEWTON = 3

SLOTS_OF_STEP = 3
PRE = "xn - kT0 kT1 qv0 qv1 Q0 Q1 V K"
EARLY = "cs0 - - cs1 - ca0 - ca1 c0 c1 o0 o1 t0 t1 - ts0 - ts1 - ta0 - ta1"
MID = "l0 l1 v0 v1 q0 k0 k1 q1"
POST = "ps0 - - ps1 - pa0 - pa1+pc r0 r1 g0 g1"
ROUTE = "ra rb rc rd rank - re rf"


def units(text, b):
    return [[(u, b) for u in slot.split("+") if u != "-"] for slot in text.split()]


def overlay(base, *others):
    slots = base + [[] for _ in range(max(at + len(more) for at, more in others) - len(base))]
    for at, more in others:
        for i, slot in enumerate(more):
            slots[at + i] = slots[at + i] + slot
    return slots


AT = 1
WEIGHTS = [[(u, e)] for u in ("wa", "wb", "wc") for e in range(E)]
PHASES = [
    ("conv", 0, overlay(WEIGHTS, (3, units(PRE, 1))), []),
    ("conv", 1, overlay(units(PRE, 2), (AT, units(EARLY, 0))), []),
    ("conv", 2, overlay(units(MID, 0), (AT, units(EARLY, 1))), []),
    ("tok", 0, overlay(units(PRE, 3), (AT, units(EARLY, 2))), []),
    ("conv", 3, overlay(units(MID, 1), (AT, units(POST, 0))), []),
    ("tok", 1, overlay(units(MID, 2), (AT, units(EARLY, 3))), []),
    ("tok", 2, overlay(units(MID, 3), (AT, units(POST, 1)), (14, units(ROUTE, 0))), []),
    ("tok", 3, overlay([], (AT, units(POST.replace("+pc", ""), 2))), []),
]
FIRST = units(PRE, 0)
BEHIND = overlay(units(POST, 3), (1, units("pc", 2)))
LAST = units("- " + ROUTE.replace(" -", ""), 1)
STEPS = NT * len(PHASES)


def flat(slots):
    return [f for slot in slots for f in slot]


LAST_UNITS = flat(LAST)
FILLERS = flat(FIRST) + [f for _, _, inner, behind in PHASES for f in flat(inner + behind)] + \
    flat(BEHIND) + LAST_UNITS
BANKED = [f for f in FILLERS if f[0] in "kT0 kT1 qv0 qv1 Q0 Q1 K V c0 c1 o0 o1 t0 t1 l0 l1 q0 q1 k0 k1 v0 v1 r0 r1 g0 g1 wa wb wc rank".split()]
NORMS = [f for f in FILLERS if f[0] in ("cs1", "ts1", "ps1")]
CONV_SET = [0, 1, 0, 0]
TOK_SET = [0, 0, 1, 0]


def build(nc, a, out):
    ctx = ExitStack()
    with ctx:
        def sb(name, shape, dt=F32):
            return ctx.enter_context(nc.sbuf_tensor(name, shape, dt))

        def ps(name, shape, dt=F32):
            return ctx.enter_context(nc.psum_tensor(name, shape, dt))

        def sem(name):
            return ctx.enter_context(nc.semaphore(name))

        ident = sb("ident", [P, P])
        ones = sb("ones", [P, P])
        spare = sb("spare", [P, 2])
        before = sb("before", [P, P])
        groups = sb("groups", [P, P])
        rev = sb("rev", [P, TT, E])
        tile_no = sb("tile_no", [P, SLOT_TILES, E])
        router_in = sb("router_in", [E, C])
        rows_in = sb("rows_in", [1, 3, P])
        q_b = sb("q_b", [P, 1])
        k_b = sb("k_b", [P, 1])
        ln_g = sb("ln_g", [P, 1])
        ln_b = sb("ln_b", [P, 1])
        wK_T = sb("wK_T", [P, C])
        wQV_T = sb("wQV_T", [P, 4, 2, C])
        q_wT = sb("q_wT", [P, P])
        k_wT = sb("k_wT", [P, P])
        v_wT = sb("v_wT", [P, P])
        o_wT = sb("o_wT", [P, P])
        o_wTg = sb("o_wTg", [P, P])
        Wq2 = sb("Wq2", [P, P])
        Wk2 = sb("Wk2", [P, P])
        Wv2 = sb("Wv2", [P, P])
        Wo2 = sb("Wo2", [P, C])
        router_T = sb("router_T", [P, P])
        v_b_rows = sb("v_b_rows", [P, P])
        o_b_rows = sb("o_b_rows", [P, P])
        b_o_rows = sb("b_o_rows", [P, P])
        w13_T = sb("w13_T", [P, E, 2 * H])
        w2_T = sb("w2_T", [P, E, CHUNKS * C])
        x = sb("x", [P, B, HW])
        chan = sb("chan", [P, B, 2, 6])
        chan_mv = sb("chan_mv", [P, B, 2])
        grp = sb("grp", [P, B, 2])
        dev = sb("dev", [P, B])
        gvar = sb("gvar", [P, 8])
        operandT = sb("operandT", [P, HW])
        wK_in, qw_in, kw_in, vw_in, ow_in = (operandT[:, k * P:(k + 1) * P] for k in range(5))
        qvT = sb("qvT", [P, 2, 2, C])
        Qhi = sb("Qhi", [P, HW], F32R)
        Qlo = sb("Qlo", [P, HW], F32R)
        Khi = sb("Khi", [P, HEADS, KEYS], F32R)
        Klo = sb("Klo", [P, HEADS, KEYS], F32R)
        QS = [sb("QS", [P, HW], F32R)[:, :], Qhi[:, :]]
        KH = [sb("KH", [P, HW], F32R)[:, :], Qlo[:, :]]
        KL = [sb("KL", [P, HW], F32R)[:, :], Khi[:, :, :].rearrange("p h k -> p (h k)")]
        heads = lambda t: t.rearrange("p (h k) -> p h k", h=HEADS)
        late = sb("late", [P, 6 * HW])
        QH_, QL_ = [Qhi[:, :], QS[0]], [Qlo[:, :], KH[0]]
        KH_, KL_ = [Khi[:, :, :], heads(KL[0])], [Klo[:, :, :], heads(sb("Klo2", [P, HW], F32R)[:, :])]
        V4 = sb("V4", [P, 2, 2, P])
        Vt = sb("Vt", [P, 2, NT, U])
        shared = sb("shared", [P, 4 * HW])
        probs = shared[:, 0:2 * HW].rearrange("p (i n) -> p i n", i=2)
        probsT = shared[:, 2 * HW:4 * HW].rearrange("p (i n) -> p i n", i=2)
        outT = sb("outT", [P, 2, P])
        piece = lambda i: late[:, i * HW:(i + 1) * HW].rearrange("p (i c) -> p i c", i=NT)
        w1stage = late[:, 3 * HW:3 * HW + CHUNKS * E * C].rearrange("p (c e n) -> p c e n", c=CHUNKS, e=E)
        normed = piece(0)
        conv_out = [piece(1), piece(2)]
        tok = [piece(3), piece(4), piece(5)]
        lnb_rep = sb("lnb_rep", [P, P])
        pixels = sb("pixels", [P, HW])
        xn_b = x_new = pixels
        taps = sb("taps", [P, 4, 256])
        wQ_in, wV_in = (taps[:, 2 * k:2 * k + 2, :].rearrange("p t n -> p (t n)") for k in range(2))
        t1 = sb("t1", [P, B * NT, C])
        w3stage = t1[:, 0:CHUNKS * E, :].rearrange("p (c e) n -> p c e n", c=CHUNKS)
        rows_both = sb("rows_both", [P, 2 * TT * ROW])
        rows = [rows_both[:, k * TT * ROW:(k + 1) * TT * ROW].rearrange("p (i c) -> p i c", i=TT) for k in range(2)]
        w2stage = rows_both[:, 0:E * H].rearrange("p (e h) -> p e h", e=E)
        logits = sb("logits", [P, 2 * TT, E])
        stats = sb("stats", [P, NT, 6])
        mv = sb("mv", [P, NT, 2])
        rs_v = sb("rs_v", [P, NT])
        rs_a = sb("rs_a", [P, NT])
        rs_y = sb("rs_y", [P, NT])
        minus_half = sb("minus_half", [P, NT])
        rs_i = sb("rs_i", [P, NT], I32)
        rowmax = sb("rowmax", [P, 2, HEADS])
        negmax = sb("negmax", [P, 2, HEADS])
        rowsum = sb("rowsum", [P, 4, HEADS])
        rowinv = sb("rowinv", [P, 4, HEADS])
        r8 = {n: sb("r_" + n, [P, TT, E]) for n in ("eq", "w", "oh1", "oh2", "l2", "ex", "a", "c0", "c1", "rank", "tmp")}
        r1 = {n: sb("r1_" + n, [P, TT]) for n in ("m1", "m2", "mw", "z", "e2", "p1", "p2", "g1", "g2", "s", "pos")}
        pos_i = sb("pos_i", [P, 2, 2, TT], I32)
        cnt = sb("cnt", [P, E])
        cnt_i = sb("cnt_i", [P, E], I32)
        cum = [sb(f"cum{k}", [P, E]) for k in range(2)]
        tile_cmp = sb("tile_cmp", [P, SLOT_TILES, E])
        tile_sum = sb("tile_sum", [P, SLOT_TILES])
        tile_expert = sb("tile_expert", [P, 2, SLOT_TILES], I32)
        empty = w13_T[:, :, :].rearrange("p e h -> p (e h)")[:, 0:SLOT_TILES * ROW].rearrange("p (k c) -> p k c", c=ROW)

        def carve(base, at, n, width):
            return base[:, at:at + n * width].rearrange("p (i n) -> p i n", i=n), at + n * width

        xs = sb("xs", [P, NB, ROW])
        hid, at = carve(late, 0, NC, CHUNKS * HC)
        y12, at = carve(late, at, NS, 4 * 2 * C)
        y12 = y12.rearrange("p i (t n) -> p i t n", t=4)
        res = x[:, 0:NS // 2, :].rearrange("p b (i n) -> p (b i) n", i=2)
        assert at <= 6 * HW
        hidT, at = carve(shared, 0, NC, CHUNKS * P)
        act_h, at = carve(shared, at, NC, H)
        xsT, at = carve(shared, at, NC, P)
        ys, at = carve(shared, at, NC, C)
        assert at <= 4 * HW

        slots = [nc.dram_tensor(f"slots{h}", [SLOTS, ROW], F32).ap() for h in range(2)]
        y_rows = [nc.dram_tensor(f"y_rows{h}", [Y_ROWS, C], F32).ap() for h in range(2)]

        S = [ps(f"S{i}", [P, HW]) for i in range(2)]
        OM, PO, TA, TB = (ps(n, [P, 512]) for n in ("OM", "PO", "TA", "TB"))

        names = """x_in w_in const_z const_set pad_z wt_done wt_used bias_done bias_used gn_pe gn_dve w1_in w3_in
            w2stage_in small_in rows_in dve_pre scores_done neg_ready exp_done pt_done ptA_copied ptB_copied
            pv_done ot_copied post_done post_used dve_step fill_done fill_copied0 fill_copied1 xn_ready
            taps_ready hi_done x_added norm_stats norm_step norm_rstd normed_ready tok_ready rows_set
            r_exp_in r_exp r_cnt_in route_done pool_step init_z init_done dispatched0 dispatched1 xs_in0
            xs_in1 xs_in2 xs_in3 xs_in4 xs_in5 xs_in6 xs_in7 xsT_pe xsT_act h_pe silu_done hid_ready hT_pe
            hT_dve y_pe ys_ready ys_out0 ys_out1 ys_out2 ys_out3 ys_out4 ys_out5 ys_out6 ys_out7 y12_in0
            y12_in1 y12_in2 y12_in3 sum_step sum_ready fin_pe fin_act out_done0 out_done1 out_done2
            out_done3""".split()
        s = {n: sem(n) for n in names}
        xs_in = [s[f"xs_in{k}"] for k in range(NB)]
        ys_out = [s[f"ys_out{k}"] for k in range(NB)]
        y12_in = [s[f"y12_in{k}"] for k in range(NS)]

        N_W = 21
        SMALL_T = [
            (wK_in[:, :], wK_T[:, :]),
            *[(wQ_in[:, tap:C * 4:4], wQV_T[:, tap, 0, :]) for tap in range(4)],
            *[(wV_in[:, tap:C * 4:4], wQV_T[:, tap, 1, :]) for tap in range(4)],
            (qw_in[:, :], q_wT[:, :]), (kw_in[:, :], k_wT[:, :]), (vw_in[:, :], v_wT[:, :]), (ow_in[:, :], o_wT[:, :]),
        ]
        SMALL_BANK = [OM, PO, TA, TB]
        BANKS = [TA, TB]
        out_r = out.rearrange("b c h w -> c b (h w)")
        block = ctx.enter_context(nc.Block())

        def tile(i):
            return slice(i * P, (i + 1) * P)

        def wait_if(eng, semaphore, value):
            if not (isinstance(value, int) and value <= 0):
                eng.wait_ge(semaphore, value)

        def nth(f):
            return BANKED.index(f) + 1

        def banked_before(f):
            return sum(g in BANKED for g in FILLERS[:FILLERS.index(f)])

        def before_it(f, *names):
            return sum(g[0] in names for g in FILLERS[:FILLERS.index(f)])

        def bank_of(f):
            return 1 if f in LAST_UNITS else BANKED.index(f) % 2

        def turn_of(f):
            return sum(bank_of(g) == bank_of(f) for g in BANKED[:BANKED.index(f) + 1])

        def wait_copied(eng, *fs):
            for f in fs:
                eng.wait_ge(s[f"fill_copied{bank_of(f)}"], turn_of(f))

        def norm_of(f):
            return NORMS.index(({"c": "cs1", "l": "ts1", "r": "ps1"}.get(f[0][0]) if f[0][1] in "01" else f[0][0] + "s1", f[1]))

        def normed_of(f):
            if f[0][0] in "ctlo" and f[1] == 2:
                return pixels[:, :].rearrange("p (i c) -> p i c", i=NT)
            return {len(NORMS) - 2: taps[:, :, :].rearrange("p t n -> p (t n)").rearrange("p (i c) -> p i c", i=NT),
                    len(NORMS) - 1: pixels[:, :].rearrange("p (i c) -> p i c", i=NT)}.get(norm_of(f), normed)

        def run_phases(step, fill, tail):
            for f in flat(FIRST):
                fill(*f)
            for p, (kind, b, inner, behind) in enumerate(PHASES):
                assert len(inner) <= SLOTS_OF_STEP * NT, (p, len(inner))
                for j in range(NT):
                    def slot(i):
                        n = SLOTS_OF_STEP * j + i
                        for f in inner[n] if n < len(inner) else []:
                            fill(*f)
                        if n == SLOTS_OF_STEP * NT - 1:
                            for f in flat(behind):
                                fill(*f)
                    step(NT * p + j, slot)
            tail()
            for f in flat(BEHIND):
                fill(*f)

        def phase_of(g):
            return PHASES[g // NT][0], PHASES[g // NT][1], g % NT

        OFFSET = {"B": 0, "T": 1, "D": -2, "C": -1}

        GROUPS = 2 * TT // 4
        SUM_AFTER = {0: 0, 2: 1, 4: 2, 6: 3}

        def sum_bank(q):
            return TA if q >= GROUPS // 2 and q % 2 == 0 else TB

        loaded = {}

        def schedule(eng, stages, fill, combine):
            def step(q, k, i=None):
                for name, stage in stages:
                    d = OFFSET[name]
                    if i is not None and not 0 <= i + d < 2 * SLOT_TILES:
                        continue
                    qq = q + (k + d) // NB
                    stage(qq * NB + (k + d) % NB, qq, (k + d) % NB)

            if any(name == "T" for name, _ in stages):
                dict(stages)["T"](0, 0, 0)
            for i in range(NB):
                step(0, i, i)
                for f in flat(LAST[i:i + 1]):
                    fill(*f)
            for k in range(2 * NB):
                step(1 + k // NB, k % NB)
            if eng is nc.tensor:
                eng.wait_ge(s["route_done"], 2)
            with eng.Fori(1, TURNS - 1) as t:
                loaded.clear()
                for k in range(2 * NB):
                    step(2 * t + (1 + k // NB), k % NB)
            loaded.clear()
            for i in range(NB + 2):
                step(2 * TURNS - 1 + i // NB, i % NB, 2 * SLOT_TILES - NB + i)
                done = i - (0 if eng is nc.vector else 1)
                if done in SUM_AFTER:
                    combine(SUM_AFTER[done])

        @block.sync
        def _(sp):
            xr = a["x"].rearrange("b c h w -> c b (h w)")
            for b in range(B):
                sp.dma_start(x[:, b, :], xr[:, b, :]).then_inc(s["x_in"], 16)
            sp.dma_start(wK_in[:, :], a["L0_conv_wK"].rearrange("o c h w -> o (c h w)")).then_inc(s["w_in"], 16)
            sp.dma_start(wQ_in[:, :], a["L0_conv_wQ"].rearrange("o c h w -> o (c h w)")).then_inc(s["w_in"], 16)
            sp.dma_start(wV_in[:, :], a["L0_conv_wV"].rearrange("o c h w -> o (c h w)")).then_inc(s["w_in"], 16)
            sp.dma_start(qw_in[:, :], a["L0_conv_q_w"]).then_inc(s["w_in"], 16)
            sp.dma_start(ow_in[:, :], a["L0_conv_o_w"]).then_inc(s["w_in"], 16)
            sp.wait_ge(s["small_in"], 16 * 8)
            for w, stage, done in (("L1_ffn_w1", w1stage, "w1_in"), ("L1_ffn_w3", w3stage, "w3_in")):
                for c in range(CHUNKS):
                    n = min(HC, H - c * HC)
                    sp.dma_start(stage[0:n, c, :, :], a[w][:, c * HC:c * HC + n, :].rearrange("e h c -> h e c")).then_inc(s[done], 16)
            sp.dma_start(w2stage[:, :, :], a["L1_ffn_w2"].rearrange("e c h -> c e h")).then_inc(s["w2stage_in"], 16)

            y_view = [y_rows[h][0:2 * HALF_TOK, :].rearrange("(i p r) c -> p i (r c)", p=P, r=2) for h in range(2)]

            def load_outputs(q):
                wait_if(sp, s["sum_ready"], q - NS + 1)
                h, r = q // (TT // 4), q % (TT // 4)
                sp.dma_start(y12[:, q % NS, :, :], y_view[h][:, r * 4:r * 4 + 4, :]).then_inc(y12_in[q % NS], 16)

            def store(q):
                sp.wait_ge(s["fin_act"], q + 1)
                sp.dma_start(out_r[:, q // 2, (q % 2) * 512:(q % 2) * 512 + 512], res[:, q % NS, :]).then_inc(s[f"out_done{q % NS}"], 16)

            def wait_outputs(half):
                for k in range(NB):
                    sp.wait_ge(ys_out[k], 16 * (half + 1) * TURNS)

            for half in range(2):
                sp.wait_ge(s["init_done"], 32)
                for b in range(HALF_B):
                    sp.wait_ge(s[f"dispatched{b}"], 16 * 2 * NT * (half + 1))

                def load(i, q, k):
                    wait_if(sp, ys_out[k], q * 16)
                    row = bass.ds(i * P, P) if not isinstance(i, int) else slice(i * P, i * P + P)
                    sp.dma_start(xs[:, k, :], slots[half][row, :]).then_inc(xs_in[k], 16)

                for k in range(NB):
                    load(k, half * TURNS, k)
                with sp.Fori(1, TURNS - 1) as t:
                    for k in range(NB):
                        load(t * NB + k, t + half * TURNS, k)
                if half == 1:
                    wait_outputs(0)
                    for q in range(GROUPS // 2):
                        load_outputs(q)
                for k in range(NB):
                    load((TURNS - 1) * NB + k, half * TURNS + TURNS - 1, k)

            for q in range(GROUPS // 2):
                store(q)
            wait_outputs(1)
            for q in range(GROUPS // 2, GROUPS):
                load_outputs(q)
            for q in range(GROUPS // 2, GROUPS):
                store(q)
            for k in range(NS):
                sp.wait_ge(s[f"out_done{k}"], 16 * GROUPS // NS)

        @block.gpsimd
        def _(pool):
            for k, (m, v) in enumerate(((ident, 0.0), (ones, 1.0), (before, 1.0), (groups, 1.0 / GROUP), (router_T, 0.0),
                                        (w2_T, 0.0), (empty, 0.0))):
                nc.gpsimd.memset(m if m is empty else m[:], v).then_inc(s["const_z"], 1)
            nc.gpsimd.memset(minus_half[:], -0.5)
            pool.wait_ge(s["const_z"], 7)
            nc.gpsimd.affine_select(out=ident[:, :], in_=ident[:, :], compare_op=ALU.not_equal, fill=1.0, base=0,
                                    pattern=[[-1, P]], channel_multiplier=1).then_inc(s["const_set"], 1)
            nc.gpsimd.affine_select(out=before[:, :], in_=before[:, :], compare_op=ALU.is_gt, fill=0.0, base=0,
                                    pattern=[[1, P]], channel_multiplier=-1).then_inc(s["const_set"], 1)
            gv = groups[:, :].rearrange("p (g r) -> p g r", r=GROUP)
            nc.gpsimd.affine_select(out=gv, in_=gv, compare_op=ALU.is_ge, fill=0.0, base=0,
                                    pattern=[[-GROUP, P // GROUP], [0, GROUP]], channel_multiplier=1).then_inc(s["const_z"], 1)
            pool.wait_ge(s["const_z"], 8)
            nc.gpsimd.affine_select(out=gv, in_=gv, compare_op=ALU.is_ge, fill=0.0, base=GROUP - 1,
                                    pattern=[[GROUP, P // GROUP], [0, GROUP]], channel_multiplier=-1).then_inc(s["const_set"], 1)
            nc.gpsimd.iota(rev[:, :, :], pattern=[[0, TT], [-1, E]], base=E, channel_multiplier=0,
                           allow_small_or_imprecise_dtypes=True).then_inc(s["const_set"], 1)
            nc.gpsimd.iota(tile_no[:, :, :], pattern=[[1, SLOT_TILES], [0, E]], base=0, channel_multiplier=0,
                           allow_small_or_imprecise_dtypes=True).then_inc(s["const_set"], 1)
            nc.gpsimd.iota(empty[:, :, C:C + 1].bitcast(I32), pattern=[[1, SLOT_TILES]], base=2 * HALF_TOK,
                           channel_multiplier=SLOT_TILES).then_inc(s["init_z"], 1)
            pool.wait_ge(s["init_z"], 1)
            pool.wait_ge(s["small_in"], 16 * 8)
            for half in range(2):
                pool.dma_start(slots[half].rearrange("(p k) c -> p (k c)", k=SLOT_TILES),
                               empty[:, :, :].rearrange("p k c -> p (k c)")).then_inc(s["init_done"], 16)
            wait_copied(pool, ("wc", E - 2), ("wc", E - 1))
            for k in range(2):
                nc.gpsimd.iota(rows[k][:, :, C:C + 1].bitcast(I32), pattern=[[2 * P, TT]], base=k,
                               channel_multiplier=2).then_inc(s["init_z"], 1)
            def dispatch(half, j):
                pool.indirect_dma_start(
                    slots[half], bass.IndirectOffsetOnAxis(pos_i[:, half, j % 2, j // 2:j // 2 + 1], 0),
                    rows[j % 2][:, j // 2, :], None).then_inc(s[f"dispatched{j // (2 * NT)}"], 16)

            def scatter(half, k):
                pool.indirect_dma_start(
                    y_rows[half], bass.IndirectOffsetOnAxis(xs[:, k, C:C + 1].bitcast(I32), 0),
                    ys[:, k % NC, :], None).then_inc(ys_out[k], 16)

            def fill(u, b):
                f = (u, b)
                if u == "xn":
                    pool.wait_ge(s["xn_ready"], b + 1)
                    xv = x[:, b, :].rearrange("p (j f) -> p j f", j=NT)
                    nc.gpsimd.tensor_tensor(xv, xv, o_b_rows[:, :].unsqueeze(1).broadcast_to((P, NT, P)), ALU.add).then_inc(s["x_added"], 1)
                elif f in NORMS:
                    n = NORMS.index(f)
                    pool.wait_ge(s["norm_stats"], n + 1)
                    nc.gpsimd.tensor_scalar(rs_v[:, :], mv[:, :, 1], 1e-5, None, ALU.add).then_inc(s["norm_step"], 1)
                    pool.wait_ge(s["norm_step"], n + 1)
                    nc.gpsimd.tensor_tensor(rs_y[:, :], rs_v[:, :], minus_half[:, :], ALU.pow).then_inc(s["norm_rstd"], 1)
                elif u == "ta1":
                    pool.wait_ge(s["normed_ready"], 2 * norm_of(f) + 2)
                    t = tok[b % 3][:, :, :]
                    nc.gpsimd.tensor_tensor(t, t, normed_of(f), ALU.add).then_inc(s["tok_ready"], 1)
                    pool.wait_ge(s["tok_ready"], 2 * before_it(f, "ta1") + 1)
                    nc.gpsimd.tensor_tensor(t, t, b_o_rows[:, :].unsqueeze(1).broadcast_to((P, NT, C)), ALU.add).then_inc(s["tok_ready"], 1)

            pool.wait_ge(s["bias_used"], 2)
            for f in FILLERS:
                fill(*f)
                if f == ("rf", 0):
                    pool.wait_ge(s["init_done"], 32)
                    pool.wait_ge(s["rows_set"], 2 * HALF_B)
                    pool.wait_ge(s["route_done"], 1)
                    for j in range(4):
                        dispatch(0, j)
                if f == ("ps1", 2):
                    for j in range(4, 2 * TT):
                        dispatch(0, j)
            for n in range(SLOT_TILES):
                if n == DISPATCH_FROM:
                    pool.wait_ge(s["rows_set"], 2 * B)
                    pool.wait_ge(s["route_done"], 2)
                if n >= DISPATCH_FROM:
                    m = n - DISPATCH_FROM
                    for j in range(3 * m // 2, min(3 * (m + 1) // 2, 2 * TT)):
                        dispatch(1, j)
                pool.wait_ge(s["ys_ready"], n + 1)
                scatter(0, n % NB)
            carry = lambda: nc.gpsimd.tensor_tensor(spare[:, 1:2], ones[:, 0:1], ones[:, 1:2], ALU.mult).then_inc(s["pool_step"], 1)
            carry()
            with pool.Fori(TURNS, 2 * TURNS) as t:
                for k in range(NB):
                    pool.wait_ge(s["ys_ready"], t * NB + (k + 1))
                    pool.wait_ge(s["pool_step"], t * NB + (k - SLOT_TILES + 1))
                    carry()
                    scatter(1, k)

        @block.scalar
        def _(act):
            kv = lambda w: w.rearrange("(k d) e -> k d e", k=2)
            for k in range(2):
                for src, dst in ((a["L0_conv_k_w"], kw_in), (a["L0_conv_v_w"], vw_in)):
                    for g in range(2):
                        act.dma_start(dst[(2 * k + g) * HD:(2 * k + g + 1) * HD, :], kv(src)[k]).then_inc(s["w_in"], 16)
            col = lambda v: v.rearrange("(p a) -> p a", a=1)
            act.dma_start(q_b[:, :], col(a["L0_conv_q_b"])).then_inc(s["w_in"], 16)
            act.dma_start(ln_g[:, :], col(a["L0_conv_ln_g"])).then_inc(s["w_in"], 16)
            act.dma_start(ln_b[:, :], col(a["L0_conv_ln_b"])).then_inc(s["w_in"], 16)
            for k in range(2):
                for g in range(2):
                    h = 2 * k + g
                    act.dma_start(k_b[h * HD:(h + 1) * HD, :],
                                 col(a["L0_conv_k_b"])[k * HD:(k + 1) * HD, :]).then_inc(s["w_in"], 16)
            act.dma_start(router_in[:, :], a["L1_ffn_router_w"]).then_inc(s["w_in"], 16)
            row = lambda v: v.rearrange("(a n) -> a n", a=1)
            for h in range(HEADS):
                act.dma_start(rows_in[0:1, 0, h * HD:(h + 1) * HD],
                              row(a["L0_conv_v_b"])[:, (h // 2) * HD:(h // 2 + 1) * HD]).then_inc(s["rows_in"], 16)
            act.dma_start(rows_in[0:1, 1, :], row(a["L0_conv_o_b"])).then_inc(s["rows_in"], 16)
            act.dma_start(rows_in[0:1, 2, :], row(a["L1_attn_b_o"])).then_inc(s["rows_in"], 16)
            for dst, w in ((Wq2, "L1_attn_W_q"), (Wk2, "L1_attn_W_k"), (Wv2, "L1_attn_W_v")):
                for k in range(2):
                    act.dma_start(dst[:, k * U:(k + 1) * U], a[w]).then_inc(s["small_in"], 16)
            for k in range(2):
                act.dma_start(Wo2[k * U:(k + 1) * U, :], a["L1_attn_W_o"]).then_inc(s["small_in"], 16)

            def exps(g):
                kind, b, j = phase_of(g)
                act.wait_ge(s["neg_ready"], g + 1)
                wait_if(act, s["pt_done"], g - 1)
                wait_if(act, s["post_used"], g - 3)
                if kind == "conv":
                    for h in range(HEADS):
                        ins = act.activation(probs[:, g % 2, h * KEYS:(h + 1) * KEYS],
                                             S[g % 2][:, h * KEYS:(h + 1) * KEYS], ACT.Exp,
                                             bias=negmax[:, g % 2, h:h + 1], scale=CONV_SCALE,
                                             accum_out=rowsum[:, g % 4, h:h + 1])
                else:
                    ins = act.activation(probs[:, g % 2, :], S[g % 2][:, :], ACT.Exp, bias=negmax[:, g % 2, 0:1],
                                         scale=TOK_SCALE, accum_out=rowsum[:, g % 4, 0:1])
                ins.then_inc(s["exp_done"], 1)

            def probs_copy(g):
                act.wait_ge(s["pt_done"], g + 1)
                wait_if(act, s["pv_done"], g - 1)
                act.activation(probsT[:, g % 2, CUT:HW], S[g % 2][:, CUT:HW], ACT.Copy).then_inc(s["ptB_copied"], 1)

            def out_copy(g):
                act.wait_ge(s["pv_done"], g + 1)
                wait_if(act, s["post_done"], g - 1)
                act.activation(outT[:, g % 2, :], OM[:, 0:P], ACT.Copy).then_inc(s["ot_copied"], 1)

            def step(g, slot):
                if g == 0:
                    exps(0)
                slot(0)
                probs_copy(g)
                slot(1)
                if g >= 1:
                    out_copy(g - 1)
                if g % NT < NT - 1:
                    exps(g + 1)
                slot(2)
                if g % NT == NT - 1 and g + 1 < STEPS:
                    exps(g + 1)

            def tail():
                out_copy(STEPS - 1)

            def fill(u, b):
                f = (u, b)
                if f == ("wa", 0):
                    act.wait_ge(s["init_done"], 32)
                if f in BANKED and u not in ("V", "wc", "o0", "o1", "g0", "g1", "rank"):
                    act.wait_ge(s["fill_done"], nth(f))
                bank = BANKS[bank_of(f)] if f in BANKED else None
                half = int(u[-1]) if u[-1] in "01" else 0
                r = slice(half * 512, (half + 1) * 512)
                copied = lambda ins: ins.then_inc(s[f"fill_copied{bank_of(f)}"], 1)
                T = TOK_SET[b] if b < B else 0
                if u == "xn":
                    act.wait_ge(s["xn_ready"], b + 1)
                    wait_if(act, s["fill_done"], banked_before(f))
                    grid = pixels[:, :].rearrange("p (oy dy ox dx) -> p dy dx oy ox", oy=16, dy=2, ox=16, dx=2)
                    for dy in range(2):
                        ins = act.activation(taps[:, 2 * dy:2 * dy + 2, :].rearrange("p x (oy ox) -> p x oy ox", oy=16),
                                             grid[:, dy], ACT.Copy)
                    ins.then_inc(s["taps_ready"], 1)
                elif u in ("kT0", "kT1", "c0", "c1", "l0", "l1", "r0", "r1"):
                    copied(act.activation(operandT[:, r], bank[:, :], ACT.Copy))
                elif u in ("wa", "wb"):
                    m = "ab".index(u[1])
                    copied(act.activation(w13_T[:, b, m * H:(m + 1) * H], bank[:, 0:H], ACT.Copy))
                elif u in ("qv0", "qv1"):
                    copied(act.activation(qvT[:, half, :, :].rearrange("p m c -> p (m c)"), bank[:, 0:2 * C], ACT.Copy))
                elif u in ("Q0", "Q1"):
                    act.activation(QH_[CONV_SET[b]][:, r], bank[:, :], ACT.Identity, bias=q_b[:, 0:1]).then_inc(s["hi_done"], 1)
                elif u == "K":
                    if CONV_SET[b] == 1:
                        act.wait_ge(s["pad_z"], 2)
                    for h in range(HEADS):
                        p = slice(h * HD, (h + 1) * HD)
                        ins = act.activation(KH_[CONV_SET[b]][p, h, :], bank[p, 0:KEYS], ACT.Identity, bias=k_b[p, 0:1])
                    ins.then_inc(s["hi_done"], 1)
                elif u in ("t0", "t1"):
                    if b >= 3:
                        act.wait_ge(s["post_used"], NT * [p[:2] for p in PHASES].index(("tok", b - 3)) + NT)
                    copied(act.activation(tok[b % 3][:, 4 * half:4 * half + 4, :].rearrange("p i c -> p (i c)"), bank[:, :], ACT.Copy))
                elif u in ("q0", "q1"):
                    act.activation(QS[T][:, r], bank[:, :], ACT.Copy).then_inc(s["hi_done"], 1)
                elif u in ("k0", "k1"):
                    act.activation(KH[T][:, r], bank[:, :], ACT.Copy).then_inc(s["hi_done"], 1)
                elif u in ("v0", "v1"):
                    copied(act.activation(Vt[:, b % 2, 4 * half:4 * half + 4, :],
                                          bank[:, :].rearrange("p (i u) -> p i u", i=4)[:, :, 0:U], ACT.Copy))
                elif u == "pc":
                    act.wait_ge(s["init_z"], 3)
                    act.wait_ge(s["normed_ready"], 2 * norm_of(f) + 2)
                    wait_if(act, s[f"dispatched{b % HALF_B}"], 16 * 2 * NT * (b // HALF_B))
                    i = (b % HALF_B) * NT
                    for k in range(2):
                        act.activation(rows[k][:, i:i + NT, 0:C], normed_of(f), ACT.Copy).then_inc(s["rows_set"], 1)
                elif u == "rb":
                    act.wait_ge(s["r_exp_in"], b + 1)
                    act.activation(r8["ex"][:, :, :], r8["ex"][:, :, :], ACT.Exp).then_inc(s["r_exp"], 1)

            act.wait_ge(s["w_in"], 16 * N_W)
            run_phases(step, fill, tail)

            def x_copy(n, q, k):
                act.wait_ge(s["xsT_pe"], n + 1)
                wait_if(act, s["h_pe"], n - (NC - 1))
                act.activation(xsT[:, k % NC, :], OM[:, 0:P], ACT.Copy).then_inc(s["xsT_act"], 1)

            def silu(n, q, k):
                act.wait_ge(s["h_pe"], n + 1)
                wait_if(act, s["hid_ready"], n - (NC - 1))
                act.activation(act_h[:, k % NC, :], S[k % 2][:, 0:H], ACT.Silu).then_inc(s["silu_done"], 1)

            def gate(n, q, k):
                act.wait_ge(s["y_pe"], n + 1)
                wait_if(act, ys_out[(k - NC) % NB], (q + (k - NC) // NB + 1) * 16)
                act.activation(ys[:, k % NC, :], PO[:, 0:P], ACT.Copy, scale=xs[:, k, C + 1:C + 2]).then_inc(s["ys_ready"], 1)

            def combine(q):
                act.wait_ge(s["fin_pe"], q + 1)
                wait_if(act, s[f"out_done{q % NS}"], 16 * (q // NS))
                act.activation(res[:, q % NS, :], sum_bank(q)[:, :], ACT.Copy).then_inc(s["fin_act"], 1)

            schedule(act, (("B", silu), ("T", x_copy), ("D", gate)), fill, combine)
            for q in range(GROUPS // 2, GROUPS):
                combine(q)

        @block.vector
        def _(dve):
            class Steps:
                def __init__(self, semaphore, base):
                    self.semaphore, self.base, self.n = semaphore, base, 0

                def __call__(self, ins):
                    ins.then_inc(self.semaphore, 1)
                    self.n += 1
                    dve.wait_ge(self.semaphore, self.base + self.n)

            def rsqrt(link, y, v, n, eps):
                h, t = rs_v[:, 0:n], rs_a[:, 0:n]
                link(nc.vector.tensor_scalar(h, v, eps, None, ALU.add))
                link(nc.vector.tensor_scalar(rs_i[:, 0:n], h.bitcast(I32), 1, None, ALU.logical_shift_right))
                link(nc.vector.tensor_scalar(y.bitcast(I32), rs_i[:, 0:n], -1.0, float(MAGIC), ALU.mult, ALU.add))
                for _ in range(NEWTON):
                    link(nc.vector.tensor_tensor(t, y, y, ALU.mult))
                    link(nc.vector.scalar_tensor_tensor(out=t, in0=t, scalar=-0.5, in1=h, op0=ALU.mult, op1=ALU.mult))
                    link(nc.vector.scalar_tensor_tensor(out=y, in0=t, scalar=1.5, in1=y, op0=ALU.add, op1=ALU.mult))

            pre = Steps(s["dve_pre"], 0)
            dve.wait_ge(s["x_in"], 16 * B)
            for b in range(B):
                for i in range(2):
                    last = nc.vector.bn_stats(chan[:, b, i, :], x[:, b, i * 512:(i + 1) * 512])
            pre(last)
            for b in range(B):
                last = nc.vector.bn_aggr(chan_mv[:, b, :], chan[:, b, :, :].rearrange("p i s -> p (i s)"))
            last.then_inc(s["gn_dve"], 1)
            dve.wait_ge(s["gn_dve"], 1)
            dve.wait_ge(s["gn_pe"], 1)
            pre(nc.vector.tensor_copy(grp[:, :, :].rearrange("p b s -> p (b s)"), S[0][:, 0:2 * B]))
            pre(nc.vector.tensor_tensor(dev[:, :], chan_mv[:, :, 0], grp[:, :, 0], ALU.subtract))
            nc.vector.tensor_tensor(dev[:, :], dev[:, :], dev[:, :], ALU.mult).then_inc(s["gn_dve"], 1)
            dve.wait_ge(s["gn_pe"], 2)
            pre(nc.vector.tensor_tensor(gvar[:, 0:B], S[0][:, 0:B], grp[:, :, 1], ALU.add))
            rsqrt(pre, gvar[:, 4:4 + B], gvar[:, 0:B], B, 1e-5)
            nc.vector.memset(Khi[:, :, :].bitcast(F32), 0.0)
            nc.vector.memset(Klo[:, :, :].bitcast(F32), 0.0).then_inc(s["pad_z"], 1)
            for i, (_, dst) in enumerate(SMALL_T):
                if i % 4 == 0:
                    dve.wait_ge(s["wt_done"], i // 4 + 1)
                last = nc.vector.tensor_copy(dst, SMALL_BANK[i // 4][:, tile(i % 4)])
                if i % 4 == 3 or i == len(SMALL_T) - 1:
                    if i == len(SMALL_T) - 1:
                        dve.wait_ge(s["const_z"], 7)
                        last = nc.vector.tensor_copy(router_T[:, 0:E], TB[:, P:P + E])
                    last.then_inc(s["wt_used"], 1)
            dve.wait_ge(s["wt_used"], 4)
            nc.vector.tensor_scalar(o_wTg[:, :], o_wT[:, :], ln_g[:, 0:1], None, ALU.mult)
            dve.wait_ge(s["const_z"], 7)
            nc.vector.tensor_scalar(lnb_rep[:, :], ones[:, :], ln_b[:, 0:1], None, ALU.mult).then_inc(s["bias_used"], 1)
            dve.wait_ge(s["bias_done"], 1)
            nc.vector.tensor_copy(v_b_rows[:, :], OM[:, tile(0)])
            nc.vector.tensor_copy(o_b_rows[:, :], OM[:, tile(1)])
            nc.vector.tensor_copy(b_o_rows[:, :], OM[:, tile(2)]).then_inc(s["bias_used"], 1)
            dve.wait_ge(s["bias_used"], 2)
            link = Steps(s["dve_step"], 0)

            def row_max(g):
                kind, b, j = phase_of(g)
                dve.wait_ge(s["scores_done"], g + 1)
                wait_if(dve, s["exp_done"], g - 1)
                n = HEADS if kind == "conv" else 1
                link(nc.vector.tensor_reduce(rowmax[:, g % 2, 0:n], S[g % 2][:, :].rearrange("p (h k) -> p h k", h=n),
                                             AX.X, ALU.max))
                nc.vector.tensor_scalar(negmax[:, g % 2, 0:n], rowmax[:, g % 2, 0:n],
                                        -(CONV_SCALE if kind == "conv" else TOK_SCALE), None, ALU.mult).then_inc(s["neg_ready"], 1)

            def probs_copy(g):
                dve.wait_ge(s["pt_done"], g + 1)
                wait_if(dve, s["pv_done"], g - 1)
                nc.vector.tensor_copy(probsT[:, g % 2, 0:CUT], S[g % 2][:, 0:CUT]).then_inc(s["ptA_copied"], 1)

            def normalise(g):
                kind, b, j = phase_of(g)
                n = HEADS if kind == "conv" else 1
                link(nc.vector.reciprocal(rowinv[:, g % 4, 0:n], rowsum[:, g % 4, 0:n]))
                dve.wait_ge(s["post_done"], g + 1)
                post = PO[:, 0:P]
                if kind == "conv":
                    nc.vector.tensor_tensor(conv_out[b % 2][:, j, :].rearrange("p (h d) -> p h d", h=HEADS),
                                            post.rearrange("p (h d) -> p h d", h=HEADS),
                                            rowinv[:, g % 4, :].unsqueeze(2).broadcast_to((P, HEADS, HD)),
                                            ALU.mult).then_inc(s["post_used"], 1)
                else:
                    dve.wait_ge(s["tok_ready"], 2 * b + 2)
                    nc.vector.scalar_tensor_tensor(out=t1[:, b * NT + j, :], in0=post, scalar=rowinv[:, g % 4, 0:1],
                                                   in1=tok[b % 3][:, j, :], op0=ALU.mult, op1=ALU.add).then_inc(s["post_used"], 1)

            def step(g, slot):
                if g == 0:
                    row_max(0)
                if g % NT < NT - 1:
                    row_max(g + 1)
                if g >= 2:
                    normalise(g - 2)
                slot(0)
                probs_copy(g)
                slot(1)
                slot(2)
                if g % NT == NT - 1 and g + 1 < STEPS:
                    row_max(g + 1)

            def tail():
                normalise(STEPS - 2)
                normalise(STEPS - 1)

            def statistics(f, src, half):
                tiles = range(4 * half, 4 * half + 4)
                for i in tiles:
                    last = nc.vector.bn_stats(stats[:, i, :], src[:, i, :])
                link(last)
                for i in tiles:
                    last = nc.vector.bn_aggr(mv[:, i, :], stats[:, i, :])
                if half == 1:
                    last.then_inc(s["norm_stats"], 1)

            def apply_norm(f, src, half):
                n = norm_of(f)
                dve.wait_ge(s["norm_rstd"], n + 1)
                wait_if(dve, s["fill_done"], banked_before(f))
                wait_if(dve, s["tok_ready"], 2 * before_it(f, "ta1"))
                wait_if(dve, s["rows_set"], 2 * before_it(f, "pc") if f[1] < HALF_B else 0)
                for i in range(4 * half, 4 * half + 4):
                    last = nc.vector.tensor_scalar(normed_of(f)[:, i, :], src[:, i, :], mv[:, i, 0:1], rs_y[:, i:i + 1],
                                                   ALU.subtract, ALU.mult)
                last.then_inc(s["normed_ready"], 1)

            def fill(u, b):
                f = (u, b)
                V = nc.vector
                if u in ("Q0", "Q1", "K", "q0", "q1", "k0", "k1"):
                    dve.wait_ge(s["hi_done"], sum(g[0] in ("Q0", "Q1", "K", "q0", "q1", "k0", "k1") for g in FILLERS[:FILLERS.index(f) + 1]))
                elif u in ("V", "wc", "o0", "o1", "g0", "g1", "re"):
                    dve.wait_ge(s["fill_done"], nth(f if u != "re" else ("rank", b)))
                bank = BANKS[bank_of(f)] if f in BANKED else None
                half = int(u[-1]) if u[-1] in "01" else 0
                r = slice(half * 512, (half + 1) * 512)
                copied = lambda ins: ins.then_inc(s[f"fill_copied{bank_of(f)}"], 1)
                T = TOK_SET[b] if b < B else 0
                V = nc.vector
                if u == "xn":
                    wait_if(dve, s["fill_done"], banked_before(f))
                    V.tensor_scalar(pixels[:, :], x[:, b, :], grp[:, b, 0:1], gvar[:, b + 4:b + 5],
                                    ALU.subtract, ALU.mult).then_inc(s["xn_ready"], 1)
                elif u in ("Q0", "Q1"):
                    copied(V.scalar_tensor_tensor(out=QL_[CONV_SET[b]][:, r], in0=bank[:, :], scalar=q_b[:, 0:1], in1=QH_[CONV_SET[b]][:, r].bitcast(F32),
                                                  op0=ALU.add, op1=ALU.subtract))
                elif u == "K":
                    for h in range(HEADS):
                        p = slice(h * HD, (h + 1) * HD)
                        last = V.scalar_tensor_tensor(out=KL_[CONV_SET[b]][p, h, :], in0=bank[p, 0:KEYS], scalar=k_b[p, 0:1],
                                                      in1=KH_[CONV_SET[b]][p, h, :].bitcast(F32), op0=ALU.add, op1=ALU.subtract)
                    copied(last)
                elif u == "V":
                    copied(V.tensor_tensor(V4[:, b % 2, :, :], bank[:, 0:2 * P].rearrange("p (j v) -> p j v", j=2),
                                           v_b_rows[:, :].unsqueeze(1).broadcast_to((P, 2, P)), ALU.add))
                elif u == "wc":
                    V.tensor_copy(w2_T[0:HC, b, 0:2 * C], bank[0:HC, 0:2 * C])
                    copied(V.tensor_copy(w2_T[0:HC - 1, b, 2 * C:3 * C], bank[0:HC - 1, 2 * C:3 * C]))
                elif u in ("cs0", "cs1"):
                    g = NT * [p[:2] for p in PHASES].index(("conv", b)) + 4 * half + 4
                    dve.wait_ge(s["post_used"], g)
                    statistics(f, conv_out[b % 2], half)
                elif u in ("ca0", "ca1"):
                    apply_norm(f, conv_out[b % 2], half)
                elif u in ("o0", "o1"):
                    dve.wait_ge(s["x_added"], b + 1)
                    dve.wait_ge(s["taps_ready"], before_it(f, "xn"))
                    copied(V.tensor_tensor(pixels[:, r], bank[:, :], x[:, b, r], ALU.add))
                elif u in ("ts0", "ts1"):
                    wait_copied(dve, (f"t{half}", b))
                    statistics(f, tok[b % 3], half)
                elif u in ("ta0", "ta1"):
                    apply_norm(f, tok[b % 3], half)
                elif u in ("q0", "q1"):
                    copied(V.tensor_tensor(QS[T][U:P, r], bank[U:P, :], QS[T][U:P, r].bitcast(F32), ALU.subtract))
                elif u in ("k0", "k1"):
                    copied(V.tensor_tensor(KL[T][:, r], bank[:, :], KH[T][:, r].bitcast(F32), ALU.subtract))
                elif u in ("ps0", "ps1"):
                    g = NT * [p[:2] for p in PHASES].index(("tok", b)) + 4 * half + 4
                    dve.wait_ge(s["post_used"], g)
                    statistics(f, t1[:, b * NT:(b + 1) * NT, :], half)
                elif u in ("pa0", "pa1"):
                    apply_norm(f, t1[:, b * NT:(b + 1) * NT, :], half)
                elif u in ("g0", "g1"):
                    i = b * NT + 4 * half
                    copied(V.tensor_copy(logits[:, i:i + 4, :], bank[:, :].rearrange("p (i e) -> p i e", i=4)[:, :, 0:E]))
                elif u in ("ra", "rb", "rc", "rd", "re", "rf"):
                    route(u, b)

            def route(part, half):
                step = link
                V = nc.vector
                f = ("rank", half)
                bank = BANKS[bank_of(f)]
                copied = lambda ins: ins.then_inc(s[f"fill_copied{bank_of(f)}"], 1)
                L = logits[:, half * TT:(half + 1) * TT, :]
                wide = lambda t: t[:, :].unsqueeze(2).broadcast_to((P, TT, E))
                R, r = r8, r1

                def first_of(values, m, onehot):
                    step(V.tensor_reduce(r[m][:, :], values, AX.X, ALU.max))
                    step(V.tensor_tensor(R["eq"][:, :, :], values, wide(r[m]), ALU.is_equal))
                    step(V.tensor_tensor(R["w"][:, :, :], R["eq"][:, :, :], rev[:, :, :], ALU.mult))
                    step(V.tensor_reduce(r["mw"][:, :], R["w"][:, :, :], AX.X, ALU.max))
                    step(V.tensor_tensor(R[onehot][:, :, :], R["w"][:, :, :], wide(r["mw"]), ALU.is_equal))

                if part == "ra":
                    wait_copied(dve, *((g, HALF_B * half + k) for g in ("g0", "g1") for k in range(HALF_B)))
                    first_of(L, "m1", "oh1")
                    V.tensor_tensor(R["ex"][:, :, :], L, wide(r["m1"]), ALU.subtract).then_inc(s["r_exp_in"], 1)
                    step(V.scalar_tensor_tensor(out=R["l2"][:, :, :], in0=R["oh1"][:, :, :], scalar=BIG, in1=L,
                                                op0=ALU.mult, op1=ALU.add))
                if part == "rb":
                    first_of(R["l2"][:, :, :], "m2", "oh2")
                    step(V.tensor_tensor(R["a"][:, :, :], R["oh1"][:, :, :], R["oh2"][:, :, :], ALU.add))
                if part == "rc":
                    src = "a"
                    for n, d in enumerate((1, 2, 4, 8)):
                        dst = ("c0", "c1")[n % 2]
                        V.tensor_copy(R[dst][:, 0:d, :], R[src][:, 0:d, :])
                        step(V.tensor_tensor(R[dst][:, d:TT, :], R[src][:, d:TT, :], R[src][:, 0:TT - d, :], ALU.add))
                        src = dst
                    V.tensor_tensor(R["c0"][:, :, :], R["c1"][:, :, :], R["a"][:, :, :], ALU.subtract).then_inc(s["r_cnt_in"], 1)
                if part == "rd":
                    dve.wait_ge(s["r_exp"], half + 1)
                    step(V.tensor_reduce(r["z"][:, :], R["ex"][:, :, :], AX.X, ALU.add))
                    step(V.tensor_tensor(R["tmp"][:, :, :], R["ex"][:, :, :], R["oh2"][:, :, :], ALU.mult))
                    step(V.tensor_reduce(r["e2"][:, :], R["tmp"][:, :, :], AX.X, ALU.add))
                    step(V.reciprocal(r["p1"][:, :], r["z"][:, :]))
                    step(V.tensor_tensor(r["p2"][:, :], r["e2"][:, :], r["p1"][:, :], ALU.mult))
                    step(V.scalar_tensor_tensor(out=r["s"][:, :], in0=r["p1"][:, :], scalar=1e-9, in1=r["p2"][:, :],
                                                op0=ALU.add, op1=ALU.add))
                    step(V.reciprocal(r["z"][:, :], r["s"][:, :]))
                    dve.wait_ge(s["init_z"], 3)
                    if half == 1:
                        for b in range(HALF_B):
                            dve.wait_ge(s[f"dispatched{b}"], 16 * 2 * NT)
                    for k, p in enumerate(("p1", "p2")):
                        step(V.tensor_tensor(rows[k][:, :, C + 1], r[p][:, :], r["z"][:, :], ALU.mult))
                if part == "re":
                    step(V.tensor_scalar(cnt_i[:, :], bank[:, 128:128 + E], float(P - 1), None, ALU.add))
                    step(V.tensor_scalar(cnt_i[:, :], cnt_i[:, :], 7, None, ALU.logical_shift_right))
                    step(V.tensor_copy(cnt[:, :], cnt_i[:, :]))
                    src = cnt
                    for n, d in enumerate((1, 2, 4)):
                        V.tensor_copy(cum[n % 2][:, 0:d], src[:, 0:d])
                        step(V.tensor_tensor(cum[n % 2][:, d:E], src[:, d:E], src[:, 0:E - d], ALU.add))
                        src = cum[n % 2]
                    step(V.tensor_tensor(tile_cmp[:, :, :], tile_no[:, :, :],
                                         cum[0][:, :].unsqueeze(1).broadcast_to((P, SLOT_TILES, E)), ALU.is_ge))
                    step(V.tensor_reduce(tile_sum[:, :], tile_cmp[:, :, :], AX.X, ALU.add))
                    step(V.tensor_scalar(tile_expert[:, half, :], tile_sum[:, :], float(E - 1), None, ALU.min))
                    step(V.tensor_tensor(cum[1][:, :], cum[0][:, :], cnt[:, :], ALU.subtract))
                    step(V.tensor_scalar(cum[1][:, :], cum[1][:, :], float(P), None, ALU.mult))
                    copied(V.tensor_tensor(R["rank"][:, :, :], bank[:, 0:TT * E].rearrange("p (i e) -> p i e", e=E),
                                           cum[1][:, :].unsqueeze(1).broadcast_to((P, TT, E)), ALU.add))
                    wait_copied(dve, f)
                if part == "rf":
                    for k, oh in enumerate(("oh1", "oh2")):
                        step(V.tensor_tensor(R["tmp"][:, :, :], R["rank"][:, :, :], R[oh][:, :, :], ALU.mult))
                        step(V.tensor_reduce(r["pos"][:, :], R["tmp"][:, :, :], AX.X, ALU.add))
                        last = V.tensor_copy(pos_i[:, half, k, :], r["pos"][:, :])
                        if k == 0:
                            step(last)
                    last.then_inc(s["route_done"], 1)

            dve.wait_ge(s["w_in"], 16 * N_W)
            nc.vector.memset(KH_[1].bitcast(F32), 0.0)
            nc.vector.memset(KL_[1].bitcast(F32), 0.0).then_inc(s["pad_z"], 1)
            run_phases(step, fill, tail)

            def hidden(n, q, k):
                dve.wait_ge(s["silu_done"], n + 1)
                wait_if(dve, s["hT_pe"], n - (NC - 1))
                nc.vector.tensor_tensor(hid[:, k % NC, 0:H], S[k % 2][:, 512:512 + H], act_h[:, k % NC, :], ALU.mult).then_inc(s["hid_ready"], 1)

            def hidden_copy(n, q, k):
                dve.wait_ge(s["hT_pe"], n + 1)
                wait_if(dve, s["y_pe"], n - (NC - 1))
                nc.vector.tensor_copy(hidT[0:HC, k % NC, :], TA[0:HC, 0:CHUNKS * P]).then_inc(s["hT_dve"], 1)

            def combine(q):
                dve.wait_ge(y12_in[q % NS], 16 * (q // NS + 1))
                t = t1[:, 4 * q:4 * q + 4, :]
                nc.vector.tensor_tensor(t, t, y12[:, q % NS, :, 0:C], ALU.add).then_inc(s["sum_step"], 1)
                dve.wait_ge(s["sum_step"], q + 1)
                nc.vector.tensor_tensor(t, t, y12[:, q % NS, :, C:2 * C], ALU.add).then_inc(s["sum_ready"], 1)

            nc.vector.memset(hid[:, :, :], 0.0).then_inc(s["pad_z"], 1)
            dve.wait_ge(s["pad_z"], 3)
            schedule(dve, (("B", hidden), ("C", hidden_copy)), fill, combine)
            for q in range(GROUPS // 2, GROUPS):
                combine(q)

        @block.tensor
        def _(pe):
            mm, tr = nc.tensor.matmul, nc.tensor.transpose

            pe.wait_ge(s["const_set"], 5)
            pe.wait_ge(s["gn_dve"], 1)
            mm(S[0][:, 0:2 * B], groups[:, :], chan_mv[:, :, :].rearrange("p b s -> p (b s)"), start=True, stop=True).then_inc(s["gn_pe"], 1)
            pe.wait_ge(s["gn_dve"], 2)
            mm(S[0][:, 0:B], groups[:, :], dev[:, :], start=True, stop=True).then_inc(s["gn_pe"], 1)
            pe.wait_ge(s["w_in"], 16 * N_W)
            for i, (src, _) in enumerate(SMALL_T):
                last = tr(SMALL_BANK[i // 4][:, tile(i % 4)], src, ident[:, :])
                if i == len(SMALL_T) - 1:
                    last = tr(TB[:, P:P + E], router_in[:, :], ident[0:E, 0:E])
                if i % 4 == 3 or i == len(SMALL_T) - 1:
                    last.then_inc(s["wt_done"], 1)
            pe.wait_ge(s["rows_in"], 16 * 6)
            pe.wait_ge(s["bias_used"], 1)
            mm(OM[:, tile(0)], ones[0:1, :], rows_in[0:1, 0, :], start=True, stop=True)
            mm(OM[:, tile(1)], lnb_rep[:, :], o_wT[:, :], start=True, stop=False)
            mm(OM[:, tile(1)], ones[0:1, :], rows_in[0:1, 1, :], start=False, stop=True)
            mm(OM[:, tile(2)], ones[0:1, :], rows_in[0:1, 2, :], start=True, stop=True).then_inc(s["bias_done"], 1)
            pe.wait_ge(s["wt_used"], 4)
            pe.wait_ge(s["small_in"], 16 * 8)
            pe.wait_ge(s["pad_z"], 1)
            pe.wait_ge(s["bias_used"], 2)

            def scores(g):
                kind, b, j = phase_of(g)
                wait_if(pe, s["ptA_copied"], g - 1)
                wait_if(pe, s["ptB_copied"], g - 1)
                if j == 0:
                    wait_copied(pe, *((u, b) for u in (("Q0", "Q1", "K", "V") if kind == "conv" else ("q0", "q1", "k0", "k1", "v0", "v1"))))
                for half in range(2):
                    r = slice(half * 512, (half + 1) * 512)
                    dst = S[g % 2][:, r]
                    if kind == "conv":
                        qh, ql = QH_[CONV_SET[b]], QL_[CONV_SET[b]]
                        kh = KH_[CONV_SET[b]][:, 2 * half:2 * half + 2, :].rearrange("p h k -> p (h k)")
                        kl = KL_[CONV_SET[b]][:, 2 * half:2 * half + 2, :].rearrange("p h k -> p (h k)")
                        mm(dst, qh[:, tile(j)], kh, start=True, stop=False)
                        mm(dst, qh[:, tile(j)], kl, start=False, stop=False)
                        last = mm(dst, ql[:, tile(j)], kh, start=False, stop=True)
                    else:
                        T = TOK_SET[b]
                        mm(dst, QS[T][:, tile(j)], KH[T][:, r], start=True, stop=False)
                        last = mm(dst, QS[T][:, tile(j)], KL[T][:, r], start=False, stop=True)
                last.then_inc(s["scores_done"], 1)

            def probs_T(g):
                pe.wait_ge(s["exp_done"], g + 1)
                for k in range(8):
                    last = tr(S[g % 2][:, tile(k)], probs[:, g % 2, tile(k)], ident[:, :])
                last.then_inc(s["pt_done"], 1)

            def values(g):
                kind, b, j = phase_of(g)
                pe.wait_ge(s["ptA_copied"], g + 1)
                pe.wait_ge(s["ptB_copied"], g + 1)
                wait_if(pe, s["ot_copied"], g)
                out_ = OM[:, 0:P]
                pT = probsT[:, g % 2, :]
                if kind == "conv":
                    for st in range(2):
                        for h in range(HEADS):
                            last = mm(out_[h * HD:(h + 1) * HD, :], V4[:, b % 2, st, h * HD:(h + 1) * HD],
                                      pT[:, tile(2 * h + st)], start=(st == 0), stop=(st == 1))
                else:
                    for kt in range(NT):
                        r = slice((kt % 2) * U, (kt % 2 + 1) * U)
                        last = mm(out_[r, :], Vt[:, b % 2, kt, :], pT[:, tile(kt)], start=(kt < 2), stop=(kt >= NT - 2))
                last.then_inc(s["pv_done"], 1)

            def post_of(g):
                kind, b, j = phase_of(g)
                pe.wait_ge(s["ot_copied"], g + 1)
                wait_if(pe, s["post_used"], g)
                out_ = PO[:, 0:P]
                if kind == "conv":
                    last = tr(out_, outT[:, g % 2, :], ident[:, :])
                else:
                    last = mm(out_, outT[:, g % 2, :], Wo2[:, :], start=True, stop=True)
                last.then_inc(s["post_done"], 1)

            def step(g, slot):
                if g == 0:
                    scores(0)
                if g % NT < NT - 1:
                    scores(g + 1)
                if g >= 2:
                    post_of(g - 2)
                slot(0)
                probs_T(g)
                slot(1)
                if g >= 1:
                    values(g - 1)
                slot(2)
                if g % NT == NT - 1 and g + 1 < STEPS:
                    scores(g + 1)

            def tail():
                post_of(STEPS - 2)
                values(STEPS - 1)
                post_of(STEPS - 1)

            def fill(u, b):
                f = (u, b)
                if f not in BANKED:
                    return
                n = nth(f)
                half = int(u[-1]) if u[-1] in "01" else 0
                r = slice(half * 512, (half + 1) * 512)
                if u in ("kT0", "kT1"):
                    pe.wait_ge(s["xn_ready"], b + 1)
                elif u in ("qv0", "qv1"):
                    pe.wait_ge(s["taps_ready"], b + 1)
                elif u in ("c0", "l0", "r0", "c1", "l1", "r1"):
                    pe.wait_ge(s["normed_ready"], 2 * norm_of(f) + 1 + half)
                elif u == "rank":
                    pe.wait_ge(s["r_cnt_in"], b + 1)
                elif u in ("wa", "wb"):
                    pe.wait_ge(s["w1_in" if u == "wa" else "w3_in"], 16 * CHUNKS)
                elif u == "wc":
                    pe.wait_ge(s["w2stage_in"], 16)
                for k, sources in {"Q": ("kT",), "K": ("qv0", "qv1"), "V": ("qv0", "qv1"), "o": ("c",), "t": ("o",),
                                   "v": ("l",), "q": ("l",) if u[:2] != "qv" else (), "k": ("l",) if u[:2] != "kT" else (),
                                   "g": ("r",)}.items():
                    if u[0] == k:
                        wait_copied(pe, *((src if src[-1] in "01" else f"{src}{half}", b) for src in sources))
                wait_if(pe, s[f"fill_copied{bank_of(f)}"], turn_of(f) - 1)
                bank = BANKS[bank_of(f)]
                if u in ("kT0", "kT1"):
                    for j in range(4):
                        last = mm(bank[:, tile(j)], pixels[:, tile(4 * half + j)], wK_T[:, :], start=True, stop=True)
                elif u in ("wa", "wb"):
                    for c in range(CHUNKS):
                        n_h = min(HC, H - c * HC)
                        last = tr(bank[:, c * HC:c * HC + n_h], (w1stage if u == "wa" else w3stage)[0:n_h, c, b, :], ident[0:n_h, 0:n_h])
                elif u == "wc":
                    for c in range(CHUNKS):
                        n_h = min(HC, H - c * HC)
                        last = tr(bank[0:n_h, tile(c)], w2stage[:, b, c * HC:c * HC + n_h], ident[:, :])
                elif u in ("qv0", "qv1"):
                    for tap in range(4):
                        last = mm(bank[:, 0:2 * C], taps[:, tap, tile(half)], wQV_T[:, tap, :, :].rearrange("p m c -> p (m c)"),
                                  start=(tap == 0), stop=(tap == 3))
                elif u in ("Q0", "Q1"):
                    last = mm(bank[:, :], q_wT[:, :], operandT[:, r], start=True, stop=True)
                elif u == "K":
                    last = mm(bank[:, 0:KEYS], k_wT[:, :], qvT[:, :, 0, :], start=True, stop=True)
                elif u == "V":
                    for j in range(2):
                        last = mm(bank[:, tile(j)], qvT[:, j, 1, :], v_wT[:, :], start=True, stop=True)
                elif u in ("c0", "c1", "l0", "l1", "r0", "r1"):
                    for i in range(4):
                        last = tr(bank[:, tile(i)], normed_of(f)[:, 4 * half + i, :], ident[:, :])
                elif u in ("o0", "o1"):
                    for j in range(4):
                        last = mm(bank[:, tile(j)], operandT[:, tile(4 * half + j)], o_wTg[:, :], start=True, stop=True)
                elif u in ("t0", "t1"):
                    for i in range(4):
                        last = tr(bank[:, tile(i)], pixels[:, tile(4 * half + i)], ident[:, :])
                elif u in ("q0", "q1"):
                    last = mm(bank[:, :], Wq2[:, :], operandT[:, r], start=True, stop=True)
                elif u in ("k0", "k1"):
                    last = mm(bank[:, :], Wk2[:, :], operandT[:, r], start=True, stop=True)
                elif u in ("v0", "v1"):
                    for i in range(4):
                        last = mm(bank[:, tile(i)], operandT[:, tile(4 * half + i)], Wv2[:, :], start=True, stop=True)
                elif u in ("g0", "g1"):
                    for i in range(4):
                        last = mm(bank[:, tile(i)], operandT[:, tile(4 * half + i)], router_T[:, :], start=True, stop=True)
                elif u == "rank":
                    mm(bank[:, 0:TT * E], before[:, :], r8["a"][:, :, :].rearrange("p i e -> p (i e)"), start=True, stop=False)
                    mm(bank[:, 0:TT * E], ones[:, :], r8["c0"][:, :, :].rearrange("p i e -> p (i e)"), start=False, stop=True)
                    last = mm(bank[:, P:P + E], ones[:, :], r8["c1"][:, TT - 1, :], start=True, stop=True)
                last.then_inc(s["fill_done"], 1)

            run_phases(step, fill, tail)

            def token_T(n, q, k):
                pe.wait_ge(xs_in[k], q * 16 + 16)
                wait_if(pe, s["xsT_act"], n)
                tr(OM[:, 0:P], xs[:, k, 0:C], ident[:, :]).then_inc(s["xsT_pe"], 1)
                loaded[k] = expert_of(n)

            def hidden(n, q, k):
                e = loaded[k] if k in loaded else expert_of(n)
                pe.wait_ge(s["xsT_act"], n + 1)
                wait_if(pe, s["hid_ready"], n - 1)
                for m in range(2):
                    last = mm(S[k % 2][:, m * 512:m * 512 + H], xsT[:, k % NC, :],
                              w13_T[:, bass.ds(e, 1), m * H:(m + 1) * H].rearrange("p a h -> p (a h)"), start=True, stop=True)
                last.then_inc(s["h_pe"], 1)

            def hidden_T(n, q, k):
                pe.wait_ge(s["hid_ready"], n + 1)
                wait_if(pe, s["hT_dve"], n)
                for c in range(CHUNKS):
                    last = tr(TA[0:HC, tile(c)], hid[:, k % NC, c * HC:(c + 1) * HC], ident[:, :])
                last.then_inc(s["hT_pe"], 1)

            def output(n, q, k):
                e = loaded[k] if k in loaded else expert_of(n)
                pe.wait_ge(s["hT_dve"], n + 1)
                wait_if(pe, s["ys_ready"], n)
                for c in range(CHUNKS):
                    last = mm(PO[:, 0:P], hidT[0:HC, k % NC, tile(c)],
                              w2_T[0:HC, bass.ds(e, 1), tile(c)].rearrange("p a c -> p (a c)"), start=(c == 0), stop=(c == CHUNKS - 1))
                last.then_inc(s["y_pe"], 1)

            def expert_of(n):
                te = tile_expert[0:1, :, :].rearrange("p h i -> p (h i)")
                i = bass.ds(n, 1) if not isinstance(n, int) else slice(n, n + 1)
                return pe.value_load(te[:, i], min_val=0, max_val=E - 1)

            def combine(q):
                pe.wait_ge(s["sum_ready"], q + 1)
                wait_if(pe, s["fin_act"], q if q < GROUPS // 2 else q - 1)
                for i in range(4):
                    last = tr(sum_bank(q)[:, tile(i)], t1[:, 4 * q + i, :], ident[:, :])
                last.then_inc(s["fin_pe"], 1)

            wait_copied(pe, [f for f in BANKED if bank_of(f) == 0][-1])
            pe.wait_ge(s["route_done"], 1)
            schedule(pe, (("B", hidden), ("T", token_T), ("D", output), ("C", hidden_T)), fill, combine)
            for q in range(GROUPS // 2, GROUPS):
                combine(q)


INPUTS = ["x"] + ["L0_conv_" + n for n in "wK wQ wV q_w q_b k_w k_b v_w v_b ln_g ln_b o_w o_b".split()] + \
    ["L1_attn_" + n for n in "W_q W_k W_v W_o b_o".split()] + ["L1_ffn_" + n for n in "router_w w1 w2 w3".split()]


def kernel(**inputs):
    import numpy as np
    from concourse import bacc
    from concourse.bass_utils import run_bass_kernel_spmd

    nc = bacc.Bacc("TRN2", target_bir_lowering=False, num_devices=1)
    arrays, aps = {}, {}
    for name in INPUTS:
        v = np.ascontiguousarray(inputs[name])
        arrays["in_" + name] = v
        aps[name] = nc.dram_tensor("in_" + name, v.shape, mybir.dt.from_np(v.dtype), kind="ExternalInput").ap()
    out = nc.dram_tensor("out", (B, C, 32, 32), F32, kind="ExternalOutput").ap()
    build(nc, aps, out)
    r = run_bass_kernel_spmd(nc, [arrays], core_ids=[0])
    return r.results[0]["out"]
```
